# Optimizing a Trainium2 kernel written in Bass

```python
import numpy as np
import jax
import jax.numpy as jnp

def _softmax(x, axis=-1):
    return jax.nn.softmax(x, axis=axis)

def _gelu(x):
    return jax.nn.gelu(x, approximate=True)

def _silu(x):
    return jax.nn.silu(x)

def _sigmoid(x):
    return jax.nn.sigmoid(x)

def _layernorm(x, axis=-1, eps=1e-05):
    m = jnp.mean(x, axis=axis, keepdims=True)
    v = jnp.var(x, axis=axis, keepdims=True)
    return (x - m) / jnp.sqrt(v + eps)

def _scatter_add(tgt, idx, src, axis=0):
    return tgt.at[idx].add(src)

def _segment_sum(src, seg, n):
    return jax.ops.segment_sum(src, seg, n)
kernel_name = 'mk_decoder_postln_d1_seqx_r8_195300'

def setup_inputs(seed: int=0):
    np.random.seed(seed)
    _w = jnp.asarray

    def _rec_inputs():
        import jax
        import jax.numpy as jnp
        _rk = jax.random.key(seed)
        x = -0.0001661 + 0.9999 * jax.random.normal(jax.random.fold_in(_rk, 1), (4, 256, 256), jnp.float32)
        _lenS = 256 - jax.random.randint(jax.random.fold_in(_rk, 7), (4,), 0, max(1, 256 // 4) + 1, jnp.int32)
        _lenS2 = 1601 - jax.random.randint(jax.random.fold_in(_rk, 8), (4,), 0, max(1, 1601 // 4) + 1, jnp.int32)
        _ctx_2048P = jax.random.normal(jax.random.fold_in(_rk, 11), (4, 16, 256), jnp.float32)
        _ctx_2048c = jax.random.dirichlet(jax.random.fold_in(_rk, 511), 0.3 * jnp.ones((16,), jnp.float32), (4, 1601))
        _ctx_2048t = jnp.einsum('bsk,bkd->bsd', _ctx_2048c, _ctx_2048P)
        _ctx_2048t = _ctx_2048t * jax.lax.rsqrt(jnp.mean(jnp.square(_ctx_2048t)) + 1e-12) * 0.953939
        ctx_2048 = -0.00016346 + 1.00032 * (_ctx_2048t + 0.3 * jax.random.normal(jax.random.fold_in(_rk, 611), (4, 1601, 256), jnp.float32))
        return (x, ctx_2048, _lenS2)
    x, ctx_2048, _lenS2 = _rec_inputs()

    def _L0_attn_setup():
        import jax, jax.numpy as jnp
        import numpy as np
        import math
        B, T = (4, 128)
        D_MODEL = 256
        HEAD_DIM = 64
        N_HEADS = 32
        N_KV = 8
        Q_MULT = N_HEADS // N_KV
        SLIDING_WINDOW = 128
        CAUSAL = True
        SM_SCALE = 1.0 / math.sqrt(HEAD_DIM)
        ROPE_THETA = 150000.0
        SCALING = 32.0
        NTK_ALPHA = 1.0
        NTK_BETA = 32.0
        ICL = 128

        def _rope_cos_sin(t_len):
            d_half = HEAD_DIM // 2
            freq = ROPE_THETA ** (np.arange(0, HEAD_DIM, 2, dtype=np.float32) / HEAD_DIM)
            concentration = 0.1 * math.log(SCALING) + 1.0
            low = d_half * math.log(ICL / (NTK_BETA * 2 * math.pi)) / math.log(ROPE_THETA)
            high = d_half * math.log(ICL / (NTK_ALPHA * 2 * math.pi)) / math.log(ROPE_THETA)
            interpolation = 1.0 / (SCALING * freq)
            extrapolation = 1.0 / freq
            ramp = np.clip((np.arange(d_half, dtype=np.float32) - low) / (high - low), 0.0, 1.0)
            mask = 1.0 - ramp
            inv_freq = interpolation * (1.0 - mask) + extrapolation * mask
            freqs = np.outer(np.arange(t_len, dtype=np.float32), inv_freq)
            return (jnp.asarray(np.cos(freqs) * concentration, jnp.float32), jnp.asarray(np.sin(freqs) * concentration, jnp.float32))

        def _apply_rope(x, cos, sin):
            x1, x2 = jnp.split(x, 2, axis=-1)
            return jnp.concatenate([x1 * cos - x2 * sin, x2 * cos + x1 * sin], axis=-1)
        key = jax.random.key(seed)
        ks = jax.random.split(key, 6)
        qkv_dim = HEAD_DIM * (N_HEADS + 2 * N_KV)
        return {'x': jax.random.normal(ks[0], (B, T, D_MODEL), jnp.float32), 'qkv_w': jax.random.normal(ks[1], (qkv_dim, D_MODEL), jnp.float32) * 0.02, 'qkv_b': jax.random.normal(ks[2], (qkv_dim,), jnp.float32) * 0.02, 'out_w': jax.random.normal(ks[3], (D_MODEL, N_HEADS * HEAD_DIM), jnp.float32) * 0.02, 'out_b': jax.random.normal(ks[4], (D_MODEL,), jnp.float32) * 0.02, 'sinks': jax.random.normal(ks[5], (N_HEADS,), jnp.float32) * (1.0 / math.sqrt(HEAD_DIM))}
    _L0_attn_all = _L0_attn_setup()
    _L0_attn_in = {k: v for k, v in _L0_attn_all.items() if k in ('qkv_w', 'qkv_b', 'out_w', 'out_b', 'sinks')}
    del _L0_attn_all

    def _L0_xattn_setup():
        import jax, jax.numpy as jnp
        import numpy as np
        DIM = 256
        HEADS = 16
        HEAD_DIM = DIM // HEADS
        EPS = 1e-06
        IMG_TOKENS = 257
        B, L1, L2 = (2, 512, 769)
        SCALE = 1.0 / np.sqrt(HEAD_DIM).astype(np.float32)

        def rms_norm(x, g):
            return x * jax.lax.rsqrt(jnp.mean(x * x, axis=-1, keepdims=True) + EPS) * g

        def attention(q, k, v, kv_mask=None):
            s = jnp.einsum('bqhd,bkhd->bhqk', q, k) * SCALE
            if kv_mask is not None:
                s = jnp.where(kv_mask[:, None, None, :], s, jnp.float32(-1000000000.0))
            p = jax.nn.softmax(s, axis=-1)
            return jnp.einsum('bhqk,bkhd->bqhd', p, v)
        key = jax.random.key(seed)
        ks = jax.random.split(key, 20)
        std = 0.02

        def lin(i):
            return (jax.random.normal(ks[i], (DIM, DIM), jnp.float32) * std, jnp.zeros((DIM,), jnp.float32))
        w_q, b_q = lin(0)
        w_k, b_k = lin(1)
        w_v, b_v = lin(2)
        w_k_img, b_k_img = lin(3)
        w_v_img, b_v_img = lin(4)
        w_o, b_o = lin(5)
        return {'x': jax.random.normal(ks[6], (B, L1, DIM), jnp.float32), 'context': jax.random.normal(ks[7], (B, L2, DIM), jnp.float32), 'context_lens': jax.random.randint(ks[8], (B,), 32, 513, jnp.int64 if jax.config.jax_enable_x64 else jnp.int32), 'w_q': w_q, 'b_q': b_q, 'w_k': w_k, 'b_k': b_k, 'w_v': w_v, 'b_v': b_v, 'w_k_img': w_k_img, 'b_k_img': b_k_img, 'w_v_img': w_v_img, 'b_v_img': b_v_img, 'w_o': w_o, 'b_o': b_o, 'g_q': jnp.ones((DIM,), jnp.float32), 'g_k': jnp.ones((DIM,), jnp.float32), 'g_k_img': jnp.ones((DIM,), jnp.float32)}
    _L0_xattn_all = _L0_xattn_setup()
    _L0_xattn_in = {k: v for k, v in _L0_xattn_all.items() if k in ('w_q', 'b_q', 'w_k', 'b_k', 'w_v', 'b_v', 'w_k_img', 'b_k_img', 'w_v_img', 'b_v_img', 'w_o', 'b_o', 'g_q', 'g_k', 'g_k_img')}
    del _L0_xattn_all

    def _L0_ffn_setup():
        import jax, jax.numpy as jnp
        import numpy as np
        from jax import lax
        B, S, H = (1, 256, 256)
        E, I, TOP_K = (64, 64, 8)
        SHARED_I = 64
        key = jax.random.key(seed)
        ks = jax.random.split(key, 8)
        sc = 0.02
        return {'hidden_states': jax.random.normal(ks[0], (B, S, H), jnp.float32), 'router_w': jax.random.normal(ks[1], (E, H), jnp.float32) * sc, 'gate_up_proj': jax.random.normal(ks[2], (E, 2 * I, H), jnp.float32) * sc, 'down_proj': jax.random.normal(ks[3], (E, H, I), jnp.float32) * sc, 'shared_gate_w': jax.random.normal(ks[4], (SHARED_I, H), jnp.float32) * sc, 'shared_up_w': jax.random.normal(ks[5], (SHARED_I, H), jnp.float32) * sc, 'shared_down_w': jax.random.normal(ks[6], (H, SHARED_I), jnp.float32) * sc, 'shared_expert_gate_w': jax.random.normal(ks[7], (1, H), jnp.float32) * sc}
    _L0_ffn_all = _L0_ffn_setup()
    _L0_ffn_in = {k: v for k, v in _L0_ffn_all.items() if k in ('router_w', 'gate_up_proj', 'down_proj', 'shared_gate_w', 'shared_up_w', 'shared_down_w', 'shared_expert_gate_w')}
    del _L0_ffn_all
    return {'x': x, 'ctx_2048': ctx_2048, '_lenS2': _lenS2, 'L0_attn_qkv_w': _L0_attn_in['qkv_w'], 'L0_attn_qkv_b': _L0_attn_in['qkv_b'], 'L0_attn_out_w': _L0_attn_in['out_w'], 'L0_attn_out_b': _L0_attn_in['out_b'], 'L0_attn_sinks': _L0_attn_in['sinks'], 'L0_xattn_w_q': _L0_xattn_in['w_q'], 'L0_xattn_b_q': _L0_xattn_in['b_q'], 'L0_xattn_w_k': _L0_xattn_in['w_k'], 'L0_xattn_b_k': _L0_xattn_in['b_k'], 'L0_xattn_w_v': _L0_xattn_in['w_v'], 'L0_xattn_b_v': _L0_xattn_in['b_v'], 'L0_xattn_w_k_img': _L0_xattn_in['w_k_img'], 'L0_xattn_b_k_img': _L0_xattn_in['b_k_img'], 'L0_xattn_w_v_img': _L0_xattn_in['w_v_img'], 'L0_xattn_b_v_img': _L0_xattn_in['b_v_img'], 'L0_xattn_w_o': _L0_xattn_in['w_o'], 'L0_xattn_b_o': _L0_xattn_in['b_o'], 'L0_xattn_g_q': _L0_xattn_in['g_q'], 'L0_xattn_g_k': _L0_xattn_in['g_k'], 'L0_xattn_g_k_img': _L0_xattn_in['g_k_img'], 'L0_ffn_router_w': _L0_ffn_in['router_w'], 'L0_ffn_gate_up_proj': _L0_ffn_in['gate_up_proj'], 'L0_ffn_down_proj': _L0_ffn_in['down_proj'], 'L0_ffn_shared_gate_w': _L0_ffn_in['shared_gate_w'], 'L0_ffn_shared_up_w': _L0_ffn_in['shared_up_w'], 'L0_ffn_shared_down_w': _L0_ffn_in['shared_down_w'], 'L0_ffn_shared_expert_gate_w': _L0_ffn_in['shared_expert_gate_w']}

def reference(x, ctx_2048, _lenS2, L0_attn_qkv_w, L0_attn_qkv_b, L0_attn_out_w, L0_attn_out_b, L0_attn_sinks, L0_xattn_w_q, L0_xattn_b_q, L0_xattn_w_k, L0_xattn_b_k, L0_xattn_w_v, L0_xattn_b_v, L0_xattn_w_k_img, L0_xattn_b_k_img, L0_xattn_w_v_img, L0_xattn_b_v_img, L0_xattn_w_o, L0_xattn_b_o, L0_xattn_g_q, L0_xattn_g_k, L0_xattn_g_k_img, L0_ffn_router_w, L0_ffn_gate_up_proj, L0_ffn_down_proj, L0_ffn_shared_gate_w, L0_ffn_shared_up_w, L0_ffn_shared_down_w, L0_ffn_shared_expert_gate_w):
    import jax
    import jax.numpy as jnp

    def _L0_attn_ref(x, qkv_w, qkv_b, out_w, out_b, sinks):
        import jax, jax.numpy as jnp
        import numpy as np
        import math
        B, T = (4, 128)
        D_MODEL = 256
        HEAD_DIM = 64
        N_HEADS = 32
        N_KV = 8
        Q_MULT = N_HEADS // N_KV
        SLIDING_WINDOW = 128
        CAUSAL = True
        SM_SCALE = 1.0 / math.sqrt(HEAD_DIM)
        ROPE_THETA = 150000.0
        SCALING = 32.0
        NTK_ALPHA = 1.0
        NTK_BETA = 32.0
        ICL = 128

        def _rope_cos_sin(t_len):
            d_half = HEAD_DIM // 2
            freq = ROPE_THETA ** (np.arange(0, HEAD_DIM, 2, dtype=np.float32) / HEAD_DIM)
            concentration = 0.1 * math.log(SCALING) + 1.0
            low = d_half * math.log(ICL / (NTK_BETA * 2 * math.pi)) / math.log(ROPE_THETA)
            high = d_half * math.log(ICL / (NTK_ALPHA * 2 * math.pi)) / math.log(ROPE_THETA)
            interpolation = 1.0 / (SCALING * freq)
            extrapolation = 1.0 / freq
            ramp = np.clip((np.arange(d_half, dtype=np.float32) - low) / (high - low), 0.0, 1.0)
            mask = 1.0 - ramp
            inv_freq = interpolation * (1.0 - mask) + extrapolation * mask
            freqs = np.outer(np.arange(t_len, dtype=np.float32), inv_freq)
            return (jnp.asarray(np.cos(freqs) * concentration, jnp.float32), jnp.asarray(np.sin(freqs) * concentration, jnp.float32))

        def _apply_rope(x, cos, sin):
            x1, x2 = jnp.split(x, 2, axis=-1)
            return jnp.concatenate([x1 * cos - x2 * sin, x2 * cos + x1 * sin], axis=-1)
        Bv, Tv, _ = x.shape
        qkv = x @ qkv_w.T + qkv_b
        q = qkv[..., :N_HEADS * HEAD_DIM].reshape(Bv, Tv, N_KV, Q_MULT, HEAD_DIM)
        k = qkv[..., N_HEADS * HEAD_DIM:(N_HEADS + N_KV) * HEAD_DIM].reshape(Bv, Tv, N_KV, HEAD_DIM)
        v = qkv[..., (N_HEADS + N_KV) * HEAD_DIM:].reshape(Bv, Tv, N_KV, HEAD_DIM)
        cos, sin = _rope_cos_sin(Tv)
        q = _apply_rope(q, cos[:, None, None, :], sin[:, None, None, :])
        k = _apply_rope(k, cos[:, None, :], sin[:, None, :])
        logits = jnp.einsum('bqhmd,bkhd->bhmqk', q, k) * SM_SCALE
        i = jnp.arange(Tv)[:, None]
        j = jnp.arange(Tv)[None, :]
        mask = jnp.zeros((Tv, Tv), dtype=bool)
        if CAUSAL:
            mask = mask | (j > i)
        if SLIDING_WINDOW > 0:
            mask = mask | (j <= i - SLIDING_WINDOW)
        logits = jnp.where(mask, -jnp.inf, logits)
        m = jnp.max(logits, axis=-1, keepdims=True)
        e = jnp.exp(logits - m)
        s = sinks.reshape(N_KV, Q_MULT)[None, :, :, None, None]
        exp_sink = jnp.exp(s - m)
        w = e / (jnp.sum(e, axis=-1, keepdims=True) + exp_sink)
        out = jnp.einsum('bhmqk,bkhd->bqhmd', w, v).reshape(Bv, Tv, N_HEADS * HEAD_DIM)
        return out @ out_w.T + out_b

    def _L0_xattn_ref(x, context, context_lens, w_q, b_q, w_k, b_k, w_v, b_v, w_k_img, b_k_img, w_v_img, b_v_img, w_o, b_o, g_q, g_k, g_k_img):
        import jax, jax.numpy as jnp
        import numpy as np
        DIM = 256
        HEADS = 16
        HEAD_DIM = DIM // HEADS
        EPS = 1e-06
        IMG_TOKENS = 257
        B, L1, L2 = (2, 512, 769)
        SCALE = 1.0 / np.sqrt(HEAD_DIM).astype(np.float32)

        def rms_norm(x, g):
            return x * jax.lax.rsqrt(jnp.mean(x * x, axis=-1, keepdims=True) + EPS) * g

        def attention(q, k, v, kv_mask=None):
            s = jnp.einsum('bqhd,bkhd->bhqk', q, k) * SCALE
            if kv_mask is not None:
                s = jnp.where(kv_mask[:, None, None, :], s, jnp.float32(-1000000000.0))
            p = jax.nn.softmax(s, axis=-1)
            return jnp.einsum('bhqk,bkhd->bqhd', p, v)
        b = x.shape[0]
        ctx_img = context[:, :IMG_TOKENS]
        ctx_txt = context[:, IMG_TOKENS:]
        q = rms_norm(x @ w_q.T + b_q, g_q).reshape(b, -1, HEADS, HEAD_DIM)
        k = rms_norm(ctx_txt @ w_k.T + b_k, g_k).reshape(b, -1, HEADS, HEAD_DIM)
        v = (ctx_txt @ w_v.T + b_v).reshape(b, -1, HEADS, HEAD_DIM)
        k_img = rms_norm(ctx_img @ w_k_img.T + b_k_img, g_k_img).reshape(b, -1, HEADS, HEAD_DIM)
        v_img = (ctx_img @ w_v_img.T + b_v_img).reshape(b, -1, HEADS, HEAD_DIM)
        txt_len = ctx_txt.shape[1]
        kv_mask = jnp.arange(txt_len)[None, :] < context_lens[:, None]
        img_x = attention(q, k_img, v_img)
        txt_x = attention(q, k, v, kv_mask)
        out = (txt_x + img_x).reshape(b, -1, DIM)
        return out @ w_o.T + b_o

    def _L0_ffn_ref(hidden_states, router_w, gate_up_proj, down_proj, shared_gate_w, shared_up_w, shared_down_w, shared_expert_gate_w):
        import jax, jax.numpy as jnp
        import numpy as np
        from jax import lax
        B, S, H = (1, 256, 256)
        E, I, TOP_K = (64, 64, 8)
        SHARED_I = 64
        b, s, h_dim = hidden_states.shape
        h = hidden_states.reshape(-1, h_dim)
        T = h.shape[0]
        shared = jnp.dot(jax.nn.silu(jnp.dot(h, shared_gate_w.T)) * jnp.dot(h, shared_up_w.T), shared_down_w.T)
        shared = jax.nn.sigmoid(jnp.dot(h, shared_expert_gate_w.T)) * shared
        logits = jnp.dot(h, router_w.T)
        probs = jax.nn.softmax(logits.astype(jnp.float32), axis=-1)
        top_vals, top_idx = lax.top_k(probs, TOP_K)
        top_vals = top_vals / jnp.sum(top_vals, axis=-1, keepdims=True)
        top_vals = top_vals.astype(h.dtype)
        comb = jnp.zeros((T, E), h.dtype).at[jnp.arange(T)[:, None], top_idx].add(top_vals)

        def body(acc, xs):
            wgu, wd, w_e = xs
            g, u = jnp.split(jnp.dot(h, wgu.T), 2, axis=-1)
            eo = jnp.dot(jax.nn.silu(g) * u, wd.T)
            return (acc + eo * w_e[:, None], None)
        expert_out, _ = lax.scan(body, jnp.zeros_like(h), (gate_up_proj, down_proj, comb.T))
        return (expert_out + shared).reshape(b, s, h_dim)
    x = _layernorm(x + _L0_attn_ref(x, L0_attn_qkv_w, L0_attn_qkv_b, L0_attn_out_w, L0_attn_out_b, L0_attn_sinks), axis=-1)
    x = _layernorm(x + _L0_xattn_ref(x, ctx_2048, _lenS2, L0_xattn_w_q, L0_xattn_b_q, L0_xattn_w_k, L0_xattn_b_k, L0_xattn_w_v, L0_xattn_b_v, L0_xattn_w_k_img, L0_xattn_b_k_img, L0_xattn_w_v_img, L0_xattn_b_v_img, L0_xattn_w_o, L0_xattn_b_o, L0_xattn_g_q, L0_xattn_g_k, L0_xattn_g_k_img), axis=-1)
    x = _layernorm(x + _L0_ffn_ref(x, L0_ffn_router_w, L0_ffn_gate_up_proj, L0_ffn_down_proj, L0_ffn_shared_gate_w, L0_ffn_shared_up_w, L0_ffn_shared_down_w, L0_ffn_shared_expert_gate_w), axis=-1)
    return x

_drawn_inputs = setup_inputs


def setup_inputs(seed=0):
    import zlib

    import numpy as np

    out = dict(_drawn_inputs(seed))
    spreads = {'L0_xattn_b_q': (0.0, 0.8),
     'L0_xattn_b_k': (0.0, 2.0),
     'L0_xattn_b_v': (0.0, 0.1),
     'L0_xattn_b_k_img': (0.0, 2.0),
     'L0_xattn_b_v_img': (0.0, 0.275),
     'L0_xattn_b_o': (0.0, 0.1),
     'L0_xattn_g_q': (1.0, 0.6),
     'L0_xattn_g_k': (1.0, 0.6),
     'L0_xattn_g_k_img': (1.0, 0.6)}
    factors = {'L0_attn_qkv_b': 3.586,
     'L0_attn_out_b': 2.927,
     'L0_attn_sinks': 36.047,
     'L0_xattn_w_k': 3.03,
     'L0_xattn_w_k_img': 3.01,
     'L0_ffn_router_w': 8.0,
     'L0_ffn_gate_up_proj': 8.0,
     'L0_ffn_down_proj': 8.0,
     'L0_ffn_shared_gate_w': 8.0,
     'L0_ffn_shared_up_w': 8.0,
     'L0_ffn_shared_down_w': 8.0,
     'L0_ffn_shared_expert_gate_w': 8.0}
    for name, (base, spread) in spreads.items():
        noise = np.random.default_rng([zlib.crc32(name.encode()), seed]).standard_normal(out[name].shape)
        drawn = base * np.exp(spread * noise) if base else spread * noise
        out[name] = jnp.asarray(drawn.astype(out[name].dtype))
    for name, factor in factors.items():
        out[name] = (out[name] * factor).astype(out[name].dtype)
    return out
```

```python
import math
from contextlib import ExitStack

import numpy as np

import concourse.bass as bass
from concourse import mybir

F32 = mybir.dt.float32
BF16 = mybir.dt.bfloat16
I32 = mybir.dt.int32
ACT = mybir.ActivationFunctionType
ALU = mybir.AluOpType
AX_X = mybir.AxisListType.X

P = 128
B, T, D = 4, 256, 256
QT = T // P
KT = D // P
N_TILES = B * QT
LN_EPS = 1e-5

DH, N_HEADS, N_KV, WINDOW = 64, 32, 8, 128
Q_MULT = N_HEADS // N_KV
QKV = DH * (N_HEADS + 2 * N_KV)
CHUNK = 512
Q_CHUNKS = N_HEADS * DH // CHUNK
QK_CHUNKS = Q_CHUNKS + 1
N_CHUNKS = QKV // CHUNK
SM_SCALE = 1.0 / math.sqrt(DH)
NEG = -1.0e30

XH, XD = 16, 16
L_IMG, L_ALL = 257, 1601
L_TXT = L_ALL - L_IMG
RMS_EPS = 1e-6

E, EI, TOP_K = 64, 64, 8
N_PAIRS = E // 2 + 1
N_TOK = B * T


def rope_tables():
    theta, scaling, alpha, beta, icl = 150000.0, 32.0, 1.0, 32.0, 128
    half = DH // 2
    freq = theta ** (np.arange(0, DH, 2, dtype=np.float32) / DH)
    low = half * math.log(icl / (beta * 2 * math.pi)) / math.log(theta)
    high = half * math.log(icl / (alpha * 2 * math.pi)) / math.log(theta)
    ramp = np.clip((np.arange(half, dtype=np.float32) - low) / (high - low), 0.0, 1.0)
    keep = 1.0 - ramp
    inv = (1.0 / (scaling * freq)) * (1.0 - keep) + (1.0 / freq) * keep
    ang = np.outer(np.arange(T, dtype=np.float32), inv)
    conc = 0.1 * math.log(scaling) + 1.0
    cos = (np.cos(ang) * conc).astype(np.float32)
    sin = (np.sin(ang) * conc).astype(np.float32)
    return np.concatenate([cos, cos], 1), np.concatenate([-sin, sin], 1)


def window_masks():
    i = np.arange(P)[:, None]
    j = np.arange(P)[None, :]
    diag = np.where(j > i, NEG, 0.0)
    behind = np.where(j <= i, NEG, 0.0)
    return np.concatenate([diag, behind, diag], 1).astype(np.float32)


def broadcast_rows(ap, rows=P):
    return ap.partition_broadcast(rows)


def self_attention(nc, dram, keep):
    G_UNITS = 3
    N_GROUPS = N_KV
    N_UNITS = G_UNITS * N_GROUPS
    N_QK = QT * QK_CHUNKS
    N_PROJ = QT * N_CHUNKS
    T_FILLS = QT * (Q_CHUNKS + 2)
    TR_FILLS = T_FILLS + N_UNITS
    N_PAIR = N_GROUPS // 2
    KEYS = P + 2 * P

    with ExitStack() as ctx:
        def sb(name, shape, dt=F32):
            return ctx.enter_context(nc.sbuf_tensor(name, shape, dt))

        def psum(name, shape, dt=F32):
            return ctx.enter_context(nc.psum_tensor(name, shape, dt))

        def sem(name):
            return ctx.enter_context(nc.semaphore(name))

        w_qkv = sb("w_qkv", [P, KT, QKV])
        b_qkv = sb("b_qkv", [P, QKV])
        w_out = sb("w_out", [P, N_PAIR, Q_MULT, D])
        b_out = sb("b_out", [P, D])
        sinks = sb("sinks", [P, N_HEADS])
        cos = sb("cos", [P, QT, DH])
        sin = sb("sin", [P, QT, DH])
        masks = sb("masks", [P, KEYS])
        masks_bf = sb("masks_bf", [P, KEYS], BF16)
        ident_bf = sb("ident_bf1", [P, P], BF16)
        half_power = sb("half_power1", [P, 1])

        xT = sb("xT", [P, KT, T])
        x_res = sb("x_res", [P, QT, D])
        x_bias = sb("x_bias", [P, QT, D])
        y = sb("y", [P, 3, CHUNK])
        y_cos = sb("y_cos", [P, 2, CHUNK])
        y_sin = sb("y_sin", [P, 3, CHUNK])
        roped = sb("roped", [P, 3, CHUNK])
        k_twice = sb("k_twice", [P, QT, N_KV, 2, DH])
        v = sb("v", [P, QT, N_KV, DH])
        qT = sb("qT", [P, N_HEADS // 2, T])
        kT = sb("kT", [P, N_KV, 2, T])
        negm = sb("negm", [P, 3, QT, Q_MULT])
        mx = sb("mx", [P, 3, QT, Q_MULT])
        sink_arg = sb("sink_arg", [P, 3, QT, Q_MULT])
        sink_exp = sb("sink_exp", [P, 3, QT, Q_MULT])
        sums = sb("sums", [P, 3, QT, Q_MULT])
        den = sb("den", [P, 3, QT, Q_MULT])
        rden = sb("rden", [P, 3, QT, Q_MULT])
        probs = sb("probs", [P, 3, Q_MULT, KEYS])
        probsT = sb("probsT", [P, 2, G_UNITS, CHUNK])
        oT = sb("oT", [P, N_PAIR, Q_MULT, T])
        z = sb("z", [P, QT, D])
        stats = sb("stats1", [P, QT, 6])
        mean_var = sb("mean_var1", [P, QT, 2])
        var_eps = sb("var_eps1", [P, QT, 1])
        rstd = sb("rstd1", [P, QT, 1])

        proj = [psum(f"proj{i}", [P, CHUNK]) for i in range(2)]
        turn = [psum(f"turn{i}", [P, CHUNK]) for i in range(2)]
        score = [psum(f"score{i}", [P, CHUNK]) for i in range(G_UNITS)]

        consts_in = sem("consts_in")
        consts_cast = sem("consts_cast")
        half_power_set = sem("half_power_set")
        kT_zeroed = sem("kT_zeroed")
        xT_in = sem("xT_in")
        x_in = sem("x_in")
        xb_ready = sem("xb_ready")
        proj_done = sem("proj_done")
        y_ready = sem("y_ready")
        cos_done = sem("cos_done")
        sin_done = sem("sin_done")
        roped_ready = sem("roped_ready")
        turn_done = sem("turn_done")
        turn_copied = sem("turn_copied")
        score_done = sem("score_done")
        mx_ready = sem("mx_ready")
        negm_ready = sem("negm_ready")
        exp_done = sem("exp_done")
        sink_arg_ready = sem("sink_arg_ready")
        sink_exp_done = sem("sink_exp_done")
        den_ready = sem("den_ready")
        rden_ready = sem("rden_ready")
        normed = sem("normed")
        pv_done = sem("pv_done")
        oT_copied = sem("oT_copied")
        out_done = sem("out_done")
        z_ready = sem("z_ready")
        stats_ready = sem("stats_ready")
        mv_ready = sem("mv_ready")
        var_ready = sem("var_ready")
        rstd_ready = sem("rstd_ready")
        x1_ready = sem("x1_ready")

        dve_seen = sem("dve_seen")

        def at(b, per_batch, count):
            return b * per_batch + (1 + count)

        block = ctx.enter_context(nc.Block())

        @block.sync
        def _(sp):
            sp.dma_start(w_qkv[:, :, :], dram["qkv_wT"].rearrange("(k p) n -> p k n", p=P)).then_inc(consts_in, 16)
            sp.dma_start(cos[:, :, :], dram["cos"].rearrange("(q p) n -> p q n", p=P)).then_inc(consts_in, 16)
            sp.dma_start(sin[:, :, :], dram["sin"].rearrange("(q p) n -> p q n", p=P)).then_inc(consts_in, 16)
            sp.dma_start(masks[:, :], dram["masks"]).then_inc(consts_in, 16)
            sp.dma_start(keep.ident[:, :], dram["ident"]).then_inc(consts_in, 16)
            sp.dma_start(b_qkv[:, :], broadcast_rows(dram["qkv_b"])).then_inc(consts_in, 16)
            sp.dma_start(sinks[:, :], broadcast_rows(dram["sinks"])).then_inc(consts_in, 16)
            sp.dma_start(b_out[:, :], broadcast_rows(dram["out_b"])).then_inc(consts_in, 16)
            sp.dma_start(w_out[:, :, :, :].rearrange("p g m n -> p (g m n)"), dram["out_wT"]).then_inc(consts_in, 16)
            with sp.Fori(0, B) as b:
                sp.wait_ge(proj_done, at(b, N_PROJ, 0))
                sp.dma_start(xT[:, :, :], dram["xT"][bass.ds(b, 1)].rearrange("a (k p) t -> p (a k) t", p=P))\
                  .then_inc(xT_in, 16)
                sp.wait_ge(xb_ready, at(b, 1, 0))
                sp.dma_start(x_res[:, :, :], dram["x"][bass.ds(b, 1)].rearrange("a (q p) d -> p (a q) d", p=P))\
                  .then_inc(x_in, 16)

        N_CONSTS = 9

        @block.tensor
        def _(pe):
            pe.wait_ge(consts_in, 16 * N_CONSTS)
            pe.wait_ge(consts_cast, 2)
            pe.wait_ge(kT_zeroed, 2)
            for s in (proj_done, turn_done, score_done, pv_done, out_done):
                pe.sem_inc(s, 1)
            with pe.Fori(0, B) as b:
                def claim_turn(f):
                    pe.wait_ge(turn_copied, at(b, TR_FILLS, max(f - 1, 0)))

                def turn_qk(i):
                    q, c = i // QK_CHUNKS, i % QK_CHUNKS
                    pe.wait_ge(roped_ready, at(b, N_QK, i + 1))
                    for part in range(1 if c < Q_CHUNKS else 2):
                        f = q * (Q_CHUNKS + 2) + c + part
                        claim_turn(f)
                        for n in range(4):
                            if c < Q_CHUNKS:
                                piece = roped[:, i % 3, n * P:(n + 1) * P]
                            else:
                                piece = k_twice[:, q, part * 4 + n, :, :].rearrange("p s d -> p (s d)")
                            mm = nc.tensor.transpose(turn[f % 2][:, n * P:(n + 1) * P], piece, keep.ident[:, :])
                        mm.then_inc(turn_done, 1)

                pe.wait_ge(xT_in, b * 16 + 16)
                for q in range(QT):
                    for c in range(N_CHUNKS):
                        j = q * N_CHUNKS + c
                        if j >= 2:
                            pe.wait_ge(y_ready, at(b, N_PROJ, j - 1))
                        else:
                            pe.wait_ge(z_ready, at(b, QT, 0))
                        for k in range(KT):
                            mm = nc.tensor.matmul(proj[j % 2][:, :], xT[:, k, q * P:(q + 1) * P],
                                                  w_qkv[:, k, c * CHUNK:(c + 1) * CHUNK],
                                                  start=(k == 0), stop=(k == KT - 1))
                        mm.then_inc(proj_done, 1)
                        i = q * QK_CHUNKS + c
                        if c < QK_CHUNKS and i >= 2:
                            turn_qk(i - 2)
                turn_qk(N_QK - 2)
                turn_qk(N_QK - 1)
                pe.wait_ge(turn_copied, at(b, TR_FILLS, T_FILLS))

                def scores(g):
                    for u in range(G_UNITS):
                        n = g * G_UNITS + u
                        pe.wait_ge(exp_done, at(b, N_UNITS, max(n - 2, 0)))
                        heads = range(4) if u == 0 else range(2 * u - 2, 2 * u)
                        q, w = (0, P) if u == 0 else (1, 2 * P)
                        m = masks_bf[:, 0:P] if u == 0 else masks_bf[:, P:KEYS]
                        nc.tensor.matmul(score[u][:, :], ident_bf[:, :],
                                         m.unsqueeze(1).broadcast_to([P, len(heads), w]), start=True, stop=False)
                        pairs = range(heads[0] // 2, (heads[-1] + 1) // 2)
                        for e, pair in enumerate(pairs):
                            mm = nc.tensor.matmul(score[u][:, e * 2 * w:(e + 1) * 2 * w],
                                                  qT[:, g * Q_MULT // 2 + pair, q * P:(q + 1) * P],
                                                  kT[:, g, :, 0:w], start=False, stop=(pair == pairs[-1]))
                        mm.then_inc(score_done, 1)

                def turn_probs(g):
                    pe.wait_ge(normed, at(b, N_GROUPS, g + 1))
                    for u in range(G_UNITS):
                        f = T_FILLS + g * G_UNITS + u
                        claim_turn(f)
                        for m in range(Q_MULT):
                            mm = nc.tensor.transpose(turn[f % 2][:, m * P:(m + 1) * P],
                                                     probs[:, g % 3, m, u * P:(u + 1) * P], keep.ident[:, :])
                        mm.then_inc(turn_done, 1)

                def weigh_values(pair):
                    pe.wait_ge(turn_copied, at(b, TR_FILLS, T_FILLS + (2 * pair + 2) * G_UNITS))
                    if pair:
                        pe.wait_ge(oT_copied, at(b, N_GROUPS, 2 * pair))
                    for u, (bank, tile, first) in enumerate(((0, 0, True), (1, 0, True), (1, 1, False))):
                        for s in range(2):
                            mm = nc.tensor.matmul(proj[bank][s * DH:(s + 1) * DH, :], v[:, tile, 2 * pair + s, :],
                                                  probsT[:, s, u, :], start=first, stop=(u != 1))
                    mm.then_inc(pv_done, 1)

                scores(0)
                scores(1)
                for g in range(N_GROUPS):
                    if g + 2 < N_GROUPS:
                        scores(g + 2)
                    if g % 2 == 0 and g:
                        weigh_values(g // 2 - 1)
                    turn_probs(g)
                weigh_values(N_PAIR - 1)

                pe.wait_ge(oT_copied, at(b, N_GROUPS, N_GROUPS))
                for q in range(QT):
                    for k in range(N_PAIR * Q_MULT):
                        mm = nc.tensor.matmul(proj[q][:, 0:D], oT[:, k // Q_MULT, k % Q_MULT, q * P:(q + 1) * P],
                                              w_out[:, k // Q_MULT, k % Q_MULT, :],
                                              start=(k == 0), stop=(k == N_PAIR * Q_MULT - 1))
                    mm.then_inc(out_done, 1)

        @block.vector
        def _(dve):
            dve.wait_ge(consts_in, 16 * N_CONSTS)
            nc.vector.memset(kT[0:DH, :, 1, :], 0.0).then_inc(kT_zeroed, 1)
            nc.vector.memset(kT[DH:P, :, 0, :], 0.0).then_inc(kT_zeroed, 1)
            nc.vector.tensor_copy(ident_bf[:, :], keep.ident[:, :]).then_inc(consts_cast, 1)
            nc.vector.tensor_copy(masks_bf[:, :], masks[:, :]).then_inc(consts_cast, 1)
            for s in (y_ready, cos_done, roped_ready, mx_ready, negm_ready, sink_arg_ready, den_ready,
                      rden_ready, z_ready, stats_ready, mv_ready, var_ready, x1_ready):
                dve.sem_inc(s, 1)
            with dve.Fori(0, B) as b:
                def add_sin(i):
                    dve.wait_ge(sin_done, at(b, N_QK, i + 1))
                    dve.wait_ge(cos_done, at(b, N_QK, i + 1))
                    c, before = i % QK_CHUNKS, i - 3
                    if before >= 0:
                        fills = (before // QK_CHUNKS) * (Q_CHUNKS + 2) + before % QK_CHUNKS + 1
                        fills += before % QK_CHUNKS == Q_CHUNKS
                        dve.wait_ge(turn_done, at(b, TR_FILLS, fills))
                    if c < Q_CHUNKS:
                        out, rope_cos, rope_sin = roped[:, i % 3, :], y_cos[:, i % 2, :], y_sin[:, i % 3, :]
                    else:
                        out = k_twice[:, i // QK_CHUNKS]
                        rope_cos, rope_sin = [
                            s.rearrange("p (h d) -> p h d", d=DH).unsqueeze(2).broadcast_to([P, N_KV, 2, DH])
                            for s in (y_cos[:, i % 2, :], y_sin[:, i % 3, :])]
                    nc.vector.tensor_tensor(out, rope_cos, rope_sin, ALU.add).then_inc(roped_ready, 1)

                i = 0
                for q in range(QT):
                    for c in range(N_CHUNKS):
                        j = q * N_CHUNKS + c
                        dve.wait_ge(proj_done, at(b, N_PROJ, j + 1))
                        if c < QK_CHUNKS:
                            if i >= 3:
                                dve.wait_ge(sin_done, at(b, N_QK, i - 2))
                            nc.vector.tensor_tensor(y[:, i % 3, :], proj[j % 2][:, :],
                                                    b_qkv[:, c * CHUNK:(c + 1) * CHUNK], ALU.add).then_inc(y_ready, 1)
                            if i:
                                add_sin(i - 1)
                            dve.wait_ge(y_ready, at(b, N_PROJ, j + 1))
                            nc.vector.tensor_tensor(
                                y_cos[:, i % 2, :].rearrange("p (h d) -> p h d", d=DH),
                                y[:, i % 3, :].rearrange("p (h d) -> p h d", d=DH),
                                cos[:, q, :].unsqueeze(1).broadcast_to([P, CHUNK // DH, DH]), ALU.mult)\
                              .then_inc(cos_done, 1)
                            i += 1
                        else:
                            nc.vector.tensor_tensor(v[:, q, :, :], proj[j % 2][:, :].rearrange("p (h d) -> p h d", d=DH),
                                                    b_qkv[:, c * CHUNK:].rearrange("p (h d) -> p h d", d=DH), ALU.add)\
                              .then_inc(y_ready, 1)
                add_sin(N_QK - 1)

                def maxima(g):
                    for u in range(G_UNITS):
                        n = g * G_UNITS + u
                        dve.wait_ge(score_done, at(b, N_UNITS, n + 1))
                        q, lo, hi = (0, 0, 4) if u == 0 else (1, 2 * u - 2, 2 * u)
                        nc.vector.tensor_reduce(mx[:, g % 3, q, lo:hi],
                                                score[u][:, :].rearrange("p (h k) -> p h k", h=hi - lo), AX_X, ALU.max)\
                          .then_inc(mx_ready, 1)
                        dve.wait_ge(mx_ready, at(b, N_UNITS, n + 1))
                        nc.vector.tensor_scalar(negm[:, g % 3, q, lo:hi], mx[:, g % 3, q, lo:hi], -SM_SCALE, None, ALU.mult)\
                          .then_inc(negm_ready, 1)
                    dve.wait_ge(negm_ready, at(b, N_UNITS, (g + 1) * G_UNITS))
                    nc.vector.tensor_tensor(sink_arg[:, g % 3], negm[:, g % 3],
                                            sinks[:, g * Q_MULT:(g + 1) * Q_MULT].unsqueeze(1).broadcast_to([P, QT, Q_MULT]),
                                            ALU.add).then_inc(sink_arg_ready, 1)

                def denominators(g):
                    dve.wait_ge(sink_exp_done, at(b, N_GROUPS, g + 1))
                    nc.vector.tensor_tensor(den[:, g % 3], sums[:, g % 3], sink_exp[:, g % 3], ALU.add)\
                      .then_inc(den_ready, 1)
                    dve.wait_ge(den_ready, at(b, N_GROUPS, g + 1))
                    if g >= 3:
                        dve.wait_ge(normed, at(b, N_GROUPS, g - 2))
                    nc.vector.reciprocal(rden[:, g % 3], den[:, g % 3]).then_inc(rden_ready, 1)

                for g in range(N_GROUPS + 1):
                    if g < N_GROUPS:
                        maxima(g)
                    if g:
                        denominators(g - 1)

                dve.wait_ge(xb_ready, at(b, 1, 1))
                for q in range(QT):
                    dve.wait_ge(out_done, at(b, QT, q + 1))
                    nc.vector.tensor_tensor(z[:, q, :], proj[q][:, 0:D], x_bias[:, q, :], ALU.add).then_inc(z_ready, 1)
                for q in range(QT):
                    dve.wait_ge(z_ready, at(b, QT, q + 1))
                    nc.vector.bn_stats(stats[:, q, :], z[:, q, :]).then_inc(stats_ready, 1)
                for q in range(QT):
                    dve.wait_ge(stats_ready, at(b, QT, q + 1))
                    dve.sem_inc(dve_seen, 1)
                    nc.vector.bn_aggr(mean_var[:, q, :], stats[:, q, :]).then_inc(mv_ready, 1)
                dve.wait_ge(mv_ready, at(b, QT, QT))
                nc.vector.tensor_scalar(var_eps[:, :, :], mean_var[:, :, 1:2], LN_EPS, None, ALU.add).then_inc(var_ready, 1)
                dve.wait_ge(rstd_ready, at(b, 1, 1))
                for q in range(QT):
                    nc.vector.tensor_scalar(keep.x[:, bass.ds(b * QT + q, 1), :], z[:, q:q + 1, :], mean_var[:, q, 0:1],
                                            rstd[:, q, :], ALU.subtract, ALU.mult).then_inc(x1_ready, 1)

        @block.gpsimd
        def _(pool):
            nc.gpsimd.memset(half_power[:, :], -0.5).then_inc(half_power_set, 1)
            for s in (xb_ready, sin_done, normed, rstd_ready):
                pool.sem_inc(s, 1)
            pool.wait_ge(consts_in, 16 * N_CONSTS)
            pool.wait_ge(half_power_set, 1)
            with pool.Fori(0, B) as b:
                pool.wait_ge(x_in, b * 16 + 16)
                pool.wait_ge(z_ready, at(b, QT, 0))
                nc.gpsimd.tensor_tensor(x_bias[:, :, :], x_res[:, :, :],
                                        b_out[:, :].unsqueeze(1).broadcast_to([P, QT, D]), ALU.add).then_inc(xb_ready, 1)
                i = 0
                for q in range(QT):
                    for c in range(QK_CHUNKS):
                        pool.wait_ge(y_ready, at(b, N_PROJ, q * N_CHUNKS + c + 1))
                        if i >= 3:
                            pool.wait_ge(roped_ready, at(b, N_QK, i - 2))
                        else:
                            pool.wait_ge(roped_ready, at(b, N_QK, 0))
                        for half in range(2):
                            lo, other = half * DH // 2, (1 - half) * DH // 2
                            op = nc.gpsimd.tensor_tensor(
                                y_sin[:, i % 3, :].rearrange("p (h d) -> p h d", d=DH)[:, :, lo:lo + DH // 2],
                                y[:, i % 3, :].rearrange("p (h d) -> p h d", d=DH)[:, :, other:other + DH // 2],
                                sin[:, q, lo:lo + DH // 2].unsqueeze(1).broadcast_to([P, CHUNK // DH, DH // 2]), ALU.mult)
                        op.then_inc(sin_done, 1)
                        i += 1
                for g in range(N_GROUPS):
                    pool.wait_ge(rden_ready, at(b, N_GROUPS, g + 1))
                    for q, lo, hi in ((0, 0, P), (1, P, KEYS)):
                        p = probs[:, g % 3, :, lo:hi]
                        op = nc.gpsimd.tensor_tensor(p, p, rden[:, g % 3, q, :].unsqueeze(2).broadcast_to([P, Q_MULT, hi - lo]),
                                                     ALU.mult)
                    op.then_inc(normed, 1)
                pool.wait_ge(var_ready, at(b, 1, 1))
                nc.gpsimd.tensor_tensor(rstd[:, :, 0], var_eps[:, :, 0], half_power[:, :].broadcast_to([P, QT]), ALU.pow)\
                  .then_inc(rstd_ready, 1)

        @block.scalar
        def _(act):
            for s in (turn_copied, exp_done, sink_exp_done, oT_copied):
                act.sem_inc(s, 1)
            with act.Fori(0, B) as b:
                f = 0
                for q in range(QT):
                    for c in range(Q_CHUNKS + 2):
                        act.wait_ge(turn_done, at(b, TR_FILLS, f + 1))
                        src = turn[f % 2][:, :].rearrange("p (n t) -> p n t", n=4)
                        if c < Q_CHUNKS:
                            op = nc.scalar.activation(qT[:, 4 * c:4 * c + 4, q * P:(q + 1) * P], src, ACT.Copy)
                        else:
                            for s in range(2):
                                rows, lo = slice(s * DH, (s + 1) * DH), 4 * (c - Q_CHUNKS)
                                op = nc.scalar.activation(kT[rows, lo:lo + 4, s, q * P:(q + 1) * P], src[rows], ACT.Copy)
                        op.then_inc(turn_copied, 1)
                        f += 1

                def exponentials(g):
                    for u in range(G_UNITS):
                        n = g * G_UNITS + u
                        act.wait_ge(negm_ready, at(b, N_UNITS, n + 1))
                        if u == 0:
                            if g >= 3:
                                act.wait_ge(turn_done, at(b, TR_FILLS, T_FILLS + (g - 2) * G_UNITS))
                                act.wait_ge(den_ready, at(b, N_GROUPS, g - 2))
                            heads, q, w = range(4), 0, P
                        else:
                            heads, q, w = range(2 * u - 2, 2 * u), 1, 2 * P
                        for e, m in enumerate(heads):
                            op = nc.scalar.activation(probs[:, g % 3, m, q * P:q * P + w], score[u][:, e * w:(e + 1) * w],
                                                      ACT.Exp, bias=negm[:, g % 3, q, m:m + 1], scale=SM_SCALE,
                                                      accum_out=sums[:, g % 3, q, m:m + 1])
                        op.then_inc(exp_done, 1)
                    act.wait_ge(sink_arg_ready, at(b, N_GROUPS, g + 1))
                    nc.scalar.activation(sink_exp[:, g % 3], sink_arg[:, g % 3], ACT.Exp).then_inc(sink_exp_done, 1)

                def copy_probs(g):
                    for u in range(G_UNITS):
                        f = T_FILLS + g * G_UNITS + u
                        act.wait_ge(turn_done, at(b, TR_FILLS, f + 1))
                        if u == 0 and g >= 2:
                            act.wait_ge(pv_done, at(b, N_PAIR, g // 2))
                        nc.scalar.activation(probsT[:, g % 2, u, :], turn[f % 2][:, :], ACT.Copy).then_inc(turn_copied, 1)

                def copy_outputs(pair):
                    act.wait_ge(pv_done, at(b, N_PAIR, pair + 1))
                    if pair == 0:
                        act.wait_ge(out_done, at(b, QT, 0))
                    for q in range(QT):
                        nc.scalar.activation(oT[:, pair, :, q * P:(q + 1) * P],
                                             proj[q][:, :].rearrange("p (m t) -> p m t", m=Q_MULT), ACT.Copy)\
                          .then_inc(oT_copied, 1)

                exponentials(0)
                exponentials(1)
                for g in range(N_GROUPS):
                    if g + 2 < N_GROUPS:
                        exponentials(g + 2)
                    if g % 2 == 0 and g:
                        copy_outputs(g // 2 - 1)
                    copy_probs(g)
                copy_outputs(N_PAIR - 1)


def cross_attention(nc, dram, keep):
    K_TILES = -(-L_ALL // P)
    MIX = L_IMG // P
    assert L_IMG % P == 1
    SIZE = [min(P, L_ALL - t * P) for t in range(K_TILES)]
    TXT_COLS = L_TXT // 3
    GH, N_GROUPS = 4, XH // 4
    UNITS = GH * QT
    ROW_MAX = 6 * XD
    ROW_MASK = ROW_MAX + 6
    N_EXTRA = 7
    V_COLS = 32
    LAG_RSTD, LAG_KN, LAG_PARTS, LAG_TURN = 2, 3, 4, 5
    STEPS = K_TILES + LAG_TURN
    N_S = N_GROUPS * K_TILES * 2
    N_PV = N_GROUPS * K_TILES

    with ExitStack() as ctx:
        def sb(name, shape, dt=F32):
            return ctx.enter_context(nc.sbuf_tensor(name, shape, dt))

        def psum(name, shape, dt=F32):
            return ctx.enter_context(nc.psum_tensor(name, shape, dt))

        def sem(name):
            return ctx.enter_context(nc.semaphore(name))

        ident_bf = sb("ident_bf2", [P, P], BF16)
        w_kv = [sb(f"w_kv{i}", [P, KT, 2, D]) for i in range(2)]
        b_kv = [sb(f"b_kv{i}", [P, 2, D]) for i in range(3)]
        g_k = [sb(f"g_k{i}", [P, D]) for i in range(3)]
        w_q = sb("w_q", [P, KT, D])
        b_q = sb("b_q", [P, D])
        g_q = sb("g_q", [P, D])
        w_o = sb("w_o", [P, KT, D])
        b_o = sb("b_o", [P, D])
        key_index = sb("key_index", [P, K_TILES])
        kinds = sb("kinds", [P, K_TILES, 6])
        half_power = sb("half_power2", [P, K_TILES])

        ctxT = sb("ctxT", [P, KT, L_ALL])
        mix = sb("mix", [P, 2, KT, P])
        len_i = sb("len_i", [P, 1], I32)
        len_f = sb("len_f", [P, 1])
        valid = sb("valid", [P, K_TILES])
        extra = sb("extra", [P, K_TILES, N_EXTRA], BF16)
        yk = sb("yk", [P, 5, D])
        junk = sb("junk", [P, 2, D])
        ssq = sb("ssq", [P, K_TILES])
        ms = sb("ms", [P, K_TILES])
        rstd_k = sb("rstd_k", [P, K_TILES])
        rstd_v = sb("rstd_v", [P, K_TILES])
        kn = sb("kn", [P, 2, D])
        k_rest = sb("k_rest", [P, 2, D])
        k_stack = sb("k_stack", [P, 2, XH, P], BF16)
        kT = sb("kTx", [P, XH, L_ALL], BF16)
        v1 = sb("v1", [P, K_TILES + 1, XH, V_COLS])

        x1c = sb("x1c", [P, QT, D])
        x1T = sb("x1T", [P, KT, T])
        yq = sb("yq", [P, QT, D])
        junk_q = sb("junk_q", [P, QT, D])
        ssq_q = sb("ssq_q", [P, QT])
        ms_q = sb("ms_q", [P, QT])
        rstd_q = sb("rstd_q", [P, QT])
        qn = sb("qn", [P, QT, D])
        q_rest = sb("q_rest", [P, QT, D])
        q_stack = sb("q_stack", [P, QT, XH, P], BF16)
        qT0 = sb("qT0", [P, XH, T], BF16)
        qT = sb("qTx", [P, 2, GH, T], BF16)
        mx = sb("mx2", [P, QT, GH, 2])
        m_rest = sb("m_rest", [P, QT * GH * 2])
        m_parts = sb("m_parts", [P, QT * GH * 2, 3], BF16)
        probs = sb("probs2", [P, 6, 2, T])
        o_sb = sb("o_sb", [P, 2, T])
        rden = sb("rden2", [P, 2 * QT * GH])
        o_norm = sb("o_norm", [P, 2, QT, GH * XD])
        attn = sb("attn", [P, QT, D])
        attnT = sb("attnT", [P, KT, T])
        x_bias = x1c
        z = sb("z2", [P, QT, D])
        x2 = z
        stats = sb("stats2", [P, QT, 6])
        mean_var = sb("mean_var2", [P, QT, 2])
        var_eps = sb("var_eps2", [P, QT])
        rstd = sb("rstd2", [P, QT])

        score = [psum(f"xscore{i}", [P, 512]) for i in range(2)]
        wide = psum("wide", [P, 4, 512])
        outs = psum("outs", [P, 2, T])
        turn = psum("xturn", [P, 512])
        turn_bf = turn[:, :].bitcast(BF16)
        wide_bf = [wide[:, i, :].bitcast(BF16) for i in range(4)]

        consts_in, w_in = sem("consts_in2"), sem("w_in2")
        consts_set = sem("consts_set2")
        pool_set = sem("pool_set2")
        stack_set = sem("stack_set2")
        ctx_in, len_in = sem("ctx_in"), sem("len_in")
        mix_ready, len_ready, valid_ready, mask_ready = [sem(n) for n in ("mix_ready", "len_ready", "valid_ready", "mask_ready")]
        kv_done, kb_ready, vb_ready, ssq_done = [sem(n) for n in ("kv_done", "kb_ready", "vb_ready", "ssq_done")]
        ms_ready, rstd_ready, rv_ready, kn_ready = [sem(n) for n in ("ms_ready", "rstd_ready", "rv_ready", "kn_ready")]
        hi_done, rest_ready, mid_ready, lo_ready = [sem(n) for n in ("hi_done", "rest_ready", "mid_ready", "lo_ready")]
        extra_done, kturn_done, kcopy_act, kcopy_dve = [sem(n) for n in ("extra_done", "kturn_done", "kcopy_act", "kcopy_dve")]
        vmix_ready = sem("vmix_ready")
        x1c_ready, xb_ready, x1T_done, x1T_copied = [sem(n) for n in ("x1c_ready", "xb_ready2", "x1T_done", "x1T_copied")]
        qp_done, yq_ready, ssq_q_done, ms_q_ready = [sem(n) for n in ("qp_done", "yq_ready", "ssq_q_done", "ms_q_ready")]
        rstd_q_ready, qn_ready, q_hi, q_rest_ready = [sem(n) for n in ("rstd_q_ready", "qn_ready", "q_hi", "q_rest_ready")]
        q_mid, q_lo, q_zeroed, qturn_done, qT0_copied = [sem(n) for n in ("q_mid", "q_lo", "q_zeroed", "qturn_done", "qT0_copied")]
        wide_img, wide_txt, mx_img, mx_txt = [sem(n) for n in ("wide_img", "wide_txt", "mx_img", "mx_txt")]
        m_step, m_written, mturn_done, qT_copied = [sem(n) for n in ("m_step", "m_written", "mturn_done", "qT_copied")]
        s_done, exp_done, pv_done, o_copied = [sem(n) for n in ("s_done", "exp_done2", "pv_done2", "o_copied")]
        oturn_done, rden_ready, norm_ready, attn_ready = [sem(n) for n in ("oturn_done", "rden_ready2", "norm_ready", "attn_ready")]
        aturn_done, attnT_copied, wo_done, z_ready = [sem(n) for n in ("aturn_done", "attnT_copied", "wo_done", "z_ready2")]
        stats_ready, mv_ready, var_ready, ln_rstd = [sem(n) for n in ("stats_ready2", "mv_ready2", "var_ready2", "ln_rstd")]
        x2_ready, x2_kept, hturn_done, hT_copied = [sem(n) for n in ("x2_ready", "x2_kept", "hturn_done", "hT_copied")]

        sp_seen, pe_seen, dve_seen, pool_seen = [sem(n) for n in ("sp_seen", "pe_seen2", "dve_seen2", "pool_seen")]

        def at(b, per_batch, count):
            return b * per_batch + (1 + count)

        def kind(t):
            return 0 if t < MIX else 2 if t == MIX else 1

        N_W, N_C = 6, 17

        block = ctx.enter_context(nc.Block())

        @block.sync
        def _(sp):
            rows = lambda name: dram[name].rearrange("(k p) n -> p k n", p=P)
            for i, tag in enumerate(("_img", "")):
                sp.dma_start(w_kv[i][:, :, 0, :], rows("w_k" + tag)).then_inc(w_in, 16)
                sp.dma_start(w_kv[i][:, :, 1, :], rows("w_v" + tag)).then_inc(w_in, 16)
            sp.dma_start(w_q[:, :, :], rows("w_q")).then_inc(w_in, 16)
            sp.dma_start(w_o[:, :, :], rows("w_o")).then_inc(w_in, 16)
            for i, parts in enumerate(((("_img", 0, P),), (("", 0, P),), (("_img", 0, 1), ("", 1, P)))):
                for tag, lo, hi in parts:
                    sp.dma_start(b_kv[i][lo:hi, 0, :], broadcast_rows(dram["b_k" + tag], hi - lo)).then_inc(consts_in, 16)
                    sp.dma_start(b_kv[i][lo:hi, 1, :], broadcast_rows(dram["b_v" + tag], hi - lo)).then_inc(consts_in, 16)
                    sp.dma_start(g_k[i][lo:hi, :], broadcast_rows(dram["g_k" + tag], hi - lo)).then_inc(consts_in, 16)
            sp.dma_start(b_q[:, :], broadcast_rows(dram["b_q"])).then_inc(consts_in, 16)
            sp.dma_start(g_q[:, :], broadcast_rows(dram["g_q"])).then_inc(consts_in, 16)
            sp.dma_start(b_o[:, :], broadcast_rows(dram["b_o"])).then_inc(consts_in, 16)
            sp.dma_start(key_index[:, :], dram["key_index"]).then_inc(consts_in, 16)
            sp.dma_start(kinds[:, :, :], dram["kinds"].rearrange("p (t n) -> p t n", n=6)).then_inc(consts_in, 16)
            with sp.Fori(0, B) as b:
                sp.wait_ge(kv_done, at(b, K_TILES, 0))
                sp.dma_start(ctxT[:, :, :], dram["ctxT"][bass.ds(b, 1)].rearrange("a (k p) t -> p (a k) t", p=P))\
                  .then_inc(ctx_in, 16)
                sp.wait_ge(len_ready, at(b, 1, 0))
                sp.sem_inc(sp_seen, 1)
                sp.dma_start(len_i[:, :], dram["lens"][:, bass.ds(b, 1)].partition_broadcast(P)).then_inc(len_in, 16)

        @block.tensor
        def _(pe):
            for s in (kv_done, kturn_done, x1T_done, qp_done, qturn_done, wide_img, wide_txt, mturn_done, s_done,
                      pv_done, oturn_done, aturn_done, wo_done, hturn_done):
                pe.sem_inc(s, 1)
            pe.wait_ge(w_in, 16 * N_W)
            pe.wait_ge(consts_set, 3)
            pe.wait_ge(pool_set, 3)
            pe.wait_ge(stack_set, 4)
            with pe.Fori(0, B) as b:
                def project_kv(t):
                    if t >= 2:
                        pe.wait_ge(vb_ready, at(b, K_TILES, t - 1))
                    else:
                        pe.wait_ge(z_ready, at(b, QT, 0))
                    n = SIZE[t]
                    if t == MIX:
                        pe.wait_ge(mix_ready, at(b, 1, 1))
                        parts = [(mix[:, i, k, :], w_kv[i][:, k]) for i in range(2) for k in range(KT)]
                    else:
                        parts = [(ctxT[:, k, t * P:t * P + n], w_kv[t > MIX][:, k]) for k in range(KT)]
                    for i, (keys, w) in enumerate(parts):
                        mm = nc.tensor.matmul(score[t % 2][0:n, :], keys, w.rearrange("p s d -> p (s d)"),
                                              start=(i == 0), stop=(i == len(parts) - 1))
                    mm.then_inc(kv_done, 1)

                def turn_keys(t):
                    n = SIZE[t]
                    pe.wait_ge(lo_ready, at(b, K_TILES, t + 1))
                    pe.wait_ge(extra_done, at(b, K_TILES, t + 1))
                    for half in range(2):
                        f = 2 * t + half
                        if t >= 2:
                            pe.wait_ge(kcopy_dve if half else kcopy_act, at(b, K_TILES, t - 1))
                        for e in range(8):
                            mm = nc.tensor.transpose(wide_bf[f % 4][:, e * P:e * P + n],
                                                     k_stack[0:n, t % 2, 8 * half + e, :], ident_bf[0:n, 0:n])
                        mm.then_inc(kturn_done, 1)

                def turn_x1():
                    pe.wait_ge(x1c_ready, at(b, 1, 1))
                    pe.wait_ge(hT_copied, at(b, 1, 0))
                    for q in range(QT):
                        for k in range(KT):
                            mm = nc.tensor.transpose(turn[:, k * T + q * P:k * T + (q + 1) * P],
                                                     x1c[:, q, k * P:(k + 1) * P], keep.ident[:, :])
                    mm.then_inc(x1T_done, 1)

                def project_q():
                    pe.wait_ge(x1T_copied, at(b, 1, 1))
                    for q in range(QT):
                        for k in range(KT):
                            mm = nc.tensor.matmul(turn[:, q * D:(q + 1) * D], x1T[:, k, q * P:(q + 1) * P], w_q[:, k, :],
                                                  start=(k == 0), stop=(k == KT - 1))
                    mm.then_inc(qp_done, 1)

                def turn_q(f):
                    q, half = f // 2, f % 2
                    if f == 0:
                        pe.wait_ge(q_lo, at(b, 1, 1))
                        pe.wait_ge(q_zeroed, at(b, 1, 1))
                    else:
                        pe.wait_ge(qT0_copied, at(b, 4, f))
                    for e in range(8):
                        mm = nc.tensor.transpose(turn_bf[:, e * P:(e + 1) * P], q_stack[:, q, 8 * half + e, :], ident_bf[:, :])
                    mm.then_inc(qturn_done, 1)

                side = {0: [turn_x1], 2: [project_q]}
                for i in range(4):
                    side[6 + 2 * i] = [lambda i=i: turn_q(i)]
                pe.wait_ge(ctx_in, b * 16 + 16)
                for step in range(STEPS):
                    if step < K_TILES:
                        project_kv(step)
                    for f in side.get(step, ()):
                        f()
                    if step >= LAG_TURN:
                        turn_keys(step - LAG_TURN)

                def max_unit(g, n):
                    u = g * UNITS + n
                    h, q = g * GH + n // QT, n % QT
                    if g == 0 and n == 0:
                        pe.wait_ge(qT0_copied, at(b, 4, 4))
                        pe.wait_ge(kcopy_dve, at(b, K_TILES, K_TILES))
                        pe.wait_ge(kcopy_act, at(b, K_TILES, K_TILES))
                    query = qT0[:, h, q * P:(q + 1) * P]
                    pe.wait_ge(mx_img, at(b, N_GROUPS * UNITS, u))
                    nc.tensor.matmul(wide[:, 0, 0:L_IMG], query, kT[:, h, 0:L_IMG], start=True, stop=True).then_inc(wide_img, 1)
                    pe.wait_ge(mx_txt, at(b, N_GROUPS * UNITS, u))
                    for i in range(3):
                        lo = L_IMG + i * TXT_COLS
                        mm = nc.tensor.matmul(wide[:, 1 + i, 0:TXT_COLS], query, kT[:, h, lo:lo + TXT_COLS],
                                              start=True, stop=True)
                    mm.then_inc(wide_txt, 1)

                def turn_maxima(g):
                    pe.wait_ge(m_written, at(b, N_GROUPS, g + 1))
                    for e in range(GH):
                        for q in range(QT):
                            mm = nc.tensor.transpose(turn_bf[:, e * T + q * P:e * T + (q + 1) * P],
                                                     q_stack[:, q, g * GH + e, :], ident_bf[:, :])
                    mm.then_inc(mturn_done, 1)

                def scores(g, t):
                    n = SIZE[t]
                    if t == 0:
                        pe.wait_ge(qT_copied, at(b, N_GROUPS, g + 1))
                    for pair in range(2):
                        m = (g * K_TILES + t) * 2 + pair
                        pe.wait_ge(exp_done, at(b, N_S, max(m - 1, 0)))
                        for e in range(2):
                            j = 2 * pair + e
                            mm = nc.tensor.matmul(score[pair][0:n, e * T:(e + 1) * T], kT[:, g * GH + j, t * P:t * P + n],
                                                  qT[:, g % 2, j, :], start=True, stop=True)
                        mm.then_inc(s_done, 1)

                def weigh_values(g, t):
                    n = SIZE[t]
                    slot = (g * K_TILES + t) * 2
                    if t == 0:
                        pe.wait_ge(o_copied, at(b, N_GROUPS, g))
                        if g == 0:
                            pe.wait_ge(vmix_ready, at(b, 1, 1))
                    pe.wait_ge(exp_done, at(b, N_S, slot + 2))
                    if t == MIX:
                        pe.sem_inc(pe_seen, 1)
                    for side_, v_tile, rows in ([(0, t, n)] if t < MIX else [(0, t, 1), (1, K_TILES, n)] if t == MIX
                                                else [(1, t, n)]):
                        first = (side_ == 0 and t == 0) or (side_ == 1 and t == MIX)
                        last = (side_ == 0 and t == MIX) or (side_ == 1 and t == K_TILES - 1)
                        for j in range(GH):
                            mm = nc.tensor.matmul(outs[32 * j:32 * j + V_COLS, side_, :], v1[0:rows, v_tile, g * GH + j, :],
                                                  probs[0:rows, (slot + j // 2) % 6, j % 2, :], start=first, stop=last)
                    mm.then_inc(pv_done, 1)

                def turn_outputs(g):
                    pe.wait_ge(o_copied, at(b, N_GROUPS, g + 1))
                    if g + 1 < N_GROUPS:
                        pe.wait_ge(qT_copied, at(b, N_GROUPS, g + 2))
                    else:
                        pe.wait_ge(norm_ready, at(b, N_GROUPS, g))
                    for s in range(2):
                        for q in range(QT):
                            i = s * QT + q
                            mm = nc.tensor.transpose(turn[:, i * P:(i + 1) * P], o_sb[:, s, q * P:(q + 1) * P], keep.ident[:, :])
                    mm.then_inc(oturn_done, 1)

                for n in range(UNITS):
                    max_unit(0, n)
                turn_maxima(0)
                for g in range(N_GROUPS):
                    scores(g, 0)
                    for t in range(K_TILES):
                        if t + 1 < K_TILES:
                            scores(g, t + 1)
                        if g + 1 < N_GROUPS and t < UNITS:
                            max_unit(g + 1, t)
                        weigh_values(g, t)
                        if t == 3 and g:
                            turn_outputs(g - 1)
                        if t == K_TILES - 2 and g + 1 < N_GROUPS:
                            if g:
                                pe.wait_ge(norm_ready, at(b, N_GROUPS, g))
                            turn_maxima(g + 1)
                turn_outputs(N_GROUPS - 1)

                pe.wait_ge(attn_ready, at(b, N_GROUPS, N_GROUPS))
                for q in range(QT):
                    for k in range(KT):
                        mm = nc.tensor.transpose(turn[:, k * T + q * P:k * T + (q + 1) * P], attn[:, q, k * P:(k + 1) * P],
                                                 keep.ident[:, :])
                mm.then_inc(aturn_done, 1)
                pe.wait_ge(attnT_copied, at(b, 1, 1))
                for q in range(QT):
                    for k in range(KT):
                        mm = nc.tensor.matmul(score[q][:, 0:D], attnT[:, k, q * P:(q + 1) * P], w_o[:, k, :],
                                              start=(k == 0), stop=(k == KT - 1))
                    mm.then_inc(wo_done, 1)
                pe.wait_ge(x2_ready, at(b, QT, QT))
                for q in range(QT):
                    for k in range(KT):
                        mm = nc.tensor.transpose(turn[:, k * T + q * P:k * T + (q + 1) * P], x2[:, q, k * P:(k + 1) * P],
                                                 keep.ident[:, :])
                mm.then_inc(hturn_done, 1)

        @block.vector
        def _(dve):
            for s in (len_ready, valid_ready, mask_ready, kb_ready, vb_ready, ms_ready, rv_ready, kn_ready, rest_ready,
                      mid_ready, lo_ready, kcopy_dve, yq_ready, ms_q_ready, qn_ready, q_hi, q_rest_ready, q_mid, q_lo,
                      mx_img, mx_txt, m_step, m_written, qT_copied, rden_ready, norm_ready, attn_ready, z_ready,
                      stats_ready, mv_ready, var_ready, x2_ready):
                dve.sem_inc(s, 1)
            dve.wait_ge(consts_in, 16 * N_C)
            nc.vector.tensor_copy(ident_bf[:, :], keep.ident[:, :]).then_inc(consts_set, 1)
            nc.vector.tensor_scalar(g_q[:, :], g_q[:, :], 1.0 / math.sqrt(XD), None, ALU.mult).then_inc(consts_set, 1)
            nc.vector.tensor_copy(extra[:, :, 0:6], kinds[:, :, :]).then_inc(consts_set, 1)
            dve.wait_ge(consts_set, 3)
            dve.wait_ge(pool_set, 3)
            dve.wait_ge(stack_set, 4)
            with dve.Fori(0, B) as b:
                dve.wait_ge(len_in, b * 16 + 16)
                nc.vector.tensor_scalar(len_f[:, :], len_i[:, :], 0.0, None, ALU.max).then_inc(len_ready, 1)
                dve.wait_ge(len_ready, at(b, 1, 1))
                nc.vector.tensor_scalar(valid[:, :], key_index[:, :], len_f[:, :], None, ALU.is_lt).then_inc(valid_ready, 1)
                dve.wait_ge(valid_ready, at(b, 1, 1))
                nc.vector.tensor_scalar(extra[:, :, 6], valid[:, :], -1.0, 1.0e9, ALU.add, ALU.mult).then_inc(mask_ready, 1)

                def add_bias(t):
                    n, c = SIZE[t], kind(t)
                    dve.wait_ge(kv_done, at(b, K_TILES, t + 1))
                    nc.vector.tensor_tensor(yk[0:n, t % 5, :], score[t % 2][0:n, 0:D], b_kv[c][0:n, 0, :], ALU.add)\
                      .then_inc(kb_ready, 1)
                    nc.vector.tensor_tensor(v1[0:n, t, :, 0:XD], score[t % 2][0:n, D:2 * D].rearrange("p (h d) -> p h d", h=XH),
                                            b_kv[c][0:n, 1, :].rearrange("p (h d) -> p h d", h=XH), ALU.add)\
                      .then_inc(vb_ready, 1)

                def mean_square(t):
                    n = SIZE[t]
                    dve.wait_ge(ssq_done, at(b, K_TILES, t + 1))
                    nc.vector.tensor_scalar(ms[0:n, t:t + 1], ssq[0:n, t:t + 1], 1.0 / D, RMS_EPS, ALU.mult, ALU.add)\
                      .then_inc(ms_ready, 1)

                def normalize(t):
                    n = SIZE[t]
                    dve.wait_ge(rstd_ready, at(b, K_TILES, t + 1))
                    nc.vector.tensor_tensor(rstd_v[0:n, t:t + 1], rstd_k[0:n, t:t + 1], valid[0:n, t:t + 1], ALU.mult)\
                      .then_inc(rv_ready, 1)
                    dve.wait_ge(rv_ready, at(b, K_TILES, t + 1))
                    nc.vector.scalar_tensor_tensor(out=kn[0:n, t % 2, :], in0=yk[0:n, t % 5, :], scalar=rstd_v[0:n, t:t + 1],
                                                   in1=g_k[kind(t)][0:n, :], op0=ALU.mult, op1=ALU.mult).then_inc(kn_ready, 1)

                def heads_of(flat, n):
                    return flat.rearrange("p (h d) -> p h d", h=XH)

                def split_rest(t):
                    n, stack = SIZE[t], k_stack[0:SIZE[t], t % 2]
                    dve.wait_ge(hi_done, at(b, K_TILES, t + 1))
                    rest = heads_of(k_rest[0:n, t % 2, :], n)
                    nc.vector.tensor_tensor(rest, heads_of(kn[0:n, t % 2, :], n), stack[:, :, 0:XD], ALU.subtract)\
                      .then_inc(rest_ready, 1)
                    dve.wait_ge(rest_ready, at(b, K_TILES, t + 1))
                    nc.vector.tensor_copy(stack[:, :, 3 * XD:5 * XD].rearrange("p h (s d) -> p h s d", s=2),
                                          rest.unsqueeze(2).broadcast_to([n, XH, 2, XD])).then_inc(mid_ready, 1)
                    dve.wait_ge(mid_ready, at(b, K_TILES, t + 1))
                    nc.vector.tensor_tensor(stack[:, :, 5 * XD:6 * XD], rest, stack[:, :, 3 * XD:4 * XD], ALU.subtract)\
                      .then_inc(lo_ready, 1)

                def copy_keys(t):
                    n = SIZE[t]
                    dve.wait_ge(kturn_done, at(b, 2 * K_TILES, 2 * t + 2))
                    nc.vector.tensor_copy(kT[:, 8:16, t * P:t * P + n],
                                          wide_bf[(2 * t + 1) % 4].rearrange("p (h k) -> p h k", h=8)[:, :, 0:n])\
                      .then_inc(kcopy_dve, 1)

                def bias_q():
                    dve.wait_ge(qp_done, at(b, 1, 1))
                    nc.vector.tensor_tensor(yq[:, :, :], turn[:, :].rearrange("p (q d) -> p q d", q=QT),
                                            b_q[:, :].unsqueeze(1).broadcast_to([P, QT, D]), ALU.add).then_inc(yq_ready, 1)

                def mean_square_q():
                    dve.wait_ge(ssq_q_done, at(b, QT, QT))
                    nc.vector.tensor_scalar(ms_q[:, :], ssq_q[:, :], 1.0 / D, RMS_EPS, ALU.mult, ALU.add)\
                      .then_inc(ms_q_ready, 1)

                def normalize_q():
                    dve.wait_ge(rstd_q_ready, at(b, 1, 1))
                    for q in range(QT):
                        nc.vector.scalar_tensor_tensor(out=qn[:, q, :], in0=yq[:, q, :], scalar=rstd_q[:, q:q + 1],
                                                       in1=g_q[:, :], op0=ALU.mult, op1=ALU.mult).then_inc(qn_ready, 1)

                def split_q(q):
                    dve.wait_ge(qn_ready, at(b, QT, QT))
                    stack, whole, rest = q_stack[:, q], heads_of(qn[:, q, :], P), heads_of(q_rest[:, q, :], P)
                    for s in (0, 3, 5):
                        nc.vector.tensor_copy(stack[:, :, s * XD:(s + 1) * XD], whole).then_inc(q_hi, 1)
                    dve.wait_ge(q_hi, at(b, 3 * QT, 3 * q + 3))
                    nc.vector.tensor_tensor(rest, whole, stack[:, :, 0:XD], ALU.subtract).then_inc(q_rest_ready, 1)
                    dve.wait_ge(q_rest_ready, at(b, QT, q + 1))
                    for s in (1, 4):
                        nc.vector.tensor_copy(stack[:, :, s * XD:(s + 1) * XD], rest).then_inc(q_mid, 1)
                    dve.wait_ge(q_mid, at(b, 2 * QT, 2 * q + 2))
                    op = nc.vector.tensor_tensor(stack[:, :, 2 * XD:3 * XD], rest, stack[:, :, XD:2 * XD], ALU.subtract)
                    if q == QT - 1:
                        op.then_inc(q_lo, 1)

                side = {2: [bias_q], 3: [mean_square_q], 4: [normalize_q], 5: [lambda: split_q(0), lambda: split_q(1)]}
                for step in range(STEPS + 1):
                    if step < K_TILES:
                        add_bias(step)
                    for f in side.get(step, ()):
                        f()
                    if 0 <= step - LAG_RSTD < K_TILES:
                        mean_square(step - LAG_RSTD)
                    if 0 <= step - LAG_KN < K_TILES:
                        normalize(step - LAG_KN)
                    if 0 <= step - LAG_PARTS < K_TILES:
                        split_rest(step - LAG_PARTS)
                    if 0 <= step - LAG_TURN - 1 < K_TILES:
                        copy_keys(step - LAG_TURN - 1)

                def maxima(g, n):
                    u, e, q = g * UNITS + n, n // QT, n % QT
                    dve.wait_ge(wide_img, at(b, N_GROUPS * UNITS, u + 1))
                    nc.vector.tensor_reduce(mx[:, q, e, 0:1], wide[:, 0, 0:L_IMG], AX_X, ALU.max).then_inc(mx_img, 1)
                    dve.wait_ge(wide_txt, at(b, N_GROUPS * UNITS, u + 1))
                    nc.vector.tensor_reduce(mx[:, q, e, 1:2], wide[:, 1:4, 0:TXT_COLS], mybir.AxisListType.XY, ALU.max)\
                      .then_inc(mx_txt, 1)

                def write_maxima(g):
                    flat = mx[:, :, :, :].rearrange("p q h s -> p (q h s)")
                    dve.wait_ge(mx_img, at(b, N_GROUPS * UNITS, (g + 1) * UNITS))
                    dve.wait_ge(mx_txt, at(b, N_GROUPS * UNITS, (g + 1) * UNITS))
                    nc.vector.tensor_scalar(m_parts[:, :, 0], flat, -1.0, None, ALU.mult).then_inc(m_step, 1)
                    dve.wait_ge(m_step, at(b, 4 * N_GROUPS, 4 * g + 1))
                    nc.vector.scalar_tensor_tensor(out=m_rest[:, :], in0=flat, scalar=-1.0, in1=m_parts[:, :, 0],
                                                   op0=ALU.mult, op1=ALU.subtract).then_inc(m_step, 1)
                    dve.wait_ge(m_step, at(b, 4 * N_GROUPS, 4 * g + 2))
                    nc.vector.tensor_copy(m_parts[:, :, 1], m_rest[:, :]).then_inc(m_step, 1)
                    dve.wait_ge(m_step, at(b, 4 * N_GROUPS, 4 * g + 3))
                    nc.vector.tensor_tensor(m_parts[:, :, 2], m_rest[:, :], m_parts[:, :, 1], ALU.subtract).then_inc(m_step, 1)
                    dve.wait_ge(m_step, at(b, 4 * N_GROUPS, 4 * g + 4))
                    nc.vector.tensor_copy(q_stack[:, :, g * GH:(g + 1) * GH, ROW_MAX:ROW_MAX + 6],
                                          m_parts[:, :, :].rearrange("p (q h s) r -> p q h (s r)", q=QT, h=GH))\
                      .then_inc(m_written, 1)
                    dve.wait_ge(mturn_done, at(b, N_GROUPS, g + 1))
                    nc.vector.tensor_copy(qT[:, g % 2, :, :], turn_bf.rearrange("p (h t) -> p h t", h=GH)).then_inc(qT_copied, 1)

                def normalize_outputs(g):
                    dve.wait_ge(oturn_done, at(b, N_GROUPS, g + 1))
                    raw = turn[:, :].rearrange("p (n c) -> p n c", c=V_COLS)
                    nc.vector.reciprocal(rden[:, :], raw[:, :, XD]).then_inc(rden_ready, 1)
                    dve.wait_ge(rden_ready, at(b, N_GROUPS, g + 1))
                    nc.vector.tensor_tensor(o_norm[:, :, :, :].rearrange("p s q (h d) -> p (s q h) d", d=XD), raw[:, :, 0:XD],
                                            rden[:, :].unsqueeze(2).broadcast_to([P, 2 * QT * GH, XD]), ALU.mult)\
                      .then_inc(norm_ready, 1)
                    dve.wait_ge(norm_ready, at(b, N_GROUPS, g + 1))
                    nc.vector.tensor_tensor(attn[:, :, g * GH * XD:(g + 1) * GH * XD], o_norm[:, 0], o_norm[:, 1], ALU.add)\
                      .then_inc(attn_ready, 1)

                for n in range(UNITS):
                    maxima(0, n)
                write_maxima(0)
                for g in range(N_GROUPS):
                    if g + 1 < N_GROUPS:
                        for n in range(UNITS):
                            maxima(g + 1, n)
                            if n == 4 and g:
                                normalize_outputs(g - 1)
                        write_maxima(g + 1)
                    elif g:
                        normalize_outputs(g - 1)
                normalize_outputs(N_GROUPS - 1)

                dve.wait_ge(xb_ready, at(b, 1, 1))
                dve.wait_ge(hturn_done, at(b, 1, 0))
                dve.wait_ge(x2_kept, at(b, 1, 0))
                for q in range(QT):
                    dve.wait_ge(wo_done, at(b, QT, q + 1))
                    nc.vector.tensor_tensor(z[:, q, :], score[q][:, 0:D], x_bias[:, q, :], ALU.add).then_inc(z_ready, 1)
                for q in range(QT):
                    dve.wait_ge(z_ready, at(b, QT, q + 1))
                    nc.vector.bn_stats(stats[:, q, :], z[:, q, :]).then_inc(stats_ready, 1)
                for q in range(QT):
                    dve.wait_ge(stats_ready, at(b, QT, q + 1))
                    dve.sem_inc(dve_seen, 1)
                    nc.vector.bn_aggr(mean_var[:, q, :], stats[:, q, :]).then_inc(mv_ready, 1)
                dve.wait_ge(mv_ready, at(b, QT, QT))
                nc.vector.tensor_scalar(var_eps[:, :], mean_var[:, :, 1], LN_EPS, None, ALU.add).then_inc(var_ready, 1)
                dve.wait_ge(ln_rstd, at(b, 1, 1))
                for q in range(QT):
                    nc.vector.tensor_scalar(x2[:, q, :], z[:, q, :], mean_var[:, q, 0:1], rstd[:, q:q + 1],
                                            ALU.subtract, ALU.mult).then_inc(x2_ready, 1)

        @block.gpsimd
        def _(pool):
            for s in (mix_ready, rstd_ready, extra_done, vmix_ready, x1c_ready, xb_ready, rstd_q_ready, q_zeroed, ln_rstd,
                      x2_kept):
                pool.sem_inc(s, 1)
            nc.gpsimd.memset(mix[:, :, :, :], 0.0).then_inc(pool_set, 1)
            nc.gpsimd.memset(half_power[:, :], -0.5).then_inc(pool_set, 1)
            nc.gpsimd.memset(k_stack[:, :, :, ROW_MASK + 1:P], 0.0).then_inc(pool_set, 1)
            nc.gpsimd.memset(q_stack[:, :, :, ROW_MASK + 1:P], 0.0).then_inc(stack_set, 1)
            nc.gpsimd.memset(q_stack[:, :, :, ROW_MASK:ROW_MASK + 1], 1.0).then_inc(stack_set, 1)
            nc.gpsimd.memset(v1[:, :, :, XD:XD + 1], 1.0).then_inc(stack_set, 1)
            nc.gpsimd.memset(v1[:, :, :, XD + 1:V_COLS], 0.0).then_inc(stack_set, 1)
            pool.wait_ge(pool_set, 3)
            pool.wait_ge(stack_set, 4)
            pool.wait_ge(consts_set, 3)
            pool.wait_ge(consts_in, 16 * N_C)
            with pool.Fori(0, B) as b:
                pool.wait_ge(z_ready, at(b, QT, 0))
                pool.sem_inc(pool_seen, 1)
                nc.gpsimd.tensor_copy(x1c[:, :, :], keep.x[:, bass.ds(b * QT, QT), :]).then_inc(x1c_ready, 1)
                pool.wait_ge(ctx_in, b * 16 + 16)
                pool.wait_ge(kv_done, at(b, K_TILES, 0))
                pool.sem_inc(pool_seen, 1)
                nc.gpsimd.tensor_copy(mix[:, 0, :, 0:1], ctxT[:, :, MIX * P:MIX * P + 1])
                nc.gpsimd.tensor_copy(mix[:, 1, :, 1:P], ctxT[:, :, MIX * P + 1:(MIX + 1) * P]).then_inc(mix_ready, 1)
                pool.wait_ge(m_written, at(b, N_GROUPS, 0))
                pool.wait_ge(mturn_done, at(b, N_GROUPS, 0))
                pool.sem_inc(pool_seen, 1)
                nc.gpsimd.memset(q_stack[:, :, :, ROW_MAX:ROW_MAX + 6], 0.0).then_inc(q_zeroed, 1)
                pool.wait_ge(mask_ready, at(b, 1, 1))
                for step in range(STEPS):
                    t = step - LAG_RSTD
                    if 0 <= t < K_TILES:
                        n = SIZE[t]
                        pool.wait_ge(ms_ready, at(b, K_TILES, t + 1))
                        nc.gpsimd.tensor_tensor(rstd_k[0:n, t:t + 1], ms[0:n, t:t + 1], half_power[0:n, 0:1], ALU.pow)\
                          .then_inc(rstd_ready, 1)
                    if step == 3:
                        pool.wait_ge(ms_q_ready, at(b, 1, 1))
                        nc.gpsimd.tensor_tensor(rstd_q[:, :], ms_q[:, :], half_power[:, 0:QT], ALU.pow).then_inc(rstd_q_ready, 1)
                    t = step - LAG_PARTS
                    if 0 <= t < K_TILES:
                        if t >= 2:
                            pool.wait_ge(kturn_done, at(b, 2 * K_TILES, 2 * t - 2))
                        pool.sem_inc(pool_seen, 1)
                        nc.gpsimd.tensor_copy(k_stack[:, t % 2, :, ROW_MAX:ROW_MAX + N_EXTRA],
                                              extra[:, t, :].unsqueeze(1).broadcast_to([P, XH, N_EXTRA])).then_inc(extra_done, 1)
                pool.wait_ge(vb_ready, at(b, K_TILES, K_TILES))
                pool.sem_inc(pool_seen, 1)
                nc.gpsimd.tensor_scalar(v1[:, K_TILES, :, :], v1[:, MIX, :, :], kinds[:, MIX, 3:4], None, ALU.mult)\
                    .then_inc(vmix_ready, 1)
                pool.wait_ge(x1c_ready, at(b, 1, 1))
                pool.wait_ge(x1T_done, at(b, 1, 1))
                nc.gpsimd.tensor_tensor(x_bias[:, :, :], x1c[:, :, :], b_o[:, :].unsqueeze(1).broadcast_to([P, QT, D]), ALU.add)\
                  .then_inc(xb_ready, 1)
                pool.wait_ge(var_ready, at(b, 1, 1))
                nc.gpsimd.tensor_tensor(rstd[:, :], var_eps[:, :], half_power[:, 0:QT], ALU.pow).then_inc(ln_rstd, 1)
                pool.wait_ge(x2_ready, at(b, QT, QT))
                pool.sem_inc(pool_seen, 1)
                nc.gpsimd.tensor_copy(keep.x[:, bass.ds(b * QT, QT), :], x2[:, :, :]).then_inc(x2_kept, 1)

        @block.scalar
        def _(act):
            for s in (ssq_done, hi_done, kcopy_act, x1T_copied, ssq_q_done, qT0_copied, exp_done, o_copied,
                      attnT_copied, hT_copied):
                act.sem_inc(s, 1)
            with act.Fori(0, B) as b:
                def square(t):
                    n = SIZE[t]
                    act.wait_ge(kb_ready, at(b, K_TILES, t + 1))
                    act.wait_ge(ssq_done, at(b, K_TILES, max(t - 1, 0)))
                    nc.scalar.activation(junk[0:n, t % 2, :], yk[0:n, t % 5, :], ACT.Square, accum_out=ssq[0:n, t:t + 1])\
                      .then_inc(ssq_done, 1)

                def high_part(t):
                    n = SIZE[t]
                    act.wait_ge(kn_ready, at(b, K_TILES, t + 1))
                    if t >= 2:
                        act.wait_ge(kturn_done, at(b, 2 * K_TILES, 2 * t - 2))
                    nc.scalar.activation(
                        k_stack[0:n, t % 2, :, 0:3 * XD].rearrange("p h (s d) -> p h s d", s=3),
                        kn[0:n, t % 2, :].rearrange("p (h d) -> p h d", h=XH).unsqueeze(2).broadcast_to([n, XH, 3, XD]),
                        ACT.Copy).then_inc(hi_done, 1)

                def copy_keys(t):
                    n = SIZE[t]
                    act.wait_ge(kturn_done, at(b, 2 * K_TILES, 2 * t + 1))
                    nc.scalar.activation(kT[:, 0:8, t * P:t * P + n],
                                         wide_bf[(2 * t) % 4].rearrange("p (h k) -> p h k", h=8)[:, :, 0:n], ACT.Copy)\
                      .then_inc(kcopy_act, 1)

                def copy_x1T():
                    act.wait_ge(x1T_done, at(b, 1, 1))
                    act.wait_ge(qp_done, at(b, 1, 0))
                    nc.scalar.activation(x1T[:, :, :].rearrange("p k t -> p (k t)"), turn[:, :], ACT.Copy).then_inc(x1T_copied, 1)

                def square_q():
                    act.wait_ge(yq_ready, at(b, 1, 1))
                    act.wait_ge(ssq_q_done, at(b, QT, 0))
                    for q in range(QT):
                        nc.scalar.activation(junk_q[:, q, :], yq[:, q, :], ACT.Square, accum_out=ssq_q[:, q:q + 1])\
                          .then_inc(ssq_q_done, 1)

                def copy_qT0(f):
                    act.wait_ge(qturn_done, at(b, 4, f + 1))
                    nc.scalar.activation(qT0[:, 8 * (f % 2):8 * (f % 2) + 8, (f // 2) * P:(f // 2 + 1) * P],
                                         turn_bf.rearrange("p (h t) -> p h t", h=8), ACT.Copy).then_inc(qT0_copied, 1)

                side = {0: [copy_x1T], 2: [square_q]}
                for i in range(4):
                    side[6 + 2 * i] = [lambda i=i: copy_qT0(i)]
                for step in range(STEPS + 1):
                    if step < K_TILES:
                        square(step)
                    for f in side.get(step, ()):
                        f()
                    if 0 <= step - LAG_KN < K_TILES:
                        high_part(step - LAG_KN)
                    if 0 <= step - LAG_TURN - 1 < K_TILES:
                        copy_keys(step - LAG_TURN - 1)

                for g in range(N_GROUPS):
                    for t in range(K_TILES):
                        n = SIZE[t]
                        for pair in range(2):
                            m = (g * K_TILES + t) * 2 + pair
                            act.wait_ge(s_done, at(b, N_S, m + 1))
                            if pair == 0:
                                act.wait_ge(pv_done, at(b, N_PV, max(g * K_TILES + t - 2, 0)))
                            nc.scalar.activation(probs[0:n, m % 6, :, :].rearrange("p e t -> p (e t)"), score[pair][0:n, :],
                                                 ACT.Exp).then_inc(exp_done, 1)
                    act.wait_ge(pv_done, at(b, N_PV, (g + 1) * K_TILES))
                    act.wait_ge(oturn_done, at(b, N_GROUPS, g))
                    nc.scalar.activation(o_sb[:, :, :], outs[:, :, :], ACT.Copy).then_inc(o_copied, 1)

                act.wait_ge(aturn_done, at(b, 1, 1))
                nc.scalar.activation(attnT[:, :, :].rearrange("p k t -> p (k t)"), turn[:, :], ACT.Copy).then_inc(attnT_copied, 1)
                act.wait_ge(hturn_done, at(b, 1, 1))
                nc.scalar.activation(keep.hT[:, :, bass.ds(b * T, T)], turn[:, :].rearrange("p (k t) -> p k t", k=KT), ACT.Copy)\
                  .then_inc(hT_copied, 1)


def mixture_of_experts(nc, dram, keep, scratch, out):
    HALF = 512
    C = N_TOK // HALF
    SLOTS = 2 * N_PAIRS
    LOGITS = E + 1
    GU = KT * 2 * P
    LOOPS = (N_PAIRS - 1) // 2

    with ExitStack() as ctx:
        def sb(name, shape, dt=F32):
            return ctx.enter_context(nc.sbuf_tensor(name, shape, dt))

        def psum(name, shape, dt=F32):
            return ctx.enter_context(nc.psum_tensor(name, shape, dt))

        def sem(name):
            return ctx.enter_context(nc.semaphore(name))

        w_router = sb("w_router", [P, KT, LOGITS])
        weights = sb("weights", [P, 2, GU + D])
        mix_w = sb("mix_w", [P, 2, N_TOK])
        logit = sb("logit", [P, N_TILES, E])
        top_m = sb("top_m", [P, N_TILES])
        ex = sb("ex", [P, N_TILES, E])
        esum = sb("esum", [P, N_TILES])
        erec = sb("erec", [P, N_TILES])
        prob = sb("prob", [P, N_TILES, E])
        top = sb("top", [P, N_TILES, TOP_K])
        rest = sb("rest", [P, N_TILES, E])
        tsum = sb("tsum", [P, N_TILES])
        trec = sb("trec", [P, N_TILES])
        chosen = sb("chosen", [P, N_TILES, E])
        sgate = sb("sgate", [P, N_TILES])
        comb = sb("comb", [P, N_TILES, SLOTS])
        combT = sb("combT", [SLOTS, N_TOK])
        half_power = sb("half_power3", [P, N_TILES])
        th = sb("th", [P, C, HALF])
        gated = sb("gated", [P, C, HALF])
        prod = sb("prod", [P, C, HALF])
        act_w = sb("act_w", [P, C, HALF])
        zT = sb("zT", [P, KT, N_TOK])
        stats = sb("stats3", [P, N_TILES, 6])
        mean_var = sb("mean_var3", [P, N_TILES, 2])
        var_eps = sb("var_eps3", [P, N_TILES])
        rstd = sb("rstd3", [P, N_TILES])
        x3 = sb("x3", [P, N_TILES, D])

        gate_up = psum("gate_up", [P, C, 2, HALF])
        y = psum("y_sum", [P, C, KT, HALF])

        router_in, scratch_in, out_done = sem("router_in"), sem("scratch_in"), sem("out_done3")
        w_in = [sem(f"w_in3_{i}") for i in range(2)]
        c_in = [sem(f"c_in{i}") for i in range(2)]
        logits_done, top_ready, logit_ready, ex_done, sgate_done = [sem(n) for n in (
            "logits_done", "top_ready", "logit_ready", "ex_done", "sgate_done")]
        esum_ready, erec_ready, prob_ready, top8_ready, rest_ready = [sem(n) for n in (
            "esum_ready", "erec_ready", "prob_ready", "top8_ready", "rest_ready3")]
        tsum_ready, trec_ready, chosen_ready, comb_ready, pad_set = [sem(n) for n in (
            "tsum_ready", "trec_ready", "chosen_ready", "comb_ready", "pad_set")]
        comb_turned, comb_copied = sem("comb_turned"), sem("comb_copied")
        gu_done, th_done, gated_ready, prod_ready, act_ready, down_done = [sem(n) for n in (
            "gu_done", "th_done", "gated_ready", "prod_ready", "act_ready", "down_done")]
        zT_ready, z_turned, stats_ready, mv_ready, var_ready, rstd_ready, x3_ready = [sem(n) for n in (
            "zT_ready", "z_turned", "stats_ready3", "mv_ready3", "var_ready3", "rstd_ready3", "x3_ready")]

        banks = gate_up[:, :, :, :].rearrange("p c s t -> p (c s) t")

        block = ctx.enter_context(nc.Block())

        @block.sync
        def _(sp):
            def load_weights(p, slot):
                sp.dma_start(weights[:, slot, :], dram["pairs"][p].rearrange("a p n -> p (a n)")).then_inc(w_in[slot], 16)

            def load_mix(p, slot):
                sp.dma_start(mix_w[:, slot, :], scratch[p].rearrange("a e t -> (a e) t").unsqueeze(1)
                             .broadcast_to([2, EI, N_TOK])).then_inc(c_in[slot], 16)

            sp.dma_start(w_router[:, :, :], dram["router_wT"].rearrange("(k p) n -> p k n", p=P)).then_inc(router_in, 16)
            load_weights(slice(0, 1), 0)
            load_weights(slice(1, 2), 1)
            sp.wait_ge(comb_copied, C)
            sp.dma_start(scratch[:, :, :].rearrange("a e t -> (a e) t"), combT[:, :]).then_inc(scratch_in, 16)
            sp.wait_ge(scratch_in, 16)
            load_mix(slice(0, 1), 0)
            load_mix(slice(1, 2), 1)
            sp.wait_ge(down_done, 2)
            load_weights(slice(2, 3), 0)
            load_mix(slice(2, 3), 0)
            with sp.Fori(0, LOOPS - 1) as it:
                for u in range(2):
                    p = it * 2 + (3 + u)
                    sp.wait_ge(down_done, it * 4 + (2 + u) * 2)
                    load_weights(bass.ds(p, 1), 1 - u)
                    load_mix(bass.ds(p, 1), 1 - u)
            sp.wait_ge(down_done, 2 * N_PAIRS - 2)
            sp.wait_ge(down_done, 2 * N_PAIRS - 2)
            for t in range(N_TILES):
                sp.wait_ge(x3_ready, t + 1)
                sp.dma_start(out.rearrange("b (q p) d -> p (b q) d", p=P)[:, t, :], x3[:, t, :]).then_inc(out_done, 16)
            sp.wait_ge(out_done, 16 * N_TILES)

        @block.tensor
        def _(pe):
            pe.wait_ge(router_in, 16)
            for t in range(N_TILES):
                for k in range(KT):
                    mm = nc.tensor.matmul(banks[:, t // 4, (t % 4) * P:(t % 4) * P + LOGITS],
                                          keep.hT[:, k, t * P:(t + 1) * P], w_router[:, k, :], start=(k == 0), stop=(k == KT - 1))
            mm.then_inc(logits_done, 1)
            pe.wait_ge(comb_ready, 1)
            pe.wait_ge(pad_set, 2)
            pe.wait_ge(sgate_done, 2)
            for t in range(N_TILES):
                mm = nc.tensor.transpose(banks[0:SLOTS, 2 + t // 4, (t % 4) * P:(t % 4 + 1) * P], comb[:, t, :], keep.ident[:, :])
            mm.then_inc(comb_turned, 1)
            pe.wait_ge(comb_copied, C)

            def gate_and_up(n, c, slot, loads, first=False):
                if c == 0:
                    pe.wait_ge(w_in[slot], loads)
                if not first:
                    pe.wait_ge(prod_ready, n - 1)
                for s in range(2):
                    for k in range(KT):
                        lo = (k * 2 + s) * P
                        mm = nc.tensor.matmul(gate_up[:, c, s, :], weights[:, slot, lo:lo + P],
                                              keep.hT[:, k, c * HALF:(c + 1) * HALF], start=(k == 0), stop=(k == KT - 1))
                mm.then_inc(gu_done, 1)

            def down(n, c, slot, first=False, last=False):
                pe.wait_ge(act_ready, n + 1)
                for d in range(KT):
                    mm = nc.tensor.matmul(y[:, c, d, :], weights[:, slot, GU + d * P:GU + (d + 1) * P], act_w[:, c, :],
                                          start=first, stop=last)
                mm.then_inc(down_done, 1)

            gate_and_up(0, 0, 0, 16, first=True)
            gate_and_up(1, 1, 0, 16, first=True)
            down(0, 0, 0, first=True)
            gate_and_up(2, 0, 1, 16)
            down(1, 1, 0, first=True)
            gate_and_up(3, 1, 1, 16)
            down(2, 0, 1)
            with pe.Fori(0, LOOPS - 1) as it:
                for u in range(2):
                    n = it * 4 + (4 + 2 * u)
                    gate_and_up(n, 0, u, it * 16 + 32)
                    down(n - 1, 1, 1 - u)
                    gate_and_up(n + 1, 1, u, it * 16 + 32)
                    down(n, 0, u)
            n = 2 * N_PAIRS - 2
            gate_and_up(n, 0, 0, LOOPS * 16 + 16)
            down(n - 1, 1, 1)
            gate_and_up(n + 1, 1, 0, LOOPS * 16 + 16)
            down(n, 0, 0, last=True)
            down(n + 1, 1, 0, last=True)

            for t in range(N_TILES):
                if t % 4 == 0:
                    pe.wait_ge(zT_ready, t // 4 + 1)
                for k in range(KT):
                    mm = nc.tensor.transpose(banks[:, t // 2, (t % 2) * D + k * P:(t % 2) * D + (k + 1) * P],
                                             zT[:, k, t * P:(t + 1) * P], keep.ident[:, :])
                mm.then_inc(z_turned, 1)

        @block.vector
        def _(dve):
            raw = banks[:, 0:2, :].rearrange("p a (t n) -> p (a t) n", n=P)
            dve.wait_ge(logits_done, 1)
            nc.vector.tensor_reduce(top_m[:, :], raw[:, :, 0:E], AX_X, ALU.max).then_inc(top_ready, 1)
            dve.wait_ge(top_ready, 1)

            def by_tile(v):
                return v.unsqueeze(2).broadcast_to([P, N_TILES, E])

            nc.vector.tensor_tensor(logit[:, :, :], raw[:, :, 0:E], by_tile(top_m[:, :]), ALU.subtract).then_inc(logit_ready, 1)
            dve.wait_ge(ex_done, 1)
            nc.vector.tensor_reduce(esum[:, :], ex[:, :, :], AX_X, ALU.add).then_inc(esum_ready, 1)
            dve.wait_ge(esum_ready, 1)
            nc.vector.reciprocal(erec[:, :], esum[:, :]).then_inc(erec_ready, 1)
            dve.wait_ge(erec_ready, 1)
            nc.vector.tensor_tensor(prob[:, :, :], ex[:, :, :], by_tile(erec[:, :]), ALU.mult).then_inc(prob_ready, 1)
            dve.wait_ge(prob_ready, 1)
            for t in range(N_TILES):
                nc.vector.max(out=top[:, t, :], in_=prob[:, t, :]).then_inc(top8_ready, 1)
            for t in range(N_TILES):
                dve.wait_ge(top8_ready, t + 1)
                nc.vector.match_replace(out=rest[:, t, :], in_to_replace=top[:, t, :], in_values=prob[:, t, :],
                                        imm_value=-1.0).then_inc(rest_ready, 1)
            nc.vector.tensor_reduce(tsum[:, :], top[:, :, :], AX_X, ALU.add).then_inc(tsum_ready, 1)
            dve.wait_ge(tsum_ready, 1)
            nc.vector.reciprocal(trec[:, :], tsum[:, :]).then_inc(trec_ready, 1)
            dve.wait_ge(rest_ready, N_TILES)
            nc.vector.scalar_tensor_tensor(out=chosen[:, :, :], in0=rest[:, :, :], scalar=0.0, in1=prob[:, :, :],
                                           op0=ALU.is_lt, op1=ALU.mult).then_inc(chosen_ready, 1)
            dve.wait_ge(chosen_ready, 1)
            dve.wait_ge(trec_ready, 1)
            nc.vector.scalar_tensor_tensor(out=comb[:, :, 0:E], in0=chosen[:, :, :], scalar=0.5, in1=by_tile(trec[:, :]),
                                           op0=ALU.mult, op1=ALU.mult).then_inc(comb_ready, 1)
            for c in range(C):
                dve.wait_ge(comb_turned, 1)
                nc.vector.tensor_copy(combT[:, c * HALF:(c + 1) * HALF], banks[0:SLOTS, 2 + c, :]).then_inc(comb_copied, 1)

            def unit(n, c, first=False):
                dve.wait_ge(th_done, n + 1)
                if not first:
                    dve.wait_ge(act_ready, n - 1)
                nc.vector.scalar_tensor_tensor(out=gated[:, c, :], in0=th[:, c, :], scalar=1.0, in1=gate_up[:, c, 0, :],
                                               op0=ALU.add, op1=ALU.mult).then_inc(gated_ready, 1)
                dve.wait_ge(gated_ready, n + 1)
                nc.vector.tensor_tensor(prod[:, c, :], gated[:, c, :], gate_up[:, c, 1, :], ALU.mult).then_inc(prod_ready, 1)

            unit(0, 0, first=True)
            unit(1, 1, first=True)
            with dve.Fori(0, LOOPS) as it:
                for u in range(4):
                    unit(it * 4 + (2 + u), u % 2)

            for c in range(C):
                dve.wait_ge(down_done, 2 * N_PAIRS - 1 + c)
                nc.vector.tensor_tensor(zT[:, :, c * HALF:(c + 1) * HALF], y[:, c, :, :], keep.hT[:, :, c * HALF:(c + 1) * HALF],
                                        ALU.add).then_inc(zT_ready, 1)
            for t in range(N_TILES):
                z = banks[:, t // 2, (t % 2) * D:(t % 2 + 1) * D]
                dve.wait_ge(z_turned, 2 * (t // 2) + 2)
                nc.vector.bn_stats(stats[:, t, :], z).then_inc(stats_ready, 1)
            for t in range(N_TILES):
                dve.wait_ge(stats_ready, t + 1)
                nc.vector.bn_aggr(mean_var[:, t, :], stats[:, t, :]).then_inc(mv_ready, 1)
            dve.wait_ge(mv_ready, N_TILES)
            nc.vector.tensor_scalar(var_eps[:, :], mean_var[:, :, 1], LN_EPS, None, ALU.add).then_inc(var_ready, 1)
            dve.wait_ge(rstd_ready, 1)
            for t in range(N_TILES):
                z = banks[:, t // 2, (t % 2) * D:(t % 2 + 1) * D]
                nc.vector.tensor_scalar(x3[:, t, :], z, mean_var[:, t, 0:1], rstd[:, t:t + 1],
                                        ALU.subtract, ALU.mult).then_inc(x3_ready, 1)

        @block.gpsimd
        def _(pool):
            nc.gpsimd.memset(half_power[:, :], -0.5).then_inc(pad_set, 1)
            nc.gpsimd.memset(comb[:, :, E + 1:SLOTS], 0.0).then_inc(pad_set, 1)

            def unit(n, c, slot, loads, first=False):
                pool.wait_ge(prod_ready, n + 1)
                if c == 0:
                    pool.wait_ge(c_in[slot], loads)
                if not first:
                    pool.wait_ge(down_done, n - 1)
                nc.gpsimd.tensor_tensor(act_w[:, c, :], prod[:, c, :], mix_w[:, slot, c * HALF:(c + 1) * HALF], ALU.mult)\
                  .then_inc(act_ready, 1)

            unit(0, 0, 0, 16, first=True)
            unit(1, 1, 0, 16, first=True)
            with pool.Fori(0, LOOPS) as it:
                for c in range(C):
                    unit(it * 4 + (2 + c), c, 1, it * 16 + 16)
                for c in range(C):
                    unit(it * 4 + (4 + c), c, 0, it * 16 + 32)
            pool.wait_ge(var_ready, 1)
            pool.wait_ge(pad_set, 2)
            nc.gpsimd.tensor_tensor(rstd[:, :], var_eps[:, :], half_power[:, :], ALU.pow).then_inc(rstd_ready, 1)

        @block.scalar
        def _(act):
            act.wait_ge(logits_done, 1)
            act.wait_ge(logit_ready, 1)
            nc.scalar.activation(ex[:, :, :], logit[:, :, :], ACT.Exp).then_inc(ex_done, 1)
            nc.scalar.activation(sgate[:, :], banks[:, 0:2, :].rearrange("p a (t n) -> p (a t) n", n=P)[:, :, E], ACT.Tanh,
                                 scale=0.5).then_inc(sgate_done, 1)
            act.wait_ge(sgate_done, 1)
            nc.scalar.activation(comb[:, :, E], sgate[:, :], ACT.Copy, scale=0.25, bias=0.25).then_inc(sgate_done, 1)

            def unit(n, c, first=False):
                act.wait_ge(gu_done, n + 1)
                if not first:
                    act.wait_ge(prod_ready, n - 1)
                nc.scalar.activation(th[:, c, :], gate_up[:, c, 0, :], ACT.Tanh, scale=0.5).then_inc(th_done, 1)

            unit(0, 0, first=True)
            unit(1, 1, first=True)
            with act.Fori(0, LOOPS) as it:
                for u in range(4):
                    unit(it * 4 + (2 + u), u % 2)


def host_layout(inputs):
    a = {k: np.asarray(v) for k, v in inputs.items()}

    def t(name):
        return np.ascontiguousarray(a[name].T)

    out_wT = a["L0_attn_out_w"].T.reshape(N_KV // 2, 2, Q_MULT, DH, D).transpose(1, 3, 0, 2, 4).reshape(P, -1)
    eye = np.eye(P, dtype=np.float32)
    cos, sin = rope_tables()
    tiles = -(-L_ALL // P)
    key_index = (np.arange(tiles)[None, :] * P + np.arange(P)[:, None] - L_IMG).astype(np.float32)
    kinds = np.stack([key_index < 0] * 3 + [key_index >= 0] * 3, -1).astype(np.float32).reshape(P, -1)
    arrays = {
        "x": a["x"], "xT": a["x"].transpose(0, 2, 1),
        "qkv_wT": t("L0_attn_qkv_w"), "qkv_b": a["L0_attn_qkv_b"], "sinks": a["L0_attn_sinks"],
        "out_wT": out_wT, "out_b": a["L0_attn_out_b"],
        "cos": cos, "sin": sin, "masks": window_masks(), "ident": eye,
        "ctxT": a["ctx_2048"].transpose(0, 2, 1), "lens": a["_lenS2"].reshape(1, B),
        "key_index": key_index, "kinds": kinds,
    }
    for name in ("w_q", "w_k", "w_v", "w_k_img", "w_v_img", "w_o"):
        arrays[name] = t("L0_xattn_" + name)
    for name in ("b_q", "b_k", "b_v", "b_k_img", "b_v_img", "b_o", "g_q", "g_k", "g_k_img"):
        arrays[name] = a["L0_xattn_" + name]
    def in_pairs(routed, shared):
        both = np.concatenate([routed, shared[None], np.zeros_like(shared)[None]])
        return both.reshape((N_PAIRS, 2) + shared.shape)

    gate_up = a["L0_ffn_gate_up_proj"]
    gate = in_pairs(gate_up[:, :EI], a["L0_ffn_shared_gate_w"])
    up = in_pairs(gate_up[:, EI:], a["L0_ffn_shared_up_w"])
    down = in_pairs(a["L0_ffn_down_proj"], a["L0_ffn_shared_down_w"])
    gu = np.stack([gate, up], 1).reshape(N_PAIRS, 2, 2, EI, KT, P).transpose(0, 5, 4, 1, 2, 3).reshape(N_PAIRS, P, -1)
    arrays["pairs"] = np.concatenate([gu, down.transpose(0, 1, 3, 2).reshape(N_PAIRS, P, D)], 2)
    arrays["router_wT"] = np.concatenate([t("L0_ffn_router_w"), t("L0_ffn_shared_expert_gate_w")], 1)
    return {k: np.ascontiguousarray(v) for k, v in arrays.items()}


class Keep:

    def __init__(self, ident, x, hT):
        self.ident = ident
        self.x = x
        self.hT = hT


def decoder_layer(nc, dram, out):
    scratch = nc.dram_tensor("mix_rows", (N_PAIRS, 2, N_TOK), F32, kind="Internal").ap()
    with ExitStack() as ctx:
        keep = Keep(ctx.enter_context(nc.sbuf_tensor("ident", [P, P], F32)),
                    ctx.enter_context(nc.sbuf_tensor("x_keep", [P, N_TILES, D], F32)),
                    ctx.enter_context(nc.sbuf_tensor("hT", [P, KT, N_TOK], F32)))
        self_attention(nc, dram, keep)
        cross_attention(nc, dram, keep)
        mixture_of_experts(nc, dram, keep, scratch, out)


def kernel(**inputs):
    import concourse.bacc as bacc
    from concourse.bass_utils import run_bass_kernel_spmd

    nc = bacc.Bacc("TRN2", target_bir_lowering=False, num_devices=1)
    arrays = host_layout(inputs)
    dram = {name: nc.dram_tensor("in_" + name, a.shape, mybir.dt.from_np(a.dtype), kind="ExternalInput").ap()
            for name, a in arrays.items()}
    out = nc.dram_tensor("out_x", (B, T, D), F32, kind="ExternalOutput").ap()
    decoder_layer(nc, dram, out)
    r = run_bass_kernel_spmd(nc, [{"in_" + name: a for name, a in arrays.items()}], core_ids=[0])
    return r.results[0]["out_x"]
```

```python
import math
from contextlib import ExitStack

import numpy as np

import concourse.bass as bass
from concourse import mybir

F32 = mybir.dt.float32
BF16 = mybir.dt.bfloat16
I32 = mybir.dt.int32
ACT = mybir.ActivationFunctionType
ALU = mybir.AluOpType
AX_X = mybir.AxisListType.X

P = 128
B, T, D = 4, 256, 256
QT = T // P
KT = D // P
N_TILES = B * QT
LN_EPS = 1e-5

DH, N_HEADS, N_KV, WINDOW = 64, 32, 8, 128
Q_MULT = N_HEADS // N_KV
QKV = DH * (N_HEADS + 2 * N_KV)
CHUNK = 512
Q_CHUNKS = N_HEADS * DH // CHUNK
QK_CHUNKS = Q_CHUNKS + 1
N_CHUNKS = QKV // CHUNK
SM_SCALE = 1.0 / math.sqrt(DH)
NEG = -1.0e30

XH, XD = 16, 16
L_IMG, L_ALL = 257, 1601
L_TXT = L_ALL - L_IMG
RMS_EPS = 1e-6

E, EI, TOP_K = 64, 64, 8
N_PAIRS = E // 2 + 1
N_TOK = B * T


def rope_tables():
    theta, scaling, alpha, beta, icl = 150000.0, 32.0, 1.0, 32.0, 128
    half = DH // 2
    freq = theta ** (np.arange(0, DH, 2, dtype=np.float32) / DH)
    low = half * math.log(icl / (beta * 2 * math.pi)) / math.log(theta)
    high = half * math.log(icl / (alpha * 2 * math.pi)) / math.log(theta)
    ramp = np.clip((np.arange(half, dtype=np.float32) - low) / (high - low), 0.0, 1.0)
    keep = 1.0 - ramp
    inv = (1.0 / (scaling * freq)) * (1.0 - keep) + (1.0 / freq) * keep
    ang = np.outer(np.arange(T, dtype=np.float32), inv)
    conc = 0.1 * math.log(scaling) + 1.0
    cos = (np.cos(ang) * conc).astype(np.float32)
    sin = (np.sin(ang) * conc).astype(np.float32)
    return np.concatenate([cos, cos], 1), np.concatenate([-sin, sin], 1)


def window_masks():
    i = np.arange(P)[:, None]
    j = np.arange(P)[None, :]
    diag = np.where(j > i, NEG, 0.0)
    behind = np.where(j <= i, NEG, 0.0)
    return np.concatenate([diag, behind, diag], 1).astype(np.float32)


def broadcast_rows(ap, rows=P):
    return ap.partition_broadcast(rows)


def self_attention(nc, dram, keep):
    G_UNITS = 3
    N_GROUPS = N_KV
    N_UNITS = G_UNITS * N_GROUPS
    N_QK = QT * QK_CHUNKS
    N_PROJ = QT * N_CHUNKS
    T_FILLS = QT * (Q_CHUNKS + 2)
    TR_FILLS = T_FILLS + N_UNITS
    N_PAIR = N_GROUPS // 2
    KEYS = P + 2 * P

    with ExitStack() as ctx:
        def sb(name, shape, dt=F32):
            return ctx.enter_context(nc.sbuf_tensor(name, shape, dt))

        def psum(name, shape, dt=F32):
            return ctx.enter_context(nc.psum_tensor(name, shape, dt))

        def sem(name):
            return ctx.enter_context(nc.semaphore(name))

        w_qkv = sb("w_qkv", [P, KT, QKV])
        b_qkv = sb("b_qkv", [P, QKV])
        w_out = sb("w_out", [P, N_PAIR, Q_MULT, D])
        b_out = sb("b_out", [P, D])
        sinks = sb("sinks", [P, N_HEADS])
        cos = sb("cos", [P, QT, DH])
        sin = sb("sin", [P, QT, DH])
        masks = sb("masks", [P, KEYS])
        masks_bf = sb("masks_bf", [P, KEYS], BF16)
        ident_bf = sb("ident_bf1", [P, P], BF16)
        half_power = sb("half_power1", [P, 1])

        xT = sb("xT", [P, KT, T])
        x_res = sb("x_res", [P, QT, D])
        x_bias = sb("x_bias", [P, QT, D])
        y = sb("y", [P, 3, CHUNK])
        y_cos = sb("y_cos", [P, 2, CHUNK])
        y_sin = sb("y_sin", [P, 3, CHUNK])
        roped = sb("roped", [P, 3, CHUNK])
        k_twice = sb("k_twice", [P, QT, N_KV, 2, DH])
        v = sb("v", [P, QT, N_KV, DH])
        qT = sb("qT", [P, N_HEADS // 2, T])
        kT = sb("kT", [P, N_KV, 2, T])
        negm = sb("negm", [P, 3, QT, Q_MULT])
        mx = sb("mx", [P, 3, QT, Q_MULT])
        sink_arg = sb("sink_arg", [P, 3, QT, Q_MULT])
        sink_exp = sb("sink_exp", [P, 3, QT, Q_MULT])
        sums = sb("sums", [P, 3, QT, Q_MULT])
        den = sb("den", [P, 3, QT, Q_MULT])
        rden = sb("rden", [P, 3, QT, Q_MULT])
        probs = sb("probs", [P, 3, Q_MULT, KEYS])
        probsT = sb("probsT", [P, 2, G_UNITS, CHUNK])
        oT = sb("oT", [P, N_PAIR, Q_MULT, T])
        z = sb("z", [P, QT, D])
        stats = sb("stats1", [P, QT, 6])
        mean_var = sb("mean_var1", [P, QT, 2])
        var_eps = sb("var_eps1", [P, QT, 1])
        rstd = sb("rstd1", [P, QT, 1])

        proj = [psum(f"proj{i}", [P, CHUNK]) for i in range(2)]
        turn = [psum(f"turn{i}", [P, CHUNK]) for i in range(2)]
        score = [psum(f"score{i}", [P, CHUNK]) for i in range(G_UNITS)]

        consts_in = sem("consts_in")
        consts_cast = sem("consts_cast")
        half_power_set = sem("half_power_set")
        kT_zeroed = sem("kT_zeroed")
        xT_in = sem("xT_in")
        x_in = sem("x_in")
        xb_ready = sem("xb_ready")
        proj_done = sem("proj_done")
        y_ready = sem("y_ready")
        cos_done = sem("cos_done")
        sin_done = sem("sin_done")
        roped_ready = sem("roped_ready")
        turn_done = sem("turn_done")
        turn_copied = sem("turn_copied")
        score_done = sem("score_done")
        mx_ready = sem("mx_ready")
        negm_ready = sem("negm_ready")
        exp_done = sem("exp_done")
        sink_arg_ready = sem("sink_arg_ready")
        sink_exp_done = sem("sink_exp_done")
        den_ready = sem("den_ready")
        rden_ready = sem("rden_ready")
        normed = sem("normed")
        pv_done = sem("pv_done")
        oT_copied = sem("oT_copied")
        out_done = sem("out_done")
        z_ready = sem("z_ready")
        stats_ready = sem("stats_ready")
        mv_ready = sem("mv_ready")
        var_ready = sem("var_ready")
        rstd_ready = sem("rstd_ready")
        x1_ready = sem("x1_ready")

        dve_seen = sem("dve_seen")

        def at(b, per_batch, count):
            return b * per_batch + (1 + count)

        block = ctx.enter_context(nc.Block())

        @block.sync
        def _(sp):
            sp.dma_start(w_qkv[:, :, :], dram["qkv_wT"].rearrange("(k p) n -> p k n", p=P)).then_inc(consts_in, 16)
            sp.dma_start(cos[:, :, :], dram["cos"].rearrange("(q p) n -> p q n", p=P)).then_inc(consts_in, 16)
            sp.dma_start(sin[:, :, :], dram["sin"].rearrange("(q p) n -> p q n", p=P)).then_inc(consts_in, 16)
            sp.dma_start(masks[:, :], dram["masks"]).then_inc(consts_in, 16)
            sp.dma_start(keep.ident[:, :], dram["ident"]).then_inc(consts_in, 16)
            sp.dma_start(b_qkv[:, :], broadcast_rows(dram["qkv_b"])).then_inc(consts_in, 16)
            sp.dma_start(sinks[:, :], broadcast_rows(dram["sinks"])).then_inc(consts_in, 16)
            sp.dma_start(b_out[:, :], broadcast_rows(dram["out_b"])).then_inc(consts_in, 16)
            sp.dma_start(w_out[:, :, :, :].rearrange("p g m n -> p (g m n)"), dram["out_wT"]).then_inc(consts_in, 16)
            with sp.Fori(0, B) as b:
                sp.wait_ge(proj_done, at(b, N_PROJ, 0))
                sp.dma_start(xT[:, :, :], dram["xT"][bass.ds(b, 1)].rearrange("a (k p) t -> p (a k) t", p=P))\
                  .then_inc(xT_in, 16)
                sp.wait_ge(xb_ready, at(b, 1, 0))
                sp.dma_start(x_res[:, :, :], dram["x"][bass.ds(b, 1)].rearrange("a (q p) d -> p (a q) d", p=P))\
                  .then_inc(x_in, 16)

        N_CONSTS = 9

        @block.tensor
        def _(pe):
            pe.wait_ge(consts_in, 16 * N_CONSTS)
            pe.wait_ge(consts_cast, 2)
            pe.wait_ge(kT_zeroed, 2)
            for s in (proj_done, turn_done, score_done, pv_done, out_done):
                pe.sem_inc(s, 1)
            with pe.Fori(0, B) as b:
                def claim_turn(f):
                    pe.wait_ge(turn_copied, at(b, TR_FILLS, max(f - 1, 0)))

                def turn_qk(i):
                    q, c = i // QK_CHUNKS, i % QK_CHUNKS
                    pe.wait_ge(roped_ready, at(b, N_QK, i + 1))
                    for part in range(1 if c < Q_CHUNKS else 2):
                        f = q * (Q_CHUNKS + 2) + c + part
                        claim_turn(f)
                        for n in range(4):
                            if c < Q_CHUNKS:
                                piece = roped[:, i % 3, n * P:(n + 1) * P]
                            else:
                                piece = k_twice[:, q, part * 4 + n, :, :].rearrange("p s d -> p (s d)")
                            mm = nc.tensor.transpose(turn[f % 2][:, n * P:(n + 1) * P], piece, keep.ident[:, :])
                        mm.then_inc(turn_done, 1)

                pe.wait_ge(xT_in, b * 16 + 16)
                for q in range(QT):
                    for c in range(N_CHUNKS):
                        j = q * N_CHUNKS + c
                        if j >= 2:
                            pe.wait_ge(y_ready, at(b, N_PROJ, j - 1))
                        else:
                            pe.wait_ge(z_ready, at(b, QT, 0))
                        for k in range(KT):
                            mm = nc.tensor.matmul(proj[j % 2][:, :], xT[:, k, q * P:(q + 1) * P],
                                                  w_qkv[:, k, c * CHUNK:(c + 1) * CHUNK],
                                                  start=(k == 0), stop=(k == KT - 1))
                        mm.then_inc(proj_done, 1)
                        i = q * QK_CHUNKS + c
                        if c < QK_CHUNKS and i >= 2:
                            turn_qk(i - 2)
                turn_qk(N_QK - 2)
                turn_qk(N_QK - 1)
                pe.wait_ge(turn_copied, at(b, TR_FILLS, T_FILLS))

                def scores(g):
                    for u in range(G_UNITS):
                        n = g * G_UNITS + u
                        pe.wait_ge(exp_done, at(b, N_UNITS, max(n - 2, 0)))
                        heads = range(4) if u == 0 else range(2 * u - 2, 2 * u)
                        q, w = (0, P) if u == 0 else (1, 2 * P)
                        m = masks_bf[:, 0:P] if u == 0 else masks_bf[:, P:KEYS]
                        nc.tensor.matmul(score[u][:, :], ident_bf[:, :],
                                         m.unsqueeze(1).broadcast_to([P, len(heads), w]), start=True, stop=False)
                        pairs = range(heads[0] // 2, (heads[-1] + 1) // 2)
                        for e, pair in enumerate(pairs):
                            mm = nc.tensor.matmul(score[u][:, e * 2 * w:(e + 1) * 2 * w],
                                                  qT[:, g * Q_MULT // 2 + pair, q * P:(q + 1) * P],
                                                  kT[:, g, :, 0:w], start=False, stop=(pair == pairs[-1]))
                        mm.then_inc(score_done, 1)

                def turn_probs(g):
                    pe.wait_ge(normed, at(b, N_GROUPS, g + 1))
                    for u in range(G_UNITS):
                        f = T_FILLS + g * G_UNITS + u
                        claim_turn(f)
                        for m in range(Q_MULT):
                            mm = nc.tensor.transpose(turn[f % 2][:, m * P:(m + 1) * P],
                                                     probs[:, g % 3, m, u * P:(u + 1) * P], keep.ident[:, :])
                        mm.then_inc(turn_done, 1)

                def weigh_values(pair):
                    pe.wait_ge(turn_copied, at(b, TR_FILLS, T_FILLS + (2 * pair + 2) * G_UNITS))
                    if pair:
                        pe.wait_ge(oT_copied, at(b, N_GROUPS, 2 * pair))
                    for u, (bank, tile, first) in enumerate(((0, 0, True), (1, 0, True), (1, 1, False))):
                        for s in range(2):
                            mm = nc.tensor.matmul(proj[bank][s * DH:(s + 1) * DH, :], v[:, tile, 2 * pair + s, :],
                                                  probsT[:, s, u, :], start=first, stop=(u != 1))
                    mm.then_inc(pv_done, 1)

                scores(0)
                scores(1)
                for g in range(N_GROUPS):
                    if g + 2 < N_GROUPS:
                        scores(g + 2)
                    if g % 2 == 0 and g:
                        weigh_values(g // 2 - 1)
                    turn_probs(g)
                weigh_values(N_PAIR - 1)

                pe.wait_ge(oT_copied, at(b, N_GROUPS, N_GROUPS))
                for q in range(QT):
                    for k in range(N_PAIR * Q_MULT):
                        mm = nc.tensor.matmul(proj[q][:, 0:D], oT[:, k // Q_MULT, k % Q_MULT, q * P:(q + 1) * P],
                                              w_out[:, k // Q_MULT, k % Q_MULT, :],
                                              start=(k == 0), stop=(k == N_PAIR * Q_MULT - 1))
                    mm.then_inc(out_done, 1)

        @block.vector
        def _(dve):
            dve.wait_ge(consts_in, 16 * N_CONSTS)
            nc.vector.memset(kT[0:DH, :, 1, :], 0.0).then_inc(kT_zeroed, 1)
            nc.vector.memset(kT[DH:P, :, 0, :], 0.0).then_inc(kT_zeroed, 1)
            nc.vector.tensor_copy(ident_bf[:, :], keep.ident[:, :]).then_inc(consts_cast, 1)
            nc.vector.tensor_copy(masks_bf[:, :], masks[:, :]).then_inc(consts_cast, 1)
            for s in (y_ready, cos_done, roped_ready, mx_ready, negm_ready, sink_arg_ready, den_ready,
                      rden_ready, z_ready, stats_ready, mv_ready, var_ready, x1_ready):
                dve.sem_inc(s, 1)
            with dve.Fori(0, B) as b:
                def add_sin(i):
                    dve.wait_ge(sin_done, at(b, N_QK, i + 1))
                    dve.wait_ge(cos_done, at(b, N_QK, i + 1))
                    c, before = i % QK_CHUNKS, i - 3
                    if before >= 0:
                        fills = (before // QK_CHUNKS) * (Q_CHUNKS + 2) + before % QK_CHUNKS + 1
                        fills += before % QK_CHUNKS == Q_CHUNKS
                        dve.wait_ge(turn_done, at(b, TR_FILLS, fills))
                    if c < Q_CHUNKS:
                        out, rope_cos, rope_sin = roped[:, i % 3, :], y_cos[:, i % 2, :], y_sin[:, i % 3, :]
                    else:
                        out = k_twice[:, i // QK_CHUNKS]
                        rope_cos, rope_sin = [
                            s.rearrange("p (h d) -> p h d", d=DH).unsqueeze(2).broadcast_to([P, N_KV, 2, DH])
                            for s in (y_cos[:, i % 2, :], y_sin[:, i % 3, :])]
                    nc.vector.tensor_tensor(out, rope_cos, rope_sin, ALU.add).then_inc(roped_ready, 1)

                i = 0
                for q in range(QT):
                    for c in range(N_CHUNKS):
                        j = q * N_CHUNKS + c
                        dve.wait_ge(proj_done, at(b, N_PROJ, j + 1))
                        if c < QK_CHUNKS:
                            if i >= 3:
                                dve.wait_ge(sin_done, at(b, N_QK, i - 2))
                            nc.vector.tensor_tensor(y[:, i % 3, :], proj[j % 2][:, :],
                                                    b_qkv[:, c * CHUNK:(c + 1) * CHUNK], ALU.add).then_inc(y_ready, 1)
                            if i:
                                add_sin(i - 1)
                            dve.wait_ge(y_ready, at(b, N_PROJ, j + 1))
                            nc.vector.tensor_tensor(
                                y_cos[:, i % 2, :].rearrange("p (h d) -> p h d", d=DH),
                                y[:, i % 3, :].rearrange("p (h d) -> p h d", d=DH),
                                cos[:, q, :].unsqueeze(1).broadcast_to([P, CHUNK // DH, DH]), ALU.mult)\
                              .then_inc(cos_done, 1)
                            i += 1
                        else:
                            nc.vector.tensor_tensor(v[:, q, :, :], proj[j % 2][:, :].rearrange("p (h d) -> p h d", d=DH),
                                                    b_qkv[:, c * CHUNK:].rearrange("p (h d) -> p h d", d=DH), ALU.add)\
                              .then_inc(y_ready, 1)
                add_sin(N_QK - 1)

                def maxima(g):
                    for u in range(G_UNITS):
                        n = g * G_UNITS + u
                        dve.wait_ge(score_done, at(b, N_UNITS, n + 1))
                        q, lo, hi = (0, 0, 4) if u == 0 else (1, 2 * u - 2, 2 * u)
                        nc.vector.tensor_reduce(mx[:, g % 3, q, lo:hi],
                                                score[u][:, :].rearrange("p (h k) -> p h k", h=hi - lo), AX_X, ALU.max)\
                          .then_inc(mx_ready, 1)
                        dve.wait_ge(mx_ready, at(b, N_UNITS, n + 1))
                        nc.vector.tensor_scalar(negm[:, g % 3, q, lo:hi], mx[:, g % 3, q, lo:hi], -SM_SCALE, None, ALU.mult)\
                          .then_inc(negm_ready, 1)
                    dve.wait_ge(negm_ready, at(b, N_UNITS, (g + 1) * G_UNITS))
                    nc.vector.tensor_tensor(sink_arg[:, g % 3], negm[:, g % 3],
                                            sinks[:, g * Q_MULT:(g + 1) * Q_MULT].unsqueeze(1).broadcast_to([P, QT, Q_MULT]),
                                            ALU.add).then_inc(sink_arg_ready, 1)

                def denominators(g):
                    dve.wait_ge(sink_exp_done, at(b, N_GROUPS, g + 1))
                    nc.vector.tensor_tensor(den[:, g % 3], sums[:, g % 3], sink_exp[:, g % 3], ALU.add)\
                      .then_inc(den_ready, 1)
                    dve.wait_ge(den_ready, at(b, N_GROUPS, g + 1))
                    if g >= 3:
                        dve.wait_ge(normed, at(b, N_GROUPS, g - 2))
                    nc.vector.reciprocal(rden[:, g % 3], den[:, g % 3]).then_inc(rden_ready, 1)

                for g in range(N_GROUPS + 1):
                    if g < N_GROUPS:
                        maxima(g)
                    if g:
                        denominators(g - 1)

                dve.wait_ge(xb_ready, at(b, 1, 1))
                for q in range(QT):
                    dve.wait_ge(out_done, at(b, QT, q + 1))
                    nc.vector.tensor_tensor(z[:, q, :], proj[q][:, 0:D], x_bias[:, q, :], ALU.add).then_inc(z_ready, 1)
                for q in range(QT):
                    dve.wait_ge(z_ready, at(b, QT, q + 1))
                    nc.vector.bn_stats(stats[:, q, :], z[:, q, :]).then_inc(stats_ready, 1)
                for q in range(QT):
                    dve.wait_ge(stats_ready, at(b, QT, q + 1))
                    dve.sem_inc(dve_seen, 1)
                    nc.vector.bn_aggr(mean_var[:, q, :], stats[:, q, :]).then_inc(mv_ready, 1)
                dve.wait_ge(mv_ready, at(b, QT, QT))
                nc.vector.tensor_scalar(var_eps[:, :, :], mean_var[:, :, 1:2], LN_EPS, None, ALU.add).then_inc(var_ready, 1)
                dve.wait_ge(rstd_ready, at(b, 1, 1))
                for q in range(QT):
                    nc.vector.tensor_scalar(keep.x[:, bass.ds(b * QT + q, 1), :], z[:, q:q + 1, :], mean_var[:, q, 0:1],
                                            rstd[:, q, :], ALU.subtract, ALU.mult).then_inc(x1_ready, 1)

        @block.gpsimd
        def _(pool):
            nc.gpsimd.memset(half_power[:, :], -0.5).then_inc(half_power_set, 1)
            for s in (xb_ready, sin_done, normed, rstd_ready):
                pool.sem_inc(s, 1)
            pool.wait_ge(consts_in, 16 * N_CONSTS)
            pool.wait_ge(half_power_set, 1)
            with pool.Fori(0, B) as b:
                pool.wait_ge(x_in, b * 16 + 16)
                pool.wait_ge(z_ready, at(b, QT, 0))
                nc.gpsimd.tensor_tensor(x_bias[:, :, :], x_res[:, :, :],
                                        b_out[:, :].unsqueeze(1).broadcast_to([P, QT, D]), ALU.add).then_inc(xb_ready, 1)
                i = 0
                for q in range(QT):
                    for c in range(QK_CHUNKS):
                        pool.wait_ge(y_ready, at(b, N_PROJ, q * N_CHUNKS + c + 1))
                        if i >= 3:
                            pool.wait_ge(roped_ready, at(b, N_QK, i - 2))
                        else:
                            pool.wait_ge(roped_ready, at(b, N_QK, 0))
                        for half in range(2):
                            lo, other = half * DH // 2, (1 - half) * DH // 2
                            op = nc.gpsimd.tensor_tensor(
                                y_sin[:, i % 3, :].rearrange("p (h d) -> p h d", d=DH)[:, :, lo:lo + DH // 2],
                                y[:, i % 3, :].rearrange("p (h d) -> p h d", d=DH)[:, :, other:other + DH // 2],
                                sin[:, q, lo:lo + DH // 2].unsqueeze(1).broadcast_to([P, CHUNK // DH, DH // 2]), ALU.mult)
                        op.then_inc(sin_done, 1)
                        i += 1
                for g in range(N_GROUPS):
                    pool.wait_ge(rden_ready, at(b, N_GROUPS, g + 1))
                    for q, lo, hi in ((0, 0, P), (1, P, KEYS)):
                        p = probs[:, g % 3, :, lo:hi]
                        op = nc.gpsimd.tensor_tensor(p, p, rden[:, g % 3, q, :].unsqueeze(2).broadcast_to([P, Q_MULT, hi - lo]),
                                                     ALU.mult)
                    op.then_inc(normed, 1)
                pool.wait_ge(var_ready, at(b, 1, 1))
                nc.gpsimd.tensor_tensor(rstd[:, :, 0], var_eps[:, :, 0], half_power[:, :].broadcast_to([P, QT]), ALU.pow)\
                  .then_inc(rstd_ready, 1)

        @block.scalar
        def _(act):
            for s in (turn_copied, exp_done, sink_exp_done, oT_copied):
                act.sem_inc(s, 1)
            with act.Fori(0, B) as b:
                f = 0
                for q in range(QT):
                    for c in range(Q_CHUNKS + 2):
                        act.wait_ge(turn_done, at(b, TR_FILLS, f + 1))
                        src = turn[f % 2][:, :].rearrange("p (n t) -> p n t", n=4)
                        if c < Q_CHUNKS:
                            op = nc.scalar.activation(qT[:, 4 * c:4 * c + 4, q * P:(q + 1) * P], src, ACT.Copy)
                        else:
                            for s in range(2):
                                rows, lo = slice(s * DH, (s + 1) * DH), 4 * (c - Q_CHUNKS)
                                op = nc.scalar.activation(kT[rows, lo:lo + 4, s, q * P:(q + 1) * P], src[rows], ACT.Copy)
                        op.then_inc(turn_copied, 1)
                        f += 1

                def exponentials(g):
                    for u in range(G_UNITS):
                        n = g * G_UNITS + u
                        act.wait_ge(negm_ready, at(b, N_UNITS, n + 1))
                        if u == 0:
                            if g >= 3:
                                act.wait_ge(turn_done, at(b, TR_FILLS, T_FILLS + (g - 2) * G_UNITS))
                                act.wait_ge(den_ready, at(b, N_GROUPS, g - 2))
                            heads, q, w = range(4), 0, P
                        else:
                            heads, q, w = range(2 * u - 2, 2 * u), 1, 2 * P
                        for e, m in enumerate(heads):
                            op = nc.scalar.activation(probs[:, g % 3, m, q * P:q * P + w], score[u][:, e * w:(e + 1) * w],
                                                      ACT.Exp, bias=negm[:, g % 3, q, m:m + 1], scale=SM_SCALE,
                                                      accum_out=sums[:, g % 3, q, m:m + 1])
                        op.then_inc(exp_done, 1)
                    act.wait_ge(sink_arg_ready, at(b, N_GROUPS, g + 1))
                    nc.scalar.activation(sink_exp[:, g % 3], sink_arg[:, g % 3], ACT.Exp).then_inc(sink_exp_done, 1)

                def copy_probs(g):
                    for u in range(G_UNITS):
                        f = T_FILLS + g * G_UNITS + u
                        act.wait_ge(turn_done, at(b, TR_FILLS, f + 1))
                        if u == 0 and g >= 2:
                            act.wait_ge(pv_done, at(b, N_PAIR, g // 2))
                        nc.scalar.activation(probsT[:, g % 2, u, :], turn[f % 2][:, :], ACT.Copy).then_inc(turn_copied, 1)

                def copy_outputs(pair):
                    act.wait_ge(pv_done, at(b, N_PAIR, pair + 1))
                    if pair == 0:
                        act.wait_ge(out_done, at(b, QT, 0))
                    for q in range(QT):
                        nc.scalar.activation(oT[:, pair, :, q * P:(q + 1) * P],
                                             proj[q][:, :].rearrange("p (m t) -> p m t", m=Q_MULT), ACT.Copy)\
                          .then_inc(oT_copied, 1)

                exponentials(0)
                exponentials(1)
                for g in range(N_GROUPS):
                    if g + 2 < N_GROUPS:
                        exponentials(g + 2)
                    if g % 2 == 0 and g:
                        copy_outputs(g // 2 - 1)
                    copy_probs(g)
                copy_outputs(N_PAIR - 1)


def cross_attention(nc, dram, keep):
    K_TILES = -(-L_ALL // P)
    MIX = L_IMG // P
    assert L_IMG % P == 1
    SIZE = [min(P, L_ALL - t * P) for t in range(K_TILES)]
    TXT_COLS = L_TXT // 3
    GH, N_GROUPS = 4, XH // 4
    UNITS = GH * QT
    CHUNKS = [(0, L_IMG)] + [(L_IMG + i * TXT_COLS, TXT_COLS) for i in range(3)]
    N_CH = UNITS * len(CHUNKS)
    PER_TILE = 3
    ROW_MAX = 6 * XD
    ROW_MASK = ROW_MAX + 6
    N_EXTRA = 7
    V_COLS = 32
    LAG_RSTD, LAG_KN, LAG_PARTS, LAG_TURN, LAG_COPY = 2, 3, 4, 5, 6
    KEY_STEPS = K_TILES + LAG_COPY
    TURN_Q = 6
    DELAY = 2
    JOINT_STEPS = DELAY + KEY_STEPS
    S_OUT, S_ATTN = K_TILES + 2, K_TILES + 4
    EARLY, EARLY_STEP, PER_STEP = 2 * UNITS, K_TILES - 2, 2
    I_PROJ, I_STATS, I_NORM, I_TURN = EARLY + 1, EARLY + 2, EARLY + 9, EARLY + 13
    N_S = N_GROUPS * K_TILES * 2
    N_PV = N_GROUPS * K_TILES

    with ExitStack() as ctx:
        def sb(name, shape, dt=F32):
            return ctx.enter_context(nc.sbuf_tensor(name, shape, dt))

        def psum(name, shape, dt=F32):
            return ctx.enter_context(nc.psum_tensor(name, shape, dt))

        def sem(name):
            return ctx.enter_context(nc.semaphore(name))

        ident_bf = sb("ident_bf2", [P, P], BF16)
        w_kv = [sb(f"w_kv{i}", [P, KT, 2, D]) for i in range(2)]
        b_kv = [sb(f"b_kv{i}", [P, 2, D]) for i in range(3)]
        g_k = [sb(f"g_k{i}", [P, D]) for i in range(3)]
        w_q = sb("w_q", [P, KT, D])
        b_q = sb("b_q", [P, D])
        g_q = sb("g_q", [P, D])
        w_o = sb("w_o", [P, KT, D])
        b_o = sb("b_o", [P, D])
        key_index = sb("key_index", [P, K_TILES])
        kinds = sb("kinds", [P, K_TILES, 6])
        half_power = sb("half_power2", [P, K_TILES])

        ctxT = sb("ctxT", [P, KT, L_ALL])
        mix = sb("mix", [P, 2, KT, P])
        len_i = sb("len_i", [P, 1], I32)
        len_f = sb("len_f", [P, 1])
        valid = sb("valid", [P, K_TILES])
        extra = sb("extra", [P, K_TILES, N_EXTRA], BF16)
        yk = sb("yk", [P, 4, D])
        junk = sb("junk", [P, 2, D], BF16)
        ssq = sb("ssq", [P, K_TILES])
        ms = sb("ms", [P, K_TILES])
        rstd_k = sb("rstd_k", [P, K_TILES])
        rstd_v = sb("rstd_v", [P, K_TILES])
        kn = sb("kn", [P, 2, D])
        k_rest = sb("k_rest", [P, 2, D])
        k_stack = sb("k_stack", [P, 3, XH, P], BF16)
        kT = sb("kTx", [P, XH, L_ALL], BF16)
        v1 = sb("v1", [P, K_TILES + 1, XH, V_COLS])

        x1c = sb("x1c", [P, QT, D])
        x1T = sb("x1T", [P, KT, T])
        yq = sb("yq", [P, QT, D])
        ssq_q = sb("ssq_q", [P, QT])
        ms_q = sb("ms_q", [P, QT])
        rstd_q = sb("rstd_q", [P, QT])
        qn = sb("qn", [P, QT, D])
        q_rest = yq
        q_stack = sb("q_stack", [P, QT, XH, P], BF16)
        qT0 = sb("qT0", [P, XH, T], BF16)
        qT = sb("qTx", [P, 2, GH, T], BF16)
        mx = sb("mx2", [P, QT, GH, 2])
        mx_part = sb("mx_part", [P, QT, GH, 3])
        m_rest = sb("m_rest", [P, QT * GH * 2])
        m_parts = sb("m_parts", [P, QT * GH * 2, 3], BF16)
        probs = sb("probs2", [P, 6, 2, T])
        o_sb = sb("o_sb", [P, 2, T])
        rden = sb("rden2", [P, 2 * QT * GH])
        o_norm = sb("o_norm", [P, 2, QT, GH * XD])
        attn = sb("attn", [P, QT, D])
        attnT = sb("attnT", [P, KT, T])
        x_bias = sb("x_bias2", [P, QT, D])
        z = sb("z2", [P, QT, D])
        x2 = z
        stats = sb("stats2", [P, QT, 6])
        mean_var = sb("mean_var2", [P, QT, 2])
        var_eps = sb("var_eps2", [P, QT])
        rstd = sb("rstd2", [P, QT])

        score = [psum(f"xscore{i}", [P, 512]) for i in range(2)]
        wide = psum("wide", [P, 4, 512])
        outs = psum("outs", [P, 2, T])
        turn = psum("xturn", [P, 512])
        turn_bf = turn[:, :].bitcast(BF16)
        wide_bf = [wide[:, i, :].bitcast(BF16) for i in range(4)]

        consts_in, w_in = sem("consts_in2"), sem("w_in2")
        consts_set = sem("consts_set2")
        pool_set = sem("pool_set2")
        stack_set = sem("stack_set2")
        ctx_in, len_in = sem("ctx_in"), sem("len_in")
        mix_ready, len_ready, valid_ready, mask_ready = [sem(n) for n in ("mix_ready", "len_ready", "valid_ready", "mask_ready")]
        kv_done, kb_ready, vb_ready, ssq_done = [sem(n) for n in ("kv_done", "kb_ready", "vb_ready", "ssq_done")]
        ms_ready, rstd_ready, rv_ready, kn_ready = [sem(n) for n in ("ms_ready", "rstd_ready", "rv_ready", "kn_ready")]
        hi_done, rest_ready, mid_ready, lo_ready = [sem(n) for n in ("hi_done", "rest_ready", "mid_ready", "lo_ready")]
        extra_done, kturn_done, kcopy_act, kcopy_dve = [sem(n) for n in ("extra_done", "kturn_done", "kcopy_act", "kcopy_dve")]
        vmix_ready = sem("vmix_ready")
        x1c_ready, xb_ready, x1T_done, x1T_copied = [sem(n) for n in ("x1c_ready", "xb_ready2", "x1T_done", "x1T_copied")]
        qp_done, yq_ready, ssq_q_done, ms_q_ready = [sem(n) for n in ("qp_done", "yq_ready", "ssq_q_done", "ms_q_ready")]
        rstd_q_ready, qn_ready, q_hi, q_rest_ready = [sem(n) for n in ("rstd_q_ready", "qn_ready", "q_hi", "q_rest_ready")]
        q_mid, q_lo, q_zeroed, qturn_done, qT0_copied = [sem(n) for n in ("q_mid", "q_lo", "q_zeroed", "qturn_done", "qT0_copied")]
        wide_done, mx_ready = [sem(n) for n in ("wide_done", "mx_ready2")]
        m_step, m_written, mturn_done, qT_copied = [sem(n) for n in ("m_step", "m_written", "mturn_done", "qT_copied")]
        s_done, exp_done, pv_done, o_copied = [sem(n) for n in ("s_done", "exp_done2", "pv_done2", "o_copied")]
        oturn_done, rden_ready, norm_ready, attn_ready = [sem(n) for n in ("oturn_done", "rden_ready2", "norm_ready", "attn_ready")]
        aturn_done, attnT_copied, wo_done, z_ready = [sem(n) for n in ("aturn_done", "attnT_copied", "wo_done", "z_ready2")]
        stats_ready, mv_ready, var_ready, ln_rstd = [sem(n) for n in ("stats_ready2", "mv_ready2", "var_ready2", "ln_rstd")]
        x2_ready, x2_kept, hturn_done, hT_copied = [sem(n) for n in ("x2_ready", "x2_kept", "hturn_done", "hT_copied")]

        sp_seen, pe_seen, dve_seen, pool_seen = [sem(n) for n in ("sp_seen", "pe_seen2", "dve_seen2", "pool_seen")]

        def at(b, per_batch, count):
            return b * per_batch + (1 + count)

        def kind(t):
            return 0 if t < MIX else 2 if t == MIX else 1

        def max_bank(g, i):
            return score[i % 2] if g == 0 and i < EARLY else wide[:, i % 4]

        def early_chunks(step):
            first = (step - EARLY_STEP) * PER_STEP
            return range(max(first, 0), min(max(first + PER_STEP, 0), EARLY))

        N_W, N_C = 6, 17

        block = ctx.enter_context(nc.Block())

        @block.sync
        def _(sp):
            rows = lambda name: dram[name].rearrange("(k p) n -> p k n", p=P)
            for i, tag in enumerate(("_img", "")):
                sp.dma_start(w_kv[i][:, :, 0, :], rows("w_k" + tag)).then_inc(w_in, 16)
                sp.dma_start(w_kv[i][:, :, 1, :], rows("w_v" + tag)).then_inc(w_in, 16)
            sp.dma_start(w_q[:, :, :], rows("w_q")).then_inc(w_in, 16)
            sp.dma_start(w_o[:, :, :], rows("w_o")).then_inc(w_in, 16)
            for i, parts in enumerate(((("_img", 0, P),), (("", 0, P),), (("_img", 0, 1), ("", 1, P)))):
                for tag, lo, hi in parts:
                    sp.dma_start(b_kv[i][lo:hi, 0, :], broadcast_rows(dram["b_k" + tag], hi - lo)).then_inc(consts_in, 16)
                    sp.dma_start(b_kv[i][lo:hi, 1, :], broadcast_rows(dram["b_v" + tag], hi - lo)).then_inc(consts_in, 16)
                    sp.dma_start(g_k[i][lo:hi, :], broadcast_rows(dram["g_k" + tag], hi - lo)).then_inc(consts_in, 16)
            sp.dma_start(b_q[:, :], broadcast_rows(dram["b_q"])).then_inc(consts_in, 16)
            sp.dma_start(g_q[:, :], broadcast_rows(dram["g_q"])).then_inc(consts_in, 16)
            sp.dma_start(b_o[:, :], broadcast_rows(dram["b_o"])).then_inc(consts_in, 16)
            sp.dma_start(key_index[:, :], dram["key_index"]).then_inc(consts_in, 16)
            sp.dma_start(kinds[:, :, :], dram["kinds"].rearrange("p (t n) -> p t n", n=6)).then_inc(consts_in, 16)
            with sp.Fori(0, B) as b:
                sp.wait_ge(kv_done, at(b, K_TILES, 0))
                sp.dma_start(ctxT[:, :, :], dram["ctxT"][bass.ds(b, 1)].rearrange("a (k p) t -> p (a k) t", p=P))\
                  .then_inc(ctx_in, 16)
                sp.wait_ge(len_ready, at(b, 1, 0))
                sp.sem_inc(sp_seen, 1)
                sp.dma_start(len_i[:, :], dram["lens"][:, bass.ds(b, 1)].partition_broadcast(P)).then_inc(len_in, 16)

        @block.tensor
        def _(pe):
            for s in (kv_done, kturn_done, x1T_done, qp_done, qturn_done, wide_done, mturn_done, s_done,
                      pv_done, oturn_done, aturn_done, wo_done, hturn_done):
                pe.sem_inc(s, 1)
            pe.wait_ge(w_in, 16 * N_W)
            pe.wait_ge(consts_set, 3)
            pe.wait_ge(pool_set, 3)
            pe.wait_ge(stack_set, 4)

            def project_kv(b, t):
                if t >= 2:
                    pe.wait_ge(vb_ready, at(b, K_TILES, t - 1))
                else:
                    pe.wait_ge(mx_ready, at(b, N_GROUPS * N_CH, 0))
                n = SIZE[t]
                if t == MIX:
                    pe.wait_ge(mix_ready, at(b, 1, 1))
                    parts = [(mix[:, i, k, :], w_kv[i][:, k]) for i in range(2) for k in range(KT)]
                else:
                    parts = [(ctxT[:, k, t * P:t * P + n], w_kv[t > MIX][:, k]) for k in range(KT)]
                for i, (keys, w) in enumerate(parts):
                    mm = nc.tensor.matmul(wide[0:n, t % 2, :], keys, w.rearrange("p s d -> p (s d)"),
                                          start=(i == 0), stop=(i == len(parts) - 1))
                mm.then_inc(kv_done, 1)

            def turn_keys(b, t):
                n = SIZE[t]
                pe.wait_ge(lo_ready, at(b, K_TILES, t + 1))
                pe.wait_ge(extra_done, at(b, K_TILES, t + 1))
                for half in range(2):
                    if t:
                        pe.wait_ge(kcopy_dve if half else kcopy_act, at(b, K_TILES, t))
                    elif half:
                        pe.wait_ge(yq_ready, at(b, 1, 1))
                    for e in range(8):
                        mm = nc.tensor.transpose(wide_bf[2 + half][:, e * P:e * P + n],
                                                 k_stack[0:n, t % 3, 8 * half + e, :], ident_bf[0:n, 0:n])
                    mm.then_inc(kturn_done, 1)

            def turn_x1(b):
                pe.wait_ge(x1c_ready, at(b, 1, 1))
                for q in range(QT):
                    for k in range(KT):
                        mm = nc.tensor.transpose(wide[:, 2, k * T + q * P:k * T + (q + 1) * P],
                                                 x1c[:, q, k * P:(k + 1) * P], keep.ident[:, :])
                mm.then_inc(x1T_done, 1)

            def project_q(b):
                pe.wait_ge(x1T_copied, at(b, 1, 1))
                for q in range(QT):
                    for k in range(KT):
                        mm = nc.tensor.matmul(wide[:, 3, q * D:(q + 1) * D], x1T[:, k, q * P:(q + 1) * P], w_q[:, k, :],
                                              start=(k == 0), stop=(k == KT - 1))
                mm.then_inc(qp_done, 1)

            def turn_q(b, f, first):
                q, half = f // 2, f % 2
                if f == 0:
                    pe.wait_ge(q_lo, at(b, 1, 1))
                    pe.wait_ge(q_zeroed, at(b, 1, 1))
                    if not first:
                        pe.wait_ge(norm_ready, at(b, N_GROUPS, -1))
                else:
                    pe.wait_ge(qT0_copied, at(b, 4, f))
                for e in range(8):
                    mm = nc.tensor.transpose(turn_bf[:, e * P:(e + 1) * P], q_stack[:, q, 8 * half + e, :], ident_bf[:, :])
                mm.then_inc(qturn_done, 1)

            def key_step(b, step, first=False):
                if not 0 <= step < KEY_STEPS:
                    return
                if step == 0:
                    pe.wait_ge(ctx_in, b * 16 + 16)
                if step < K_TILES:
                    project_kv(b, step)
                if step == 0:
                    turn_x1(b)
                if step == 2:
                    project_q(b)
                if TURN_Q <= step < TURN_Q + 4:
                    turn_q(b, step - TURN_Q, first)
                if 0 <= step - LAG_TURN < K_TILES:
                    turn_keys(b, step - LAG_TURN)
                for i in early_chunks(step):
                    max_chunk(b, 0, i)

            def max_chunk(b, g, i):
                c, n = i // UNITS, i % UNITS
                h, q, (lo, cols) = g * GH + n % GH, n // GH, CHUNKS[c]
                if g == 0 and i == 0:
                    pe.wait_ge(exp_done, at(b, N_S, 0))
                    pe.wait_ge(qT0_copied, at(b, 4, 4))
                if g == 0 and i in (0, UNITS):
                    tiles = -(-(CHUNKS[c][0] + CHUNKS[c][1]) // P)
                    pe.wait_ge(kcopy_dve, at(b, K_TILES, tiles))
                    pe.wait_ge(kcopy_act, at(b, K_TILES, tiles))
                if g == 0 and i == EARLY:
                    pe.wait_ge(kcopy_dve, at(b, K_TILES, K_TILES))
                    pe.wait_ge(kcopy_act, at(b, K_TILES, K_TILES))
                pe.wait_ge(mx_ready, at(b, N_GROUPS * N_CH, max(g * N_CH + i + 1 - (2 if g == 0 and i < EARLY else 4), 0)))
                nc.tensor.matmul(max_bank(g, i)[:, 0:cols], qT0[:, h, q * P:(q + 1) * P], kT[:, h, lo:lo + cols],
                                 start=True, stop=True).then_inc(wide_done, 1)

            def turn_maxima(b, g):
                pe.wait_ge(m_written, at(b, N_GROUPS, g + 1))
                if g:
                    if g > 1:
                        pe.wait_ge(norm_ready, at(b, N_GROUPS, g - 1))
                else:
                    pe.wait_ge(hT_copied, at(b, 1, 0))
                for e in range(GH):
                    for q in range(QT):
                        mm = nc.tensor.transpose(turn_bf[:, e * T + q * P:e * T + (q + 1) * P],
                                                 q_stack[:, q, g * GH + e, :], ident_bf[:, :])
                mm.then_inc(mturn_done, 1)

            def scores(b, g, t):
                n = SIZE[t]
                if t == 0:
                    pe.wait_ge(qT_copied, at(b, N_GROUPS, g + 1))
                    if g == 0:
                        pe.wait_ge(z_ready, at(b, QT, 0))
                for pair in range(2):
                    m = (g * K_TILES + t) * 2 + pair
                    pe.wait_ge(exp_done, at(b, N_S, max(m - 1, 0)))
                    for e in range(2):
                        j = 2 * pair + e
                        mm = nc.tensor.matmul(score[pair][0:n, e * T:(e + 1) * T], kT[:, g * GH + j, t * P:t * P + n],
                                              qT[:, g % 2, j, :], start=True, stop=True)
                    mm.then_inc(s_done, 1)

            def weigh_values(b, g, t):
                n = SIZE[t]
                slot = (g * K_TILES + t) * 2
                if t == 0:
                    pe.wait_ge(o_copied, at(b, N_GROUPS, g))
                    if g == 0:
                        pe.wait_ge(vmix_ready, at(b, 1, 1))
                pe.wait_ge(exp_done, at(b, N_S, slot + 2))
                if t == MIX:
                    pe.sem_inc(pe_seen, 1)
                for side_, v_tile, rows in ([(0, t, n)] if t < MIX else [(0, t, 1), (1, K_TILES, n)] if t == MIX
                                            else [(1, t, n)]):
                    first = (side_ == 0 and t == 0) or (side_ == 1 and t == MIX)
                    last = (side_ == 0 and t == MIX) or (side_ == 1 and t == K_TILES - 1)
                    for j in range(GH):
                        mm = nc.tensor.matmul(outs[32 * j:32 * j + V_COLS, side_, :], v1[0:rows, v_tile, g * GH + j, :],
                                              probs[0:rows, (slot + j // 2) % 6, j % 2, :], start=first, stop=last)
                mm.then_inc(pv_done, 1)

            def turn_outputs(b, g, joined=False):
                pe.wait_ge(o_copied, at(b, N_GROUPS, g + 1))
                if g + 1 < N_GROUPS:
                    pe.wait_ge(qT_copied, at(b, N_GROUPS, g + 2))
                elif joined:
                    pe.wait_ge(qT0_copied, at(b, 4, 8))
                else:
                    pe.wait_ge(norm_ready, at(b, N_GROUPS, g))
                for s in range(2):
                    for q in range(QT):
                        i = s * QT + q
                        mm = nc.tensor.transpose(turn[:, i * P:(i + 1) * P], o_sb[:, s, q * P:(q + 1) * P], keep.ident[:, :])
                mm.then_inc(oturn_done, 1)

            def turn_attn(b):
                pe.wait_ge(attn_ready, at(b, N_GROUPS, N_GROUPS))
                for q in range(QT):
                    for k in range(KT):
                        mm = nc.tensor.transpose(turn[:, k * T + q * P:k * T + (q + 1) * P], attn[:, q, k * P:(k + 1) * P],
                                                 keep.ident[:, :])
                mm.then_inc(aturn_done, 1)

            def project_out(b):
                pe.wait_ge(attnT_copied, at(b, 1, 1))
                for q in range(QT):
                    for k in range(KT):
                        mm = nc.tensor.matmul(outs[:, q, 0:D], attnT[:, k, q * P:(q + 1) * P], w_o[:, k, :],
                                              start=(k == 0), stop=(k == KT - 1))
                    mm.then_inc(wo_done, 1)

            def turn_x2(b):
                pe.wait_ge(x2_ready, at(b, QT, QT))
                for q in range(QT):
                    for k in range(KT):
                        mm = nc.tensor.transpose(turn[:, k * T + q * P:k * T + (q + 1) * P], x2[:, q, k * P:(k + 1) * P],
                                                 keep.ident[:, :])
                mm.then_inc(hturn_done, 1)

            def batch(b, joined):
                for g in range(N_GROUPS - 1):
                    scores(b, g, 0)
                    for t in range(K_TILES):
                        if t + 1 < K_TILES:
                            scores(b, g, t + 1)
                        for i in range(t * PER_TILE, min((t + 1) * PER_TILE, N_CH)):
                            max_chunk(b, g + 1, i)
                        weigh_values(b, g, t)
                        if t == 3 and g:
                            turn_outputs(b, g - 1)
                        if t == K_TILES - 2:
                            turn_maxima(b, g + 1)
                g = N_GROUPS - 1
                scores(b, g, 0)
                for step in range(JOINT_STEPS):
                    if step + 1 < K_TILES:
                        scores(b, g, step + 1)
                    if joined:
                        key_step(b + 1, step - DELAY)
                    if step < K_TILES:
                        weigh_values(b, g, step)
                    if step == 3:
                        turn_outputs(b, g - 1)
                    if step == S_OUT:
                        turn_outputs(b, g, joined)
                    if step == S_ATTN:
                        turn_attn(b)
                for i in range(EARLY, N_CH):
                    if joined:
                        max_chunk(b + 1, 0, i)
                    if i == I_PROJ:
                        project_out(b)
                    if i == I_TURN:
                        turn_x2(b)
                if joined:
                    turn_maxima(b + 1, 0)

            for step in range(KEY_STEPS):
                key_step(0, step, first=True)
            for i in range(EARLY, N_CH):
                max_chunk(0, 0, i)
            turn_maxima(0, 0)
            with pe.Fori(0, B - 1) as b:
                batch(b, True)
            batch(B - 1, False)

        @block.vector
        def _(dve):
            for s in (len_ready, valid_ready, mask_ready, kb_ready, vb_ready, kn_ready, rest_ready,
                      mid_ready, kcopy_dve, yq_ready, ms_q_ready, qn_ready, q_hi, q_rest_ready, q_mid, q_lo,
                      mx_ready, m_step, m_written, qT_copied, rden_ready, norm_ready, attn_ready, z_ready,
                      stats_ready, mv_ready, var_ready, x2_ready):
                dve.sem_inc(s, 1)
            dve.wait_ge(consts_in, 16 * N_C)
            nc.vector.tensor_copy(ident_bf[:, :], keep.ident[:, :]).then_inc(consts_set, 1)
            nc.vector.tensor_scalar(g_q[:, :], g_q[:, :], 1.0 / math.sqrt(XD), None, ALU.mult).then_inc(consts_set, 1)
            nc.vector.tensor_copy(extra[:, :, 0:6], kinds[:, :, :]).then_inc(consts_set, 1)
            dve.wait_ge(consts_set, 3)
            dve.wait_ge(pool_set, 3)
            dve.wait_ge(stack_set, 4)

            def find_valid(b):
                dve.wait_ge(len_in, b * 16 + 16)
                nc.vector.tensor_scalar(len_f[:, :], len_i[:, :], 0.0, None, ALU.max).then_inc(len_ready, 1)
                dve.wait_ge(len_ready, at(b, 1, 1))
                nc.vector.tensor_scalar(valid[:, :], key_index[:, :], len_f[:, :], None, ALU.is_lt).then_inc(valid_ready, 1)
                dve.wait_ge(valid_ready, at(b, 1, 1))
                nc.vector.tensor_scalar(extra[:, :, 6], valid[:, :], -1.0, 1.0e9, ALU.add, ALU.mult).then_inc(mask_ready, 1)

            def add_bias(b, t, first):
                n, c = SIZE[t], kind(t)
                dve.wait_ge(kv_done, at(b, K_TILES, t + 1))
                if t >= 4:
                    dve.wait_ge(kn_ready, at(b, K_TILES, t - 3))
                nc.vector.tensor_tensor(yk[0:n, t % 4, :], wide[0:n, t % 2, 0:D], b_kv[c][0:n, 0, :], ALU.add)\
                  .then_inc(kb_ready, 1)
                if not first:
                    dve.wait_ge(pv_done, at(b, N_PV, t + 1 - K_TILES))
                nc.vector.tensor_tensor(v1[0:n, t, :, 0:XD], wide[0:n, t % 2, D:2 * D].rearrange("p (h d) -> p h d", h=XH),
                                        b_kv[c][0:n, 1, :].rearrange("p (h d) -> p h d", h=XH), ALU.add)\
                  .then_inc(vb_ready, 1)

            def normalize(b, t):
                n = SIZE[t]
                dve.wait_ge(rv_ready, at(b, K_TILES, t + 1))
                nc.vector.scalar_tensor_tensor(out=kn[0:n, t % 2, :], in0=yk[0:n, t % 4, :], scalar=rstd_v[0:n, t:t + 1],
                                               in1=g_k[kind(t)][0:n, :], op0=ALU.mult, op1=ALU.mult).then_inc(kn_ready, 1)

            def heads_of(flat, n):
                return flat.rearrange("p (h d) -> p h d", h=XH)

            def split_rest(b, t):
                n, stack = SIZE[t], k_stack[0:SIZE[t], t % 3]
                dve.wait_ge(hi_done, at(b, K_TILES, t + 1))
                rest = heads_of(k_rest[0:n, t % 2, :], n)
                if t >= 2:
                    dve.wait_ge(lo_ready, at(b, K_TILES, t - 1))
                nc.vector.tensor_tensor(rest, heads_of(kn[0:n, t % 2, :], n), stack[:, :, 0:XD], ALU.subtract)\
                  .then_inc(rest_ready, 1)
                dve.wait_ge(rest_ready, at(b, K_TILES, t + 1))
                nc.vector.tensor_copy(stack[:, :, 3 * XD:5 * XD].rearrange("p h (s d) -> p h s d", s=2),
                                      rest.unsqueeze(2).broadcast_to([n, XH, 2, XD])).then_inc(mid_ready, 1)

            def copy_keys(b, t):
                n = SIZE[t]
                dve.wait_ge(kturn_done, at(b, 2 * K_TILES, 2 * t + 2))
                nc.vector.tensor_copy(kT[:, 8:16, t * P:t * P + n],
                                      wide_bf[3].rearrange("p (h k) -> p h k", h=8)[:, :, 0:n])\
                  .then_inc(kcopy_dve, 1)

            def bias_q(b):
                dve.wait_ge(qp_done, at(b, 1, 1))
                nc.vector.tensor_tensor(yq[:, :, :], wide[:, 3, :].rearrange("p (q d) -> p q d", q=QT),
                                        b_q[:, :].unsqueeze(1).broadcast_to([P, QT, D]), ALU.add).then_inc(yq_ready, 1)

            def mean_square_q(b):
                dve.wait_ge(ssq_q_done, at(b, QT, QT))
                nc.vector.tensor_scalar(ms_q[:, :], ssq_q[:, :], 1.0 / D, RMS_EPS, ALU.mult, ALU.add)\
                  .then_inc(ms_q_ready, 1)

            def normalize_q(b):
                dve.wait_ge(rstd_q_ready, at(b, 1, 1))
                for q in range(QT):
                    nc.vector.scalar_tensor_tensor(out=qn[:, q, :], in0=yq[:, q, :], scalar=rstd_q[:, q:q + 1],
                                                   in1=g_q[:, :], op0=ALU.mult, op1=ALU.mult).then_inc(qn_ready, 1)

            def split_q(b, q):
                dve.wait_ge(qn_ready, at(b, QT, QT))
                stack, whole, rest = q_stack[:, q], heads_of(qn[:, q, :], P), heads_of(q_rest[:, q, :], P)
                for s in (0, 3, 5):
                    nc.vector.tensor_copy(stack[:, :, s * XD:(s + 1) * XD], whole).then_inc(q_hi, 1)
                dve.wait_ge(q_hi, at(b, 3 * QT, 3 * q + 3))
                nc.vector.tensor_tensor(rest, whole, stack[:, :, 0:XD], ALU.subtract).then_inc(q_rest_ready, 1)
                dve.wait_ge(q_rest_ready, at(b, QT, q + 1))
                for s in (1, 4):
                    nc.vector.tensor_copy(stack[:, :, s * XD:(s + 1) * XD], rest).then_inc(q_mid, 1)
                dve.wait_ge(q_mid, at(b, 2 * QT, 2 * q + 2))
                op = nc.vector.tensor_tensor(stack[:, :, 2 * XD:3 * XD], rest, stack[:, :, XD:2 * XD], ALU.subtract)
                if q == QT - 1:
                    op.then_inc(q_lo, 1)

            def key_step(b, step, first=False):
                if not 0 <= step < KEY_STEPS:
                    return
                if step == 0:
                    find_valid(b)
                if 0 <= step - LAG_COPY < K_TILES:
                    copy_keys(b, step - LAG_COPY)
                if step < K_TILES:
                    add_bias(b, step, first)
                if step == 2:
                    bias_q(b)
                if step == 3:
                    mean_square_q(b)
                if step == 4:
                    normalize_q(b)
                if step == 5:
                    for q in range(QT):
                        split_q(b, q)
                if 0 <= step - LAG_KN < K_TILES:
                    normalize(b, step - LAG_KN)
                if 0 <= step - LAG_PARTS < K_TILES:
                    split_rest(b, step - LAG_PARTS)
                for i in early_chunks(step):
                    maximum(b, 0, i)

            def maximum(b, g, i):
                c, n = i // UNITS, i % UNITS
                q, e, cols = n // GH, n % GH, CHUNKS[c][1]
                dve.wait_ge(wide_done, at(b, N_GROUPS * N_CH, g * N_CH + i + 1))
                nc.vector.tensor_reduce(mx_part[:, q, e, c - 1:c] if c else mx[:, q, e, 0:1], max_bank(g, i)[:, 0:cols],
                                        AX_X, ALU.max).then_inc(mx_ready, 1)

            def write_maxima(b, g):
                flat = mx[:, :, :, :].rearrange("p q h s -> p (q h s)")
                dve.wait_ge(mx_ready, at(b, N_GROUPS * N_CH, (g + 1) * N_CH))
                nc.vector.tensor_reduce(mx[:, :, :, 1], mx_part[:, :, :, :], AX_X, ALU.max).then_inc(m_step, 1)
                dve.wait_ge(m_step, at(b, 5 * N_GROUPS, 5 * g + 1))
                nc.vector.tensor_scalar(m_parts[:, :, 0], flat, -1.0, None, ALU.mult).then_inc(m_step, 1)
                dve.wait_ge(m_step, at(b, 5 * N_GROUPS, 5 * g + 2))
                nc.vector.scalar_tensor_tensor(out=m_rest[:, :], in0=flat, scalar=-1.0, in1=m_parts[:, :, 0],
                                               op0=ALU.mult, op1=ALU.subtract).then_inc(m_step, 1)
                dve.wait_ge(m_step, at(b, 5 * N_GROUPS, 5 * g + 3))
                nc.vector.tensor_copy(m_parts[:, :, 1], m_rest[:, :]).then_inc(m_step, 1)
                dve.wait_ge(m_step, at(b, 5 * N_GROUPS, 5 * g + 4))
                nc.vector.tensor_tensor(m_parts[:, :, 2], m_rest[:, :], m_parts[:, :, 1], ALU.subtract).then_inc(m_step, 1)
                dve.wait_ge(m_step, at(b, 5 * N_GROUPS, 5 * g + 5))
                nc.vector.tensor_copy(q_stack[:, :, g * GH:(g + 1) * GH, ROW_MAX:ROW_MAX + 6],
                                      m_parts[:, :, :].rearrange("p (q h s) r -> p q h (s r)", q=QT, h=GH))\
                  .then_inc(m_written, 1)
                dve.wait_ge(mturn_done, at(b, N_GROUPS, g + 1))
                nc.vector.tensor_copy(qT[:, g % 2, :, :], turn_bf.rearrange("p (h t) -> p h t", h=GH)).then_inc(qT_copied, 1)

            def normalize_outputs(b, g):
                dve.wait_ge(oturn_done, at(b, N_GROUPS, g + 1))
                raw = turn[:, :].rearrange("p (n c) -> p n c", c=V_COLS)
                nc.vector.reciprocal(rden[:, :], raw[:, :, XD]).then_inc(rden_ready, 1)
                dve.wait_ge(rden_ready, at(b, N_GROUPS, g + 1))
                nc.vector.tensor_tensor(o_norm[:, :, :, :].rearrange("p s q (h d) -> p (s q h) d", d=XD), raw[:, :, 0:XD],
                                        rden[:, :].unsqueeze(2).broadcast_to([P, 2 * QT * GH, XD]), ALU.mult)\
                  .then_inc(norm_ready, 1)
                dve.wait_ge(norm_ready, at(b, N_GROUPS, g + 1))
                nc.vector.tensor_tensor(attn[:, :, g * GH * XD:(g + 1) * GH * XD], o_norm[:, 0], o_norm[:, 1], ALU.add)\
                  .then_inc(attn_ready, 1)

            def add_residual(b):
                dve.wait_ge(xb_ready, at(b, 1, 1))
                dve.wait_ge(hturn_done, at(b, 1, 0))
                dve.wait_ge(x2_kept, at(b, 1, 0))
                for q in range(QT):
                    dve.wait_ge(wo_done, at(b, QT, QT))
                    nc.vector.tensor_tensor(z[:, q, :], outs[:, q, 0:D], x_bias[:, q, :], ALU.add).then_inc(z_ready, 1)
                for q in range(QT):
                    dve.wait_ge(z_ready, at(b, QT, q + 1))
                    nc.vector.bn_stats(stats[:, q, :], z[:, q, :]).then_inc(stats_ready, 1)
                for q in range(QT):
                    dve.wait_ge(stats_ready, at(b, QT, q + 1))
                    dve.sem_inc(dve_seen, 1)
                    nc.vector.bn_aggr(mean_var[:, q, :], stats[:, q, :]).then_inc(mv_ready, 1)
                dve.wait_ge(mv_ready, at(b, QT, QT))
                nc.vector.tensor_scalar(var_eps[:, :], mean_var[:, :, 1], LN_EPS, None, ALU.add).then_inc(var_ready, 1)

            def normalize_rows(b):
                dve.wait_ge(ln_rstd, at(b, 1, 1))
                for q in range(QT):
                    nc.vector.tensor_scalar(x2[:, q, :], z[:, q, :], mean_var[:, q, 0:1], rstd[:, q:q + 1],
                                            ALU.subtract, ALU.mult).then_inc(x2_ready, 1)

            def batch(b, joined):
                for g in range(N_GROUPS - 1):
                    for i in range(N_CH):
                        maximum(b, g + 1, i)
                        if i == 4 * PER_TILE and g:
                            normalize_outputs(b, g - 1)
                    write_maxima(b, g + 1)
                for step in range(JOINT_STEPS):
                    if joined:
                        key_step(b + 1, step - DELAY)
                    if step == 3:
                        normalize_outputs(b, N_GROUPS - 2)
                    if step == S_OUT:
                        normalize_outputs(b, N_GROUPS - 1)
                for i in range(EARLY, N_CH):
                    if joined:
                        maximum(b + 1, 0, i)
                    if i == I_STATS:
                        add_residual(b)
                    if i == I_NORM:
                        normalize_rows(b)
                if joined:
                    write_maxima(b + 1, 0)

            for step in range(KEY_STEPS):
                key_step(0, step, first=True)
            for i in range(EARLY, N_CH):
                maximum(0, 0, i)
            write_maxima(0, 0)
            with dve.Fori(0, B - 1) as b:
                batch(b, True)
            batch(B - 1, False)

        @block.gpsimd
        def _(pool):
            for s in (mix_ready, ms_ready, rstd_ready, rv_ready, lo_ready, extra_done, vmix_ready, x1c_ready, xb_ready, rstd_q_ready, q_zeroed, ln_rstd,
                      x2_kept):
                pool.sem_inc(s, 1)
            nc.gpsimd.memset(mix[:, :, :, :], 0.0).then_inc(pool_set, 1)
            nc.gpsimd.memset(half_power[:, :], -0.5).then_inc(pool_set, 1)
            nc.gpsimd.memset(k_stack[:, :, :, ROW_MASK + 1:P], 0.0).then_inc(pool_set, 1)
            nc.gpsimd.memset(q_stack[:, :, :, ROW_MASK + 1:P], 0.0).then_inc(stack_set, 1)
            nc.gpsimd.memset(q_stack[:, :, :, ROW_MASK:ROW_MASK + 1], 1.0).then_inc(stack_set, 1)
            nc.gpsimd.memset(v1[:, :, :, XD:XD + 1], 1.0).then_inc(stack_set, 1)
            nc.gpsimd.memset(v1[:, :, :, XD + 1:V_COLS], 0.0).then_inc(stack_set, 1)
            pool.wait_ge(pool_set, 3)
            pool.wait_ge(stack_set, 4)
            pool.wait_ge(consts_set, 3)
            pool.wait_ge(consts_in, 16 * N_C)

            def begin(b):
                pool.wait_ge(x1T_done, at(b, 1, 0))
                pool.wait_ge(xb_ready, at(b, 1, 0))
                pool.sem_inc(pool_seen, 1)
                nc.gpsimd.tensor_copy(x1c[:, :, :], keep.x[:, bass.ds(b * QT, QT), :]).then_inc(x1c_ready, 1)
                pool.wait_ge(ctx_in, b * 16 + 16)
                pool.wait_ge(kv_done, at(b, K_TILES, 0))
                pool.sem_inc(pool_seen, 1)
                nc.gpsimd.tensor_copy(mix[:, 0, :, 0:1], ctxT[:, :, MIX * P:MIX * P + 1])
                nc.gpsimd.tensor_copy(mix[:, 1, :, 1:P], ctxT[:, :, MIX * P + 1:(MIX + 1) * P]).then_inc(mix_ready, 1)
                pool.wait_ge(m_written, at(b, N_GROUPS, 0))
                pool.wait_ge(mturn_done, at(b, N_GROUPS, 0))
                pool.sem_inc(pool_seen, 1)
                nc.gpsimd.memset(q_stack[:, :, :, ROW_MAX:ROW_MAX + 6], 0.0).then_inc(q_zeroed, 1)
                pool.wait_ge(mask_ready, at(b, 1, 1))

            def key_step(b, step):
                if not 0 <= step < KEY_STEPS:
                    return
                if step == 0:
                    begin(b)
                t = step - LAG_RSTD
                if 0 <= t < K_TILES:
                    n = SIZE[t]
                    pool.wait_ge(ssq_done, at(b, K_TILES, t + 1))
                    pool.sem_inc(pool_seen, 1)
                    nc.gpsimd.tensor_scalar(ms[0:n, t:t + 1], ssq[0:n, t:t + 1], 1.0 / D, RMS_EPS, ALU.mult, ALU.add)\
                      .then_inc(ms_ready, 1)
                    pool.wait_ge(ms_ready, at(b, K_TILES, t + 1))
                    nc.gpsimd.tensor_tensor(rstd_k[0:n, t:t + 1], ms[0:n, t:t + 1], half_power[0:n, 0:1], ALU.pow)\
                      .then_inc(rstd_ready, 1)
                    pool.wait_ge(rstd_ready, at(b, K_TILES, t + 1))
                    nc.gpsimd.tensor_tensor(rstd_v[0:n, t:t + 1], rstd_k[0:n, t:t + 1], valid[0:n, t:t + 1], ALU.mult)\
                      .then_inc(rv_ready, 1)
                if step == 3:
                    pool.wait_ge(ms_q_ready, at(b, 1, 1))
                    nc.gpsimd.tensor_tensor(rstd_q[:, :], ms_q[:, :], half_power[:, 0:QT], ALU.pow).then_inc(rstd_q_ready, 1)
                t = step - LAG_PARTS
                if 0 <= t < K_TILES:
                    if t >= 3:
                        pool.wait_ge(kturn_done, at(b, 2 * K_TILES, 2 * t - 4))
                        pool.sem_inc(pool_seen, 1)
                    nc.gpsimd.tensor_copy(k_stack[:, t % 3, :, ROW_MAX:ROW_MAX + N_EXTRA],
                                          extra[:, t, :].unsqueeze(1).broadcast_to([P, XH, N_EXTRA])).then_inc(extra_done, 1)
                if 0 <= t < K_TILES:
                    n, stack = SIZE[t], k_stack[0:SIZE[t], t % 3]
                    pool.wait_ge(mid_ready, at(b, K_TILES, t + 1))
                    nc.gpsimd.tensor_tensor(stack[:, :, 5 * XD:6 * XD], k_rest[0:n, t % 2, :].rearrange("p (h d) -> p h d", h=XH),
                                            stack[:, :, 3 * XD:4 * XD], ALU.subtract).then_inc(lo_ready, 1)
                if step == K_TILES:
                    pool.wait_ge(vb_ready, at(b, K_TILES, K_TILES))
                    pool.sem_inc(pool_seen, 1)
                    nc.gpsimd.tensor_scalar(v1[:, K_TILES, :, :], v1[:, MIX, :, :], kinds[:, MIX, 3:4], None, ALU.mult)\
                        .then_inc(vmix_ready, 1)

            def batch(b, joined):
                pool.wait_ge(z_ready, at(b, QT, 0))
                pool.wait_ge(x1c_ready, at(b, 1, 1))
                nc.gpsimd.tensor_tensor(x_bias[:, :, :], x1c[:, :, :], b_o[:, :].unsqueeze(1).broadcast_to([P, QT, D]), ALU.add)\
                  .then_inc(xb_ready, 1)
                for step in range(JOINT_STEPS):
                    if joined:
                        key_step(b + 1, step - DELAY)
                pool.wait_ge(var_ready, at(b, 1, 1))
                nc.gpsimd.tensor_tensor(rstd[:, :], var_eps[:, :], half_power[:, 0:QT], ALU.pow).then_inc(ln_rstd, 1)
                pool.wait_ge(x2_ready, at(b, QT, QT))
                pool.sem_inc(pool_seen, 1)
                nc.gpsimd.tensor_copy(keep.x[:, bass.ds(b * QT, QT), :], x2[:, :, :]).then_inc(x2_kept, 1)

            for step in range(KEY_STEPS):
                key_step(0, step)
            with pool.Fori(0, B - 1) as b:
                batch(b, True)
            batch(B - 1, False)

        @block.scalar
        def _(act):
            for s in (ssq_done, hi_done, kcopy_act, x1T_copied, ssq_q_done, qT0_copied, exp_done, o_copied,
                      attnT_copied, hT_copied):
                act.sem_inc(s, 1)

            def square(b, t):
                n = SIZE[t]
                act.wait_ge(kb_ready, at(b, K_TILES, t + 1))
                act.wait_ge(ssq_done, at(b, K_TILES, max(t - 1, 0)))
                nc.scalar.activation(junk[0:n, t % 2, :], yk[0:n, t % 4, :], ACT.Square, accum_out=ssq[0:n, t:t + 1])\
                  .then_inc(ssq_done, 1)

            def high_part(b, t):
                n = SIZE[t]
                act.wait_ge(kn_ready, at(b, K_TILES, t + 1))
                if t >= 3:
                    act.wait_ge(kturn_done, at(b, 2 * K_TILES, 2 * t - 4))
                nc.scalar.activation(
                    k_stack[0:n, t % 3, :, 0:3 * XD].rearrange("p h (s d) -> p h s d", s=3),
                    kn[0:n, t % 2, :].rearrange("p (h d) -> p h d", h=XH).unsqueeze(2).broadcast_to([n, XH, 3, XD]),
                    ACT.Copy).then_inc(hi_done, 1)

            def copy_keys(b, t):
                n = SIZE[t]
                act.wait_ge(kturn_done, at(b, 2 * K_TILES, 2 * t + 1))
                nc.scalar.activation(kT[:, 0:8, t * P:t * P + n],
                                     wide_bf[2].rearrange("p (h k) -> p h k", h=8)[:, :, 0:n], ACT.Copy)\
                  .then_inc(kcopy_act, 1)

            def copy_x1T(b):
                act.wait_ge(x1T_done, at(b, 1, 1))
                act.wait_ge(qp_done, at(b, 1, 0))
                nc.scalar.activation(x1T[:, :, :].rearrange("p k t -> p (k t)"), wide[:, 2, :], ACT.Copy).then_inc(x1T_copied, 1)

            def square_q(b):
                act.wait_ge(yq_ready, at(b, 1, 1))
                act.wait_ge(ssq_q_done, at(b, QT, 0))
                for q in range(QT):
                    nc.scalar.activation(qn[:, q, :], yq[:, q, :], ACT.Square, accum_out=ssq_q[:, q:q + 1])\
                      .then_inc(ssq_q_done, 1)

            def copy_qT0(b, f):
                act.wait_ge(qturn_done, at(b, 4, f + 1))
                nc.scalar.activation(qT0[:, 8 * (f % 2):8 * (f % 2) + 8, (f // 2) * P:(f // 2 + 1) * P],
                                     turn_bf.rearrange("p (h t) -> p h t", h=8), ACT.Copy).then_inc(qT0_copied, 1)

            def key_step(b, step):
                if not 0 <= step < KEY_STEPS:
                    return
                if 0 <= step - LAG_COPY < K_TILES:
                    copy_keys(b, step - LAG_COPY)
                if step < K_TILES:
                    square(b, step)
                if step == 0:
                    copy_x1T(b)
                if step == 2:
                    square_q(b)
                if TURN_Q <= step < TURN_Q + 4:
                    copy_qT0(b, step - TURN_Q)
                if 0 <= step - LAG_KN < K_TILES:
                    high_part(b, step - LAG_KN)

            def exponentials(b, g, t):
                n = SIZE[t]
                for pair in range(2):
                    m = (g * K_TILES + t) * 2 + pair
                    act.wait_ge(s_done, at(b, N_S, m + 1))
                    if pair == 0:
                        act.wait_ge(pv_done, at(b, N_PV, max(g * K_TILES + t - 2, 0)))
                    nc.scalar.activation(probs[0:n, m % 6, :, :].rearrange("p e t -> p (e t)"), score[pair][0:n, :],
                                         ACT.Exp).then_inc(exp_done, 1)

            def copy_outputs(b, g):
                act.wait_ge(pv_done, at(b, N_PV, (g + 1) * K_TILES))
                act.wait_ge(oturn_done, at(b, N_GROUPS, g))
                nc.scalar.activation(o_sb[:, :, :], outs[:, :, :], ACT.Copy).then_inc(o_copied, 1)

            def batch(b, joined):
                for g in range(N_GROUPS - 1):
                    for t in range(K_TILES):
                        exponentials(b, g, t)
                    copy_outputs(b, g)
                exponentials(b, N_GROUPS - 1, 0)
                for step in range(JOINT_STEPS):
                    if step + 1 < K_TILES:
                        exponentials(b, N_GROUPS - 1, step + 1)
                    if step == K_TILES:
                        copy_outputs(b, N_GROUPS - 1)
                    if joined:
                        key_step(b + 1, step - DELAY)
                    if step == S_ATTN:
                        act.wait_ge(aturn_done, at(b, 1, 1))
                        nc.scalar.activation(attnT[:, :, :].rearrange("p k t -> p (k t)"), turn[:, :], ACT.Copy)\
                          .then_inc(attnT_copied, 1)
                act.wait_ge(hturn_done, at(b, 1, 1))
                nc.scalar.activation(keep.hT[:, :, bass.ds(b * T, T)], turn[:, :].rearrange("p (k t) -> p k t", k=KT),
                                     ACT.Copy).then_inc(hT_copied, 1)

            for step in range(KEY_STEPS):
                key_step(0, step)
            with act.Fori(0, B - 1) as b:
                batch(b, True)
            batch(B - 1, False)


def mixture_of_experts(nc, dram, keep, scratch, out):
    HALF = 512
    C = N_TOK // HALF
    SLOTS = 2 * N_PAIRS
    LOGITS = E + 1
    GU = KT * 2 * P
    LOOPS = (N_PAIRS - 1) // 2

    with ExitStack() as ctx:
        def sb(name, shape, dt=F32):
            return ctx.enter_context(nc.sbuf_tensor(name, shape, dt))

        def psum(name, shape, dt=F32):
            return ctx.enter_context(nc.psum_tensor(name, shape, dt))

        def sem(name):
            return ctx.enter_context(nc.semaphore(name))

        w_router = sb("w_router", [P, KT, LOGITS])
        weights = sb("weights", [P, 2, GU + D])
        mix_w = sb("mix_w", [P, 2, N_TOK])
        logit = sb("logit", [P, N_TILES, E])
        top_m = sb("top_m", [P, N_TILES])
        ex = sb("ex", [P, N_TILES, E])
        esum = sb("esum", [P, N_TILES])
        erec = sb("erec", [P, N_TILES])
        prob = sb("prob", [P, N_TILES, E])
        top = sb("top", [P, N_TILES, TOP_K])
        rest = sb("rest", [P, N_TILES, E])
        tsum = sb("tsum", [P, N_TILES])
        trec = sb("trec", [P, N_TILES])
        chosen = sb("chosen", [P, N_TILES, E])
        sgate = sb("sgate", [P, N_TILES])
        comb = sb("comb", [P, N_TILES, SLOTS])
        combT = sb("combT", [SLOTS, N_TOK])
        half_power = sb("half_power3", [P, N_TILES])
        th = sb("th", [P, C, HALF])
        gated = sb("gated", [P, C, HALF])
        prod = sb("prod", [P, C, HALF])
        act_w = sb("act_w", [P, C, HALF])
        zT = sb("zT", [P, KT, N_TOK])
        stats = sb("stats3", [P, N_TILES, 6])
        mean_var = sb("mean_var3", [P, N_TILES, 2])
        var_eps = sb("var_eps3", [P, N_TILES])
        rstd = sb("rstd3", [P, N_TILES])
        x3 = sb("x3", [P, N_TILES, D])

        gate_up = psum("gate_up", [P, C, 2, HALF])
        y = psum("y_sum", [P, C, KT, HALF])

        router_in, scratch_in, out_done = sem("router_in"), sem("scratch_in"), sem("out_done3")
        w_in = [sem(f"w_in3_{i}") for i in range(2)]
        c_in = [sem(f"c_in{i}") for i in range(2)]
        logits_done, top_ready, logit_ready, ex_done, sgate_done = [sem(n) for n in (
            "logits_done", "top_ready", "logit_ready", "ex_done", "sgate_done")]
        esum_ready, erec_ready, prob_ready, top8_ready, rest_ready = [sem(n) for n in (
            "esum_ready", "erec_ready", "prob_ready", "top8_ready", "rest_ready3")]
        tsum_ready, trec_ready, chosen_ready, comb_ready, pad_set = [sem(n) for n in (
            "tsum_ready", "trec_ready", "chosen_ready", "comb_ready", "pad_set")]
        comb_turned, comb_copied = sem("comb_turned"), sem("comb_copied")
        gu_done, th_done, gated_ready, prod_ready, act_ready, down_done = [sem(n) for n in (
            "gu_done", "th_done", "gated_ready", "prod_ready", "act_ready", "down_done")]
        zT_ready, z_turned, stats_ready, mv_ready, var_ready, rstd_ready, x3_ready = [sem(n) for n in (
            "zT_ready", "z_turned", "stats_ready3", "mv_ready3", "var_ready3", "rstd_ready3", "x3_ready")]

        banks = gate_up[:, :, :, :].rearrange("p c s t -> p (c s) t")

        block = ctx.enter_context(nc.Block())

        @block.sync
        def _(sp):
            def load_weights(p, slot):
                sp.dma_start(weights[:, slot, :], dram["pairs"][p].rearrange("a p n -> p (a n)")).then_inc(w_in[slot], 16)

            def load_mix(p, slot):
                sp.dma_start(mix_w[:, slot, :], scratch[p].rearrange("a e t -> (a e) t").unsqueeze(1)
                             .broadcast_to([2, EI, N_TOK])).then_inc(c_in[slot], 16)

            sp.dma_start(w_router[:, :, :], dram["router_wT"].rearrange("(k p) n -> p k n", p=P)).then_inc(router_in, 16)
            load_weights(slice(0, 1), 0)
            load_weights(slice(1, 2), 1)
            sp.wait_ge(comb_copied, C)
            sp.dma_start(scratch[:, :, :].rearrange("a e t -> (a e) t"), combT[:, :]).then_inc(scratch_in, 16)
            sp.wait_ge(scratch_in, 16)
            load_mix(slice(0, 1), 0)
            load_mix(slice(1, 2), 1)
            sp.wait_ge(down_done, 2)
            load_weights(slice(2, 3), 0)
            load_mix(slice(2, 3), 0)
            with sp.Fori(0, LOOPS - 1) as it:
                for u in range(2):
                    p = it * 2 + (3 + u)
                    sp.wait_ge(down_done, it * 4 + (2 + u) * 2)
                    load_weights(bass.ds(p, 1), 1 - u)
                    load_mix(bass.ds(p, 1), 1 - u)
            sp.wait_ge(down_done, 2 * N_PAIRS - 2)
            sp.wait_ge(down_done, 2 * N_PAIRS - 2)
            for t in range(N_TILES):
                sp.wait_ge(x3_ready, t + 1)
                sp.dma_start(out.rearrange("b (q p) d -> p (b q) d", p=P)[:, t, :], x3[:, t, :]).then_inc(out_done, 16)
            sp.wait_ge(out_done, 16 * N_TILES)

        @block.tensor
        def _(pe):
            pe.wait_ge(router_in, 16)
            for t in range(N_TILES):
                for k in range(KT):
                    mm = nc.tensor.matmul(banks[:, t // 4, (t % 4) * P:(t % 4) * P + LOGITS],
                                          keep.hT[:, k, t * P:(t + 1) * P], w_router[:, k, :], start=(k == 0), stop=(k == KT - 1))
            mm.then_inc(logits_done, 1)
            pe.wait_ge(comb_ready, 1)
            pe.wait_ge(pad_set, 2)
            pe.wait_ge(sgate_done, 2)
            for t in range(N_TILES):
                mm = nc.tensor.transpose(banks[0:SLOTS, 2 + t // 4, (t % 4) * P:(t % 4 + 1) * P], comb[:, t, :], keep.ident[:, :])
            mm.then_inc(comb_turned, 1)
            pe.wait_ge(comb_copied, C)

            def gate_and_up(n, c, slot, loads, first=False):
                if c == 0:
                    pe.wait_ge(w_in[slot], loads)
                if not first:
                    pe.wait_ge(prod_ready, n - 1)
                for s in range(2):
                    for k in range(KT):
                        lo = (k * 2 + s) * P
                        mm = nc.tensor.matmul(gate_up[:, c, s, :], weights[:, slot, lo:lo + P],
                                              keep.hT[:, k, c * HALF:(c + 1) * HALF], start=(k == 0), stop=(k == KT - 1))
                mm.then_inc(gu_done, 1)

            def down(n, c, slot, first=False, last=False):
                pe.wait_ge(act_ready, n + 1)
                for d in range(KT):
                    mm = nc.tensor.matmul(y[:, c, d, :], weights[:, slot, GU + d * P:GU + (d + 1) * P], act_w[:, c, :],
                                          start=first, stop=last)
                mm.then_inc(down_done, 1)

            gate_and_up(0, 0, 0, 16, first=True)
            gate_and_up(1, 1, 0, 16, first=True)
            down(0, 0, 0, first=True)
            gate_and_up(2, 0, 1, 16)
            down(1, 1, 0, first=True)
            gate_and_up(3, 1, 1, 16)
            down(2, 0, 1)
            with pe.Fori(0, LOOPS - 1) as it:
                for u in range(2):
                    n = it * 4 + (4 + 2 * u)
                    gate_and_up(n, 0, u, it * 16 + 32)
                    down(n - 1, 1, 1 - u)
                    gate_and_up(n + 1, 1, u, it * 16 + 32)
                    down(n, 0, u)
            n = 2 * N_PAIRS - 2
            gate_and_up(n, 0, 0, LOOPS * 16 + 16)
            down(n - 1, 1, 1)
            gate_and_up(n + 1, 1, 0, LOOPS * 16 + 16)
            down(n, 0, 0, last=True)
            down(n + 1, 1, 0, last=True)

            for t in range(N_TILES):
                if t % 4 == 0:
                    pe.wait_ge(zT_ready, t // 4 + 1)
                for k in range(KT):
                    mm = nc.tensor.transpose(banks[:, t // 2, (t % 2) * D + k * P:(t % 2) * D + (k + 1) * P],
                                             zT[:, k, t * P:(t + 1) * P], keep.ident[:, :])
                mm.then_inc(z_turned, 1)

        @block.vector
        def _(dve):
            raw = banks[:, 0:2, :].rearrange("p a (t n) -> p (a t) n", n=P)
            dve.wait_ge(logits_done, 1)
            nc.vector.tensor_reduce(top_m[:, :], raw[:, :, 0:E], AX_X, ALU.max).then_inc(top_ready, 1)
            dve.wait_ge(top_ready, 1)

            def by_tile(v):
                return v.unsqueeze(2).broadcast_to([P, N_TILES, E])

            nc.vector.tensor_tensor(logit[:, :, :], raw[:, :, 0:E], by_tile(top_m[:, :]), ALU.subtract).then_inc(logit_ready, 1)
            dve.wait_ge(ex_done, 1)
            nc.vector.tensor_reduce(esum[:, :], ex[:, :, :], AX_X, ALU.add).then_inc(esum_ready, 1)
            dve.wait_ge(esum_ready, 1)
            nc.vector.reciprocal(erec[:, :], esum[:, :]).then_inc(erec_ready, 1)
            dve.wait_ge(erec_ready, 1)
            nc.vector.tensor_tensor(prob[:, :, :], ex[:, :, :], by_tile(erec[:, :]), ALU.mult).then_inc(prob_ready, 1)
            dve.wait_ge(prob_ready, 1)
            for t in range(N_TILES):
                nc.vector.max(out=top[:, t, :], in_=prob[:, t, :]).then_inc(top8_ready, 1)
            for t in range(N_TILES):
                dve.wait_ge(top8_ready, t + 1)
                nc.vector.match_replace(out=rest[:, t, :], in_to_replace=top[:, t, :], in_values=prob[:, t, :],
                                        imm_value=-1.0).then_inc(rest_ready, 1)
            nc.vector.tensor_reduce(tsum[:, :], top[:, :, :], AX_X, ALU.add).then_inc(tsum_ready, 1)
            dve.wait_ge(tsum_ready, 1)
            nc.vector.reciprocal(trec[:, :], tsum[:, :]).then_inc(trec_ready, 1)
            dve.wait_ge(rest_ready, N_TILES)
            nc.vector.scalar_tensor_tensor(out=chosen[:, :, :], in0=rest[:, :, :], scalar=0.0, in1=prob[:, :, :],
                                           op0=ALU.is_lt, op1=ALU.mult).then_inc(chosen_ready, 1)
            dve.wait_ge(chosen_ready, 1)
            dve.wait_ge(trec_ready, 1)
            nc.vector.scalar_tensor_tensor(out=comb[:, :, 0:E], in0=chosen[:, :, :], scalar=0.5, in1=by_tile(trec[:, :]),
                                           op0=ALU.mult, op1=ALU.mult).then_inc(comb_ready, 1)
            for c in range(C):
                dve.wait_ge(comb_turned, 1)
                nc.vector.tensor_copy(combT[:, c * HALF:(c + 1) * HALF], banks[0:SLOTS, 2 + c, :]).then_inc(comb_copied, 1)

            def unit(n, c, first=False):
                dve.wait_ge(th_done, n + 1)
                if not first:
                    dve.wait_ge(act_ready, n - 1)
                nc.vector.scalar_tensor_tensor(out=gated[:, c, :], in0=th[:, c, :], scalar=1.0, in1=gate_up[:, c, 0, :],
                                               op0=ALU.add, op1=ALU.mult).then_inc(gated_ready, 1)
                dve.wait_ge(gated_ready, n + 1)
                nc.vector.tensor_tensor(prod[:, c, :], gated[:, c, :], gate_up[:, c, 1, :], ALU.mult).then_inc(prod_ready, 1)

            unit(0, 0, first=True)
            unit(1, 1, first=True)
            with dve.Fori(0, LOOPS) as it:
                for u in range(4):
                    unit(it * 4 + (2 + u), u % 2)

            for c in range(C):
                dve.wait_ge(down_done, 2 * N_PAIRS - 1 + c)
                nc.vector.tensor_tensor(zT[:, :, c * HALF:(c + 1) * HALF], y[:, c, :, :], keep.hT[:, :, c * HALF:(c + 1) * HALF],
                                        ALU.add).then_inc(zT_ready, 1)
            for t in range(N_TILES):
                z = banks[:, t // 2, (t % 2) * D:(t % 2 + 1) * D]
                dve.wait_ge(z_turned, 2 * (t // 2) + 2)
                nc.vector.bn_stats(stats[:, t, :], z).then_inc(stats_ready, 1)
            for t in range(N_TILES):
                dve.wait_ge(stats_ready, t + 1)
                nc.vector.bn_aggr(mean_var[:, t, :], stats[:, t, :]).then_inc(mv_ready, 1)
            dve.wait_ge(mv_ready, N_TILES)
            nc.vector.tensor_scalar(var_eps[:, :], mean_var[:, :, 1], LN_EPS, None, ALU.add).then_inc(var_ready, 1)
            dve.wait_ge(rstd_ready, 1)
            for t in range(N_TILES):
                z = banks[:, t // 2, (t % 2) * D:(t % 2 + 1) * D]
                nc.vector.tensor_scalar(x3[:, t, :], z, mean_var[:, t, 0:1], rstd[:, t:t + 1],
                                        ALU.subtract, ALU.mult).then_inc(x3_ready, 1)

        @block.gpsimd
        def _(pool):
            nc.gpsimd.memset(half_power[:, :], -0.5).then_inc(pad_set, 1)
            nc.gpsimd.memset(comb[:, :, E + 1:SLOTS], 0.0).then_inc(pad_set, 1)

            def unit(n, c, slot, loads, first=False):
                pool.wait_ge(prod_ready, n + 1)
                if c == 0:
                    pool.wait_ge(c_in[slot], loads)
                if not first:
                    pool.wait_ge(down_done, n - 1)
                nc.gpsimd.tensor_tensor(act_w[:, c, :], prod[:, c, :], mix_w[:, slot, c * HALF:(c + 1) * HALF], ALU.mult)\
                  .then_inc(act_ready, 1)

            unit(0, 0, 0, 16, first=True)
            unit(1, 1, 0, 16, first=True)
            with pool.Fori(0, LOOPS) as it:
                for c in range(C):
                    unit(it * 4 + (2 + c), c, 1, it * 16 + 16)
                for c in range(C):
                    unit(it * 4 + (4 + c), c, 0, it * 16 + 32)
            pool.wait_ge(var_ready, 1)
            pool.wait_ge(pad_set, 2)
            nc.gpsimd.tensor_tensor(rstd[:, :], var_eps[:, :], half_power[:, :], ALU.pow).then_inc(rstd_ready, 1)

        @block.scalar
        def _(act):
            act.wait_ge(logits_done, 1)
            act.wait_ge(logit_ready, 1)
            nc.scalar.activation(ex[:, :, :], logit[:, :, :], ACT.Exp).then_inc(ex_done, 1)
            nc.scalar.activation(sgate[:, :], banks[:, 0:2, :].rearrange("p a (t n) -> p (a t) n", n=P)[:, :, E], ACT.Tanh,
                                 scale=0.5).then_inc(sgate_done, 1)
            act.wait_ge(sgate_done, 1)
            nc.scalar.activation(comb[:, :, E], sgate[:, :], ACT.Copy, scale=0.25, bias=0.25).then_inc(sgate_done, 1)

            def unit(n, c, first=False):
                act.wait_ge(gu_done, n + 1)
                if not first:
                    act.wait_ge(prod_ready, n - 1)
                nc.scalar.activation(th[:, c, :], gate_up[:, c, 0, :], ACT.Tanh, scale=0.5).then_inc(th_done, 1)

            unit(0, 0, first=True)
            unit(1, 1, first=True)
            with act.Fori(0, LOOPS) as it:
                for u in range(4):
                    unit(it * 4 + (2 + u), u % 2)


def host_layout(inputs):
    a = {k: np.asarray(v) for k, v in inputs.items()}

    def t(name):
        return np.ascontiguousarray(a[name].T)

    out_wT = a["L0_attn_out_w"].T.reshape(N_KV // 2, 2, Q_MULT, DH, D).transpose(1, 3, 0, 2, 4).reshape(P, -1)
    eye = np.eye(P, dtype=np.float32)
    cos, sin = rope_tables()
    tiles = -(-L_ALL // P)
    key_index = (np.arange(tiles)[None, :] * P + np.arange(P)[:, None] - L_IMG).astype(np.float32)
    kinds = np.stack([key_index < 0] * 3 + [key_index >= 0] * 3, -1).astype(np.float32).reshape(P, -1)
    arrays = {
        "x": a["x"], "xT": a["x"].transpose(0, 2, 1),
        "qkv_wT": t("L0_attn_qkv_w"), "qkv_b": a["L0_attn_qkv_b"], "sinks": a["L0_attn_sinks"],
        "out_wT": out_wT, "out_b": a["L0_attn_out_b"],
        "cos": cos, "sin": sin, "masks": window_masks(), "ident": eye,
        "ctxT": a["ctx_2048"].transpose(0, 2, 1), "lens": a["_lenS2"].reshape(1, B),
        "key_index": key_index, "kinds": kinds,
    }
    for name in ("w_q", "w_k", "w_v", "w_k_img", "w_v_img", "w_o"):
        arrays[name] = t("L0_xattn_" + name)
    for name in ("b_q", "b_k", "b_v", "b_k_img", "b_v_img", "b_o", "g_q", "g_k", "g_k_img"):
        arrays[name] = a["L0_xattn_" + name]
    def in_pairs(routed, shared):
        both = np.concatenate([routed, shared[None], np.zeros_like(shared)[None]])
        return both.reshape((N_PAIRS, 2) + shared.shape)

    gate_up = a["L0_ffn_gate_up_proj"]
    gate = in_pairs(gate_up[:, :EI], a["L0_ffn_shared_gate_w"])
    up = in_pairs(gate_up[:, EI:], a["L0_ffn_shared_up_w"])
    down = in_pairs(a["L0_ffn_down_proj"], a["L0_ffn_shared_down_w"])
    gu = np.stack([gate, up], 1).reshape(N_PAIRS, 2, 2, EI, KT, P).transpose(0, 5, 4, 1, 2, 3).reshape(N_PAIRS, P, -1)
    arrays["pairs"] = np.concatenate([gu, down.transpose(0, 1, 3, 2).reshape(N_PAIRS, P, D)], 2)
    arrays["router_wT"] = np.concatenate([t("L0_ffn_router_w"), t("L0_ffn_shared_expert_gate_w")], 1)
    return {k: np.ascontiguousarray(v) for k, v in arrays.items()}


class Keep:

    def __init__(self, ident, x, hT):
        self.ident = ident
        self.x = x
        self.hT = hT


def decoder_layer(nc, dram, out):
    scratch = nc.dram_tensor("mix_rows", (N_PAIRS, 2, N_TOK), F32, kind="Internal").ap()
    with ExitStack() as ctx:
        keep = Keep(ctx.enter_context(nc.sbuf_tensor("ident", [P, P], F32)),
                    ctx.enter_context(nc.sbuf_tensor("x_keep", [P, N_TILES, D], F32)),
                    ctx.enter_context(nc.sbuf_tensor("hT", [P, KT, N_TOK], F32)))
        self_attention(nc, dram, keep)
        cross_attention(nc, dram, keep)
        mixture_of_experts(nc, dram, keep, scratch, out)


def kernel(**inputs):
    import concourse.bacc as bacc
    from concourse.bass_utils import run_bass_kernel_spmd

    nc = bacc.Bacc("TRN2", target_bir_lowering=False, num_devices=1)
    arrays = host_layout(inputs)
    dram = {name: nc.dram_tensor("in_" + name, a.shape, mybir.dt.from_np(a.dtype), kind="ExternalInput").ap()
            for name, a in arrays.items()}
    out = nc.dram_tensor("out_x", (B, T, D), F32, kind="ExternalOutput").ap()
    decoder_layer(nc, dram, out)
    r = run_bass_kernel_spmd(nc, [{"in_" + name: a for name, a in arrays.items()}], core_ids=[0])
    return r.results[0]["out_x"]
```
